# Optimizing a Trainium2 kernel written in Bass

```python
import numpy as np
import jax
import jax.numpy as jnp

def _softmax(x, axis=-1):
    return jax.nn.softmax(x, axis=axis)

def _gelu(x):
    return jax.nn.gelu(x, approximate=True)

def _silu(x):
    return jax.nn.silu(x)

def _sigmoid(x):
    return jax.nn.sigmoid(x)

def _layernorm(x, axis=-1, eps=1e-05):
    m = jnp.mean(x, axis=axis, keepdims=True)
    v = jnp.var(x, axis=axis, keepdims=True)
    return (x - m) / jnp.sqrt(v + eps)

def _scatter_add(tgt, idx, src, axis=0):
    return tgt.at[idx].add(src)

def _segment_sum(src, seg, n):
    return jax.ops.segment_sum(src, seg, n)
kernel_name = 'mk_adj_resnorm_d4_adj_r2_87b3a1'

def setup_inputs(seed: int=0):
    np.random.seed(seed)
    _w = jnp.asarray

    def _rec_inputs():
        import jax
        import jax.numpy as jnp
        _gk = jax.random.key(seed)
        x = 7.22e-05 + 1 * jax.random.normal(jax.random.fold_in(_gk, 1), (64, 128, 512), jnp.float32)
        _a = jax.random.bernoulli(jax.random.fold_in(_gk, 2), 0.015625, (128, 128))
        _a = jnp.logical_or(_a, jnp.swapaxes(_a, -1, -2))
        _a = jnp.logical_or(_a, jnp.eye(128, dtype=bool))
        _af = _a.astype(jnp.float32)
        _af = _af * jax.random.uniform(jax.random.fold_in(_gk, 3), (128, 128), jnp.float32, 0.05, 0.108252)
        adj = _af
        return (x, adj)
    x, adj = _rec_inputs()

    def _L0_gnn_setup():
        import jax, jax.numpy as jnp
        import numpy as np

        def _ada_gcn(xn, weight, bias):
            N, B, L = xn.shape
            x_norm = xn / jnp.maximum(jnp.linalg.norm(xn, axis=-1, keepdims=True), 1e-12)
            mean_sim = jnp.einsum('nbl,mbl->nm', x_norm, x_norm) / B
            k = max(int(N * 0.3), 1)
            _, idx = jax.lax.top_k(mean_sim, k + 1)
            rows = jnp.arange(N)[:, None]
            non_self = idx != rows
            order = jnp.cumsum(non_self.astype(jnp.int32), axis=1) - 1
            keep = non_self & (order < k)
            mask = jnp.zeros((N, N), dtype=bool).at[jnp.broadcast_to(rows, idx.shape), idx].set(keep)
            A = jnp.where(mask, mean_sim, jnp.zeros((), mean_sim.dtype))
            deg = A.sum(axis=0)
            dinv = jnp.where(deg > 0, jax.lax.rsqrt(deg), jnp.zeros((), deg.dtype))
            An = dinv[:, None] * A * dinv[None, :]
            xw = jnp.einsum('nbl,lo->nbo', xn, weight)
            out = jnp.einsum('sd,sbl->dbl', An, xw) + bias
            return out
        key = jax.random.key(seed)
        k1, k2 = jax.random.split(key)
        B, L, N = (32, 128, 512)
        x = jax.random.normal(k1, (B, L, N), dtype=jnp.float32)
        limit = float(np.sqrt(6.0 / (L + L)))
        weight = jax.random.uniform(k2, (L, L), dtype=jnp.float32, minval=-limit, maxval=limit)
        bias = jnp.zeros((L,), dtype=jnp.float32)
        return {'x': x, 'weight': weight, 'bias': bias}
    _L0_gnn_all = _L0_gnn_setup()
    _L0_gnn_in = {k: v for k, v in _L0_gnn_all.items() if k in ('bias',)}
    del _L0_gnn_all

    def _L1_gnn_setup():
        import jax, jax.numpy as jnp
        import numpy as np
        DIM = 199
        K_HOP = 3

        def _khop_support(n, k):
            A = np.eye(n, dtype=np.float64)
            idx = np.arange(n)
            A[idx, (idx + 1) % n] = 1.0
            A[(idx + 1) % n, idx] = 1.0
            S = np.linalg.matrix_power(A, k)
            return (S > 0).astype(np.float32)
        key = jax.random.key(seed)
        kx, kk = jax.random.split(key)
        batch, n, f = (128, DIM, 512)
        x = jax.random.normal(kx, (batch, n, f), dtype=jnp.float32)
        support = jnp.asarray(_khop_support(n, K_HOP))
        limit = float(np.sqrt(6.0 / (n + n)))
        kernel = jax.random.uniform(kk, (n, n), minval=-limit, maxval=limit, dtype=jnp.float32)
        bias = jnp.zeros((f,), dtype=jnp.float32)
        return {'x': x, 'support': support, 'kernel': kernel, 'bias': bias}
    _L1_gnn_all = _L1_gnn_setup()
    _L1_gnn_in = {k: v for k, v in _L1_gnn_all.items() if k in ('bias',)}
    del _L1_gnn_all

    def _L2_gnn_setup():
        import jax, jax.numpy as jnp
        import numpy as np
        EPS = 1e-08

        def _row_stochastic_causal(A, causal_mask):
            A = A * causal_mask
            deg = jnp.maximum(A.sum(axis=-1, keepdims=True), EPS)
            return A / deg
        key = jax.random.key(seed)
        k = jax.random.split(key, 5)
        B, N, D = (4, 1024, 512)
        s = 1.0 / np.sqrt(D)
        h = jax.random.normal(k[0], (B, N, D), dtype=jnp.float32)
        W_lang = jax.random.normal(k[1], (D, D), dtype=jnp.float32) * s
        W_grav = jax.random.normal(k[2], (D, D), dtype=jnp.float32) * s
        W_V = jax.random.normal(k[3], (D, D), dtype=jnp.float32) * s
        W_O = jax.random.normal(k[4], (D, D), dtype=jnp.float32) * s
        causal_mask = jnp.tril(jnp.ones((N, N), dtype=jnp.float32))
        gate_logit = jnp.zeros((), jnp.float32)
        log_sigma = jnp.zeros((), jnp.float32)
        return {'h': h, 'causal_mask': causal_mask, 'W_lang': W_lang, 'W_grav': W_grav, 'W_V': W_V, 'W_O': W_O, 'gate_logit': gate_logit, 'log_sigma': log_sigma}
    _L2_gnn_all = _L2_gnn_setup()
    _L2_gnn_in = {k: v for k, v in _L2_gnn_all.items() if k in ('W_lang', 'W_grav', 'W_V', 'W_O', 'gate_logit', 'log_sigma')}
    del _L2_gnn_all

    def _L3_gnn_setup():
        import jax, jax.numpy as jnp
        import numpy as np

        def _ada_gcn(xn, weight, bias):
            N, B, L = xn.shape
            x_norm = xn / jnp.maximum(jnp.linalg.norm(xn, axis=-1, keepdims=True), 1e-12)
            mean_sim = jnp.einsum('nbl,mbl->nm', x_norm, x_norm) / B
            k = max(int(N * 0.3), 1)
            _, idx = jax.lax.top_k(mean_sim, k + 1)
            rows = jnp.arange(N)[:, None]
            non_self = idx != rows
            order = jnp.cumsum(non_self.astype(jnp.int32), axis=1) - 1
            keep = non_self & (order < k)
            mask = jnp.zeros((N, N), dtype=bool).at[jnp.broadcast_to(rows, idx.shape), idx].set(keep)
            A = jnp.where(mask, mean_sim, jnp.zeros((), mean_sim.dtype))
            deg = A.sum(axis=0)
            dinv = jnp.where(deg > 0, jax.lax.rsqrt(deg), jnp.zeros((), deg.dtype))
            An = dinv[:, None] * A * dinv[None, :]
            xw = jnp.einsum('nbl,lo->nbo', xn, weight)
            out = jnp.einsum('sd,sbl->dbl', An, xw) + bias
            return out
        key = jax.random.key(seed)
        k1, k2 = jax.random.split(key)
        B, L, N = (32, 128, 512)
        x = jax.random.normal(k1, (B, L, N), dtype=jnp.float32)
        limit = float(np.sqrt(6.0 / (L + L)))
        weight = jax.random.uniform(k2, (L, L), dtype=jnp.float32, minval=-limit, maxval=limit)
        bias = jnp.zeros((L,), dtype=jnp.float32)
        return {'x': x, 'weight': weight, 'bias': bias}
    _L3_gnn_all = _L3_gnn_setup()
    _L3_gnn_in = {k: v for k, v in _L3_gnn_all.items() if k in ('bias',)}
    del _L3_gnn_all
    return {'x': x, 'adj': adj, 'L0_gnn_bias': _L0_gnn_in['bias'], 'L1_gnn_bias': _L1_gnn_in['bias'], 'L2_gnn_W_lang': _L2_gnn_in['W_lang'], 'L2_gnn_W_grav': _L2_gnn_in['W_grav'], 'L2_gnn_W_V': _L2_gnn_in['W_V'], 'L2_gnn_W_O': _L2_gnn_in['W_O'], 'L2_gnn_gate_logit': _L2_gnn_in['gate_logit'], 'L2_gnn_log_sigma': _L2_gnn_in['log_sigma'], 'L3_gnn_bias': _L3_gnn_in['bias']}

def reference(x, adj, L0_gnn_bias, L1_gnn_bias, L2_gnn_W_lang, L2_gnn_W_grav, L2_gnn_W_V, L2_gnn_W_O, L2_gnn_gate_logit, L2_gnn_log_sigma, L3_gnn_bias):
    import jax
    import jax.numpy as jnp

    def _L0_gnn_ref(x, weight, bias):
        import jax, jax.numpy as jnp
        import numpy as np

        def _ada_gcn(xn, weight, bias):
            N, B, L = xn.shape
            x_norm = xn / jnp.maximum(jnp.linalg.norm(xn, axis=-1, keepdims=True), 1e-12)
            mean_sim = jnp.einsum('nbl,mbl->nm', x_norm, x_norm) / B
            k = max(int(N * 0.3), 1)
            _, idx = jax.lax.top_k(mean_sim, k + 1)
            rows = jnp.arange(N)[:, None]
            non_self = idx != rows
            order = jnp.cumsum(non_self.astype(jnp.int32), axis=1) - 1
            keep = non_self & (order < k)
            mask = jnp.zeros((N, N), dtype=bool).at[jnp.broadcast_to(rows, idx.shape), idx].set(keep)
            A = jnp.where(mask, mean_sim, jnp.zeros((), mean_sim.dtype))
            deg = A.sum(axis=0)
            dinv = jnp.where(deg > 0, jax.lax.rsqrt(deg), jnp.zeros((), deg.dtype))
            An = dinv[:, None] * A * dinv[None, :]
            xw = jnp.einsum('nbl,lo->nbo', xn, weight)
            out = jnp.einsum('sd,sbl->dbl', An, xw) + bias
            return out
        xn = jnp.transpose(x, (2, 0, 1))
        num_levels = 1
        for _ in range(num_levels):
            xn = _ada_gcn(xn, weight, bias)
        return jnp.transpose(xn, (1, 2, 0))

    def _L1_gnn_ref(x, support, kernel, bias):
        import jax, jax.numpy as jnp
        import numpy as np
        DIM = 199
        K_HOP = 3

        def _khop_support(n, k):
            A = np.eye(n, dtype=np.float64)
            idx = np.arange(n)
            A[idx, (idx + 1) % n] = 1.0
            A[(idx + 1) % n, idx] = 1.0
            S = np.linalg.matrix_power(A, k)
            return (S > 0).astype(np.float32)
        W = support * kernel
        out = jnp.einsum('bnf,nm->bmf', x, W)
        out = out + bias
        return out

    def _L2_gnn_ref(h, causal_mask, W_lang, W_grav, W_V, W_O, gate_logit, log_sigma):
        import jax, jax.numpy as jnp
        import numpy as np
        EPS = 1e-08

        def _row_stochastic_causal(A, causal_mask):
            A = A * causal_mask
            deg = jnp.maximum(A.sum(axis=-1, keepdims=True), EPS)
            return A / deg
        z_l = jnp.einsum('bnd,ed->bne', h, W_lang)
        z_g = jnp.einsum('bnd,ed->bne', h, W_grav)
        v = jnp.einsum('bnd,ed->bne', h, W_V)
        N = h.shape[-2]
        not_eye = 1.0 - jnp.eye(N, dtype=h.dtype)
        zn = z_l / jnp.maximum(jnp.linalg.norm(z_l, axis=-1, keepdims=True), EPS)
        A_l = jnp.maximum(jnp.einsum('bnd,bmd->bnm', zn, zn), 0.0) * not_eye
        sq = jnp.sum(z_g * z_g, axis=-1, keepdims=True)
        d2 = jnp.maximum(sq + jnp.swapaxes(sq, -1, -2) - 2.0 * jnp.einsum('bnd,bmd->bnm', z_g, z_g), 0.0)
        sigma = jnp.exp(log_sigma)
        A_g = jnp.exp(-d2 / (2.0 * sigma * sigma)) * not_eye
        K_l = _row_stochastic_causal(A_l, causal_mask)
        K_g = _row_stochastic_causal(A_g, causal_mask)
        w_l = jax.nn.sigmoid(gate_logit)
        K = w_l * K_l + (1.0 - w_l) * K_g
        out = jnp.einsum('bnm,bmd->bnd', K, v)
        return jnp.einsum('bnd,ed->bne', out, W_O)

    def _L3_gnn_ref(x, weight, bias):
        import jax, jax.numpy as jnp
        import numpy as np

        def _ada_gcn(xn, weight, bias):
            N, B, L = xn.shape
            x_norm = xn / jnp.maximum(jnp.linalg.norm(xn, axis=-1, keepdims=True), 1e-12)
            mean_sim = jnp.einsum('nbl,mbl->nm', x_norm, x_norm) / B
            k = max(int(N * 0.3), 1)
            _, idx = jax.lax.top_k(mean_sim, k + 1)
            rows = jnp.arange(N)[:, None]
            non_self = idx != rows
            order = jnp.cumsum(non_self.astype(jnp.int32), axis=1) - 1
            keep = non_self & (order < k)
            mask = jnp.zeros((N, N), dtype=bool).at[jnp.broadcast_to(rows, idx.shape), idx].set(keep)
            A = jnp.where(mask, mean_sim, jnp.zeros((), mean_sim.dtype))
            deg = A.sum(axis=0)
            dinv = jnp.where(deg > 0, jax.lax.rsqrt(deg), jnp.zeros((), deg.dtype))
            An = dinv[:, None] * A * dinv[None, :]
            xw = jnp.einsum('nbl,lo->nbo', xn, weight)
            out = jnp.einsum('sd,sbl->dbl', An, xw) + bias
            return out
        xn = jnp.transpose(x, (2, 0, 1))
        num_levels = 1
        for _ in range(num_levels):
            xn = _ada_gcn(xn, weight, bias)
        return jnp.transpose(xn, (1, 2, 0))
    x = _layernorm(x + _L0_gnn_ref(x, adj, L0_gnn_bias), axis=-1)
    x = _layernorm(x + _L1_gnn_ref(x, adj, adj, L1_gnn_bias), axis=-1)
    x = _layernorm(x + _L2_gnn_ref(x, adj, L2_gnn_W_lang, L2_gnn_W_grav, L2_gnn_W_V, L2_gnn_W_O, L2_gnn_gate_logit, L2_gnn_log_sigma), axis=-1)
    x = _layernorm(x + _L3_gnn_ref(x, adj, L3_gnn_bias), axis=-1)
    return x

_drawn_inputs = setup_inputs


def setup_inputs(seed=0):
    import zlib

    import numpy as np

    out = dict(_drawn_inputs(seed))
    spreads = {'L0_gnn_bias': (0.0, 0.1), 'L1_gnn_bias': (0.0, 0.1), 'L3_gnn_bias': (0.0, 0.1)}
    factors = {}
    for name, (base, spread) in spreads.items():
        noise = np.random.default_rng([zlib.crc32(name.encode()), seed]).standard_normal(out[name].shape)
        drawn = base * np.exp(spread * noise) if base else spread * noise
        out[name] = jnp.asarray(drawn.astype(out[name].dtype))
    for name, factor in factors.items():
        out[name] = (out[name] * factor).astype(out[name].dtype)
    return out
```

```python
import concourse.bass as bass
from concourse import mybir
from contextlib import ExitStack, contextmanager

F32 = mybir.dt.float32
F16 = mybir.dt.float16
ALU = mybir.AluOpType
ACT = mybir.ActivationFunctionType
AX_X = mybir.AxisListType.X
ABSMAX = bass.bass_isa.ReduceOp.absmax
RMAX = bass.bass_isa.ReduceOp.max

B, P, N = 64, 128, 512
C = N // P
G = 4
NG = B // G
TOPK = int(N * 0.3)
ROUNDS = TOPK // 8
assert TOPK == 8 * ROUNDS + 1
LN_EPS = 1e-5
SENT = -3.0e38

S_RN = 2.0 ** 14
S_COL = 2.0 ** 15
S_W = 2.0 ** 13
S_AN = 2.0 ** 14
S_LN = 2.0 ** 10
S_K = 2.0 ** 14
S_EVAC = 2.0 ** -17

(M_ADJ, M_WL, M_WG, M_M, W_ADJ, W_WL, W_WG, W_M, W_SQ, EPS_L, K_G, GATE, UNGATE, F_OUT2, F_L1, SIG,
 NSQ_MAX, SX, SAN, F_B, TMP_A, TMP_B, HALF, TMP_C) = range(24)
NSCAL = 24


def need(eng, sem, value):
    if isinstance(value, int) and value <= 0:
        return
    eng.wait_ge(sem, value)


@contextmanager
def strided(eng, start, end, step):
    with eng.Fori(start // step, end // step) as u:
        yield u * step


def settle(eng, sem, value, idle):
    if isinstance(value, int):
        return need(eng, sem, value)
    eng.wait_ge(sem, value)
    eng.sem_inc(idle, 1)


class Step:

    def __init__(self, i, rem, total):
        self.i, self.rem, self.total = i, rem, total

    def live(self, lag):
        return not isinstance(self.i, int) or 0 <= self.i - lag < self.total

    def at(self, lag):
        return self.i - lag

    def slot(self, lag, ring=2):
        return (self.rem - lag) % ring


def pipeline(eng, total, depth, ring, step):
    head = -(-(depth + ring) // ring) * ring
    for i in range(head):
        step(Step(i, i % ring, total))
    with strided(eng, head, total, ring) as base:
        for j in range(ring):
            step(Step(base + j, j % ring, total))
    for i in range(total, total + depth):
        step(Step(i, i % ring, total))


def over(t, reps):
    return t.rearrange("p (o n) -> p o n", o=1).broadcast_to([t.shape[0], reps, t.shape[1]])


def spread(t, width):
    return t.rearrange("p (n o) -> p n o", o=1).broadcast_to([t.shape[0], t.shape[1], width])


def grouped(t, parts=C):
    return t.rearrange("p (a b) -> p a b", a=parts)


class Chip:

    def __init__(self, nc, ctx):
        self.nc, self.ctx = nc, ctx
        self.n = 0
        self.taken = []
        self.X = self.sb(ctx, "x_all", [P, B, N])
        self.ident = self.sb(ctx, "ident", [P, P])
        self.ones = self.sb(ctx, "ones", [P, P])
        self.adj = self.sb(ctx, "adj", [P, P])
        self.nsq = self.sb(ctx, "column_sq", [P, C, B])
        self.sc = self.sb(ctx, "scalars", [P, NSCAL])
        self.bias0 = self.sb(ctx, "bias0", [P, 1])
        self.bias3 = self.sb(ctx, "bias3", [P, 1])
        self.idle = {e: nc.alloc_semaphore(name=f"idle_{e}") for e in ("sp", "dve", "pool", "act")}
        self.rn_rows = nc.dram_tensor("rn_rows", (B, N), F32, kind="Internal").ap()

    def sb(self, ctx, name, shape, dt=F32):
        self.n += 1
        return ctx.enter_context(self.nc.sbuf_tensor(f"{name}_{self.n}", shape, dt))

    def ps(self, ctx, name, shape=(P, N), dt=F32):
        self.n += 1
        return ctx.enter_context(self.nc.psum_tensor(f"{name}_{self.n}", list(shape), dt))

    def sem(self, name):
        self.n += 1
        self.taken.append(self.nc.alloc_semaphore(name=f"{name}_{self.n}"))
        return self.taken[-1]

    def release_semaphores(self):
        self.nc.clear_and_free_semaphores(self.taken)
        self.taken = []
        self.nc.all_engine_barrier()

    def s(self, k):
        return self.sc[:, k:k + 1]


class Chain:

    def __init__(self, eng, sem):
        self.eng, self.sem, self.n = eng, sem, 0

    def __call__(self, ins):
        self.n += 1
        ins.then_inc(self.sem, 1)
        self.eng.wait_ge(self.sem, self.n)


def prepare(k, w, x, adj, b0, b1, b3, wl, wg, wv, wo, gate, logsig):
    nc = k.nc
    x_in = [k.sem(f"x_in{q}") for q in range(8)]
    wsem = {n: k.sem(f"{n}_in") for n in ("small", "wl", "wg", "wv", "wo")}
    consts, zeroed = k.sem("consts_set"), k.sem("ident_zeroed")
    tr_done, tr_used = k.sem("transposed"), k.sem("transpose_copied")
    mx, mxall = k.sem("maxima"), k.sem("maxima_all")
    woT_ready, prod, prod_used = k.sem("woT_ready"), k.sem("product"), k.sem("product_copied")
    m_max, m_all, hi_done, vchain, achain = (k.sem("m_max"), k.sem("m_all"), k.sem("hi_done"), k.sem("dve_chain"),
                                             k.sem("act_chain"))
    split_go = k.sem("scales_ready")
    mm_go = k.sem("m_scale_ready")
    with ExitStack() as ctx:
        nat = {n: k.sb(ctx, f"{n}_nat", [P, C, N]) for n in ("a", "b")}
        t32 = k.sb(ctx, "t32", [P, C, N])
        m32 = k.sb(ctx, "m32", [P, C, N])
        tp = [k.ps(ctx, f"tp{i}") for i in range(4)]
        mp = [k.ps(ctx, f"mp{i}") for i in range(4)]
        rows = lambda t: t.rearrange("(c p) n -> p c n", p=P)
        jobs = [("wl", "a"), ("wg", "b"), ("wo", "a")]
        with nc.Block() as block:
            @block.sync
            def _(sp):
                sp.dma_start(k.adj[:], adj).then_inc(wsem["small"], 16)
                sp.dma_start(k.bias0[:], b0.rearrange("(p o) -> p o", o=1)).then_inc(wsem["small"], 16)
                sp.dma_start(k.bias3[:], b3.rearrange("(p o) -> p o", o=1)).then_inc(wsem["small"], 16)
                sp.dma_start(k.s(GATE), gate.rearrange("(a b) -> a b", a=1).broadcast_to([P, 1])).then_inc(wsem["small"], 16)
                sp.dma_start(k.s(SIG), logsig.rearrange("(a b) -> a b", a=1).broadcast_to([P, 1])).then_inc(wsem["small"], 16)
                sp.dma_start(nat["a"][:], rows(wl)).then_inc(wsem["wl"], 16)
                sp.dma_start(nat["b"][:], rows(wg)).then_inc(wsem["wg"], 16)
                sp.wait_ge(tr_done, 4)
                sp.wait_ge(mx, 2)
                sp.dma_start(nat["a"][:], rows(wo)).then_inc(wsem["wo"], 16)
                sp.wait_ge(tr_done, 8)
                sp.wait_ge(mx, 3)
                sp.dma_start(nat["b"][:], rows(wv)).then_inc(wsem["wv"], 16)
                for q in range(16):
                    sp.dma_start(k.X[:, 4 * q:4 * q + 4, :],
                                 x[4 * q:4 * q + 4].rearrange("b l n -> l b n")).then_inc(x_in[q // 2], 16)

            @block.gpsimd
            def _(pool):
                pool.memset(k.ident[:], 0.0).then_inc(zeroed, 1)
                pool.memset(k.ones[:], 1.0).then_inc(consts, 1)
                pool.memset(k.s(HALF), -0.5).then_inc(consts, 1)
                pool.wait_ge(zeroed, 1)
                pool.affine_select(out=k.ident[:], in_=k.ident[:], compare_op=ALU.not_equal, fill=1.0, base=0,
                                   pattern=[[-1, P]], channel_multiplier=1).then_inc(consts, 1)
                pool.wait_ge(mx, 3)
                pool.partition_all_reduce(k.sc[:, M_ADJ:M_WG + 1], k.sc[:, M_ADJ:M_WG + 1], P, ABSMAX).then_inc(mxall, 1)
                pool.wait_ge(m_max, 1)
                pool.partition_all_reduce(k.s(M_M), k.s(M_M), P, ABSMAX).then_inc(m_all, 1)

            @block.tensor
            def _(pe):
                pe.wait_ge(consts, 3)
                for j, (name, buf) in enumerate(jobs):
                    pe.wait_ge(wsem[name], 16)
                    for c in range(C):
                        need(pe, tr_used, C * (j - 1) + c + 1)
                        for r in range(C):
                            last = nc.tensor.transpose(tp[c][:, r * P:(r + 1) * P], nat[buf][:, r, c * P:(c + 1) * P],
                                                       k.ident[:])
                        last.then_inc(tr_done, 1)
                pe.wait_ge(wsem["wv"], 16)
                pe.wait_ge(tr_used, 3 * C)
                for d in range(C):
                    for e in range(C):
                        last = nc.tensor.matmul(mp[d][:], nat["b"][:, e, d * P:(d + 1) * P], t32[:, e, :],
                                                start=(e == 0), stop=(e == C - 1))
                    last.then_inc(prod, 1)

            @block.vector
            def _(dve):
                ch = Chain(dve, vchain)
                red = dict(axis=mybir.AxisListType.XY, op=ALU.max, apply_absolute_value=True)
                dve.wait_ge(wsem["small"], 80)
                nc.vector.tensor_reduce(k.s(M_ADJ), k.adj[:], axis=AX_X, op=ALU.max,
                                        apply_absolute_value=True).then_inc(mx, 1)
                dve.wait_ge(wsem["wl"], 16)
                nc.vector.tensor_reduce(k.s(M_WL), nat["a"][:], **red).then_inc(mx, 1)
                dve.wait_ge(wsem["wg"], 16)
                nc.vector.tensor_reduce(k.s(M_WG), nat["b"][:], **red).then_inc(mx, 1)
                dve.wait_ge(mxall, 1)
                ch(nc.vector.tensor_scalar(k.sc[:, M_ADJ:M_WG + 1], k.sc[:, M_ADJ:M_WG + 1], 1e-18, 1.0 / S_W,
                                           ALU.max, ALU.mult))
                ch(nc.vector.reciprocal(k.sc[:, W_ADJ:W_WG + 1], k.sc[:, M_ADJ:M_WG + 1]))
                ch(nc.vector.tensor_scalar(k.s(W_SQ), k.s(W_ADJ), k.s(W_ADJ), 1.0 / S_W, ALU.mult, ALU.mult))
                ch(nc.vector.tensor_scalar(k.s(EPS_L), k.s(W_WL), 1e-8 * S_LN * S_EVAC, None, ALU.mult))
                ch(nc.vector.tensor_scalar(k.s(EPS_L), k.s(EPS_L), k.s(EPS_L), None, ALU.mult))
                ch(nc.vector.tensor_scalar(k.s(TMP_A), k.s(W_SQ), S_LN, None, ALU.mult))
                ch(nc.vector.reciprocal(k.s(F_L1), k.s(TMP_A)))
                dve.wait_ge(achain, 2)
                ch(nc.vector.tensor_scalar(k.s(TMP_A), k.s(W_WG), S_LN * S_EVAC, None, ALU.mult))
                ch(nc.vector.reciprocal(k.s(TMP_B), k.s(TMP_A)))
                ch(nc.vector.tensor_scalar(k.s(TMP_A), k.s(TMP_B), k.s(TMP_B), k.s(SIG), ALU.mult, ALU.mult))
                ch(nc.vector.tensor_copy(k.s(K_G), k.s(TMP_A)))
                ch(nc.vector.tensor_scalar(k.s(TMP_B), k.s(GATE), 1.0, None, ALU.add))
                ch(nc.vector.reciprocal(k.s(GATE), k.s(TMP_B)))
                ch(nc.vector.tensor_scalar(k.s(UNGATE), k.s(GATE), -1.0, 1.0, ALU.mult, ALU.add))
                dst = [(w["wl_h"], w["wl_l"], W_WL), (w["wg_h"], w["wg_l"], W_WG)]
                for j in range(2):
                    hi, lo, scale = dst[j]
                    for c in range(C):
                        dve.wait_ge(hi_done, C * j + c + 1)
                        nc.vector.scalar_tensor_tensor(lo[:, c, :], tp[c][:], k.s(scale), hi[:, c, :], ALU.mult,
                                                       ALU.subtract).then_inc(tr_used, 1)
                for c in range(C):
                    dve.wait_ge(tr_done, 2 * C + c + 1)
                    nc.vector.tensor_copy(t32[:, c, :], tp[c][:]).then_inc(tr_used, 1)
                for d in range(C):
                    dve.wait_ge(prod, d + 1)
                    ch(nc.vector.tensor_copy(m32[:, d, :], mp[d][:]))
                nc.vector.tensor_reduce(k.s(M_M), m32[:], **red).then_inc(m_max, 1)
                dve.wait_ge(m_all, 1)
                ch(nc.vector.tensor_scalar(k.s(M_M), k.s(M_M), 1e-18, 1.0 / S_W, ALU.max, ALU.mult))
                ch(nc.vector.reciprocal(k.s(W_M), k.s(M_M)))
                ch(nc.vector.tensor_scalar(k.s(F_OUT2), k.s(M_M), 1.0 / (S_K * S_EVAC * S_LN), None, ALU.mult))
                for d in range(C):
                    ch(nc.vector.tensor_scalar(w["m_h"][:, d, :], m32[:, d, :], k.s(W_M), None, ALU.mult))
                    ch(nc.vector.scalar_tensor_tensor(w["m_l"][:, d, :], m32[:, d, :], k.s(W_M), w["m_h"][:, d, :],
                                                      ALU.mult, ALU.subtract))

            @block.scalar
            def _(act):
                act.wait_ge(wsem["small"], 80)
                nc.scalar.activation(k.s(SIG), k.s(SIG), ACT.Exp, scale=-2.0).then_inc(achain, 1)
                nc.scalar.activation(k.s(GATE), k.s(GATE), ACT.Exp, scale=-1.0).then_inc(achain, 1)
                act.wait_ge(vchain, 2)
                dst = [(w["wl_h"], W_WL), (w["wg_h"], W_WG)]
                for j in range(2):
                    hi, scale = dst[j]
                    for c in range(C):
                        act.wait_ge(tr_done, C * j + c + 1)
                        nc.scalar.activation(hi[:, c, :], tp[c][:], ACT.Copy, scale=k.s(scale)).then_inc(hi_done, 1)
    return x_in


def first_norms(k, x_in):
    nc = k.nc
    sq_ready, sums, sums_used = k.sem("sq_ready"), k.sem("sums"), k.sem("sums_used")
    with ExitStack() as ctx:
        sq = k.sb(ctx, "sq", [P, 2, N])
        ps = [k.ps(ctx, f"sum{i}", (P, G * C)) for i in range(2)]
        per = B // len(x_in)
        with nc.Block() as block:
            @block.scalar
            def _(act):
                for q in range(len(x_in)):
                    act.wait_ge(x_in[q], 32)
                    for i in range(per):
                        b = q * per + i
                        need(act, sums, b - 1)
                        nc.scalar.activation(sq[:, b % 2, :], k.X[:, b, :], ACT.Square).then_inc(sq_ready, 1)

            @block.tensor
            def _(pe):
                def group(g, slot, i):
                    need(pe, sums_used, g - 1)
                    for j in range(G):
                        pe.wait_ge(sq_ready, g * G + j + 1)
                        for c in range(C):
                            last = nc.tensor.matmul(ps[slot][:, j * C + c:j * C + c + 1], sq[:, j % 2, c * P:(c + 1) * P],
                                                    k.ones[:, 0:1], start=True, stop=True)
                        last.then_inc(sums, 1)
                group(0, 0, 0)
                group(1, 1, 1)
                with strided(pe, 2, NG, 2) as g:
                    group(g, 0, g)
                    group(g + 1, 1, g)

            @block.vector
            def _(dve):
                with strided(dve, 0, NG, 2) as g:
                    for j in range(2):
                        dve.wait_ge(sums, (g + j + 1) * G)
                        nc.vector.tensor_copy(k.nsq[:, :, bass.ds((g + j) * G, G)].rearrange("p c b -> p b c"),
                                              ps[j][:].rearrange("p (b c) -> p b c", b=G)).then_inc(sums_used, 1)


def similarity(k, ctx_out, after):
    nc = k.nc
    pair = [k.ps(ctx_out, f"pair{i}") for i in range(C)]
    diag = k.ps(ctx_out, "diag")
    R = 4
    chain, pw, trn, rows_ready, rows_out, gmax, gmax_all = (k.sem("rn_chain"), k.sem("rn_pow"), k.sem("rn_transposed"),
        k.sem("rn_rows_ready"), k.sem("rn_rows_out"), k.sem("gmax"), k.sem("gmax_all"))
    rn_in = [k.sem(f"rn_in{r}") for r in range(R)]
    rn_ready = k.sem("rn_ready")
    unit_ready, hi_ready, lo_ready, gram_done = k.sem("unit_ready"), k.sem("hi_ready"), k.sem("lo_ready"), k.sem("gram_done")
    with ExitStack() as ctx:
        rn, d, root = (k.sb(ctx, n, [P, C, B]) for n in ("rn", "clamped_sq", "root"))
        rnT = k.sb(ctx, "rnT", [B, N])
        rnb = k.sb(ctx, "rn_bcast", [P, R, N])
        unit = k.sb(ctx, "unit", [P, R, N])
        hi = k.sb(ctx, "unit_hi", [P, R, N], F16)
        lo = k.sb(ctx, "unit_lo", [P, R, N], F16)
        tp = k.ps(ctx, "rn_tp")
        with nc.Block() as block:
            @block.sync
            def _(sp):
                sp.wait_ge(rows_ready, 1)
                sp.dma_start(k.rn_rows, rnT[:]).then_inc(rows_out, 16)
                sp.wait_ge(rows_out, 16)

                def load(b, r):
                    if not isinstance(b, int) or b >= R:
                        settle(sp, unit_ready, b - R + 1, k.idle["sp"])
                    sp.dma_start(rnb[:, r, :], k.rn_rows[b].partition_broadcast(P)).then_inc(rn_in[r], 16)
                for r in range(R):
                    load(r, r)
                with strided(sp, R, B, R) as base:
                    for r in range(R):
                        load(base + r, r)

            @block.gpsimd
            def _(pool):
                pool.wait_ge(gmax, 1)
                pool.partition_all_reduce(k.s(NSQ_MAX), k.s(NSQ_MAX), P, RMAX).then_inc(gmax_all, 1)

            @block.tensor
            def _(pe):
                pe.wait_ge(rn_ready, 1)
                for c in range(C):
                    last = nc.tensor.transpose(tp[0:B, c * P:(c + 1) * P], rn[:, c, :], k.ident[:])
                last.then_inc(trn, 1)

                def gram(b, r, first, final):
                    pe.wait_ge(lo_ready, b + 1)
                    pe.wait_ge(hi_ready, b + 1)
                    for i in range(C):
                        stat = hi[:, r, i * P:(i + 1) * P]
                        nc.tensor.matmul(pair[i][:], stat, lo[:, r, :], start=first, stop=False, skip_group_check=True)
                        if i < C - 1:
                            nc.tensor.matmul(pair[i][:, (i + 1) * P:], stat, hi[:, r, (i + 1) * P:], start=False,
                                             stop=final, skip_group_check=True)
                        last = nc.tensor.matmul(diag[:, i * P:(i + 1) * P], stat, stat, start=(first and i == 0),
                                                stop=final, skip_group_check=True)
                    last.then_inc(gram_done, 1)
                for r in range(R):
                    gram(r, r, r == 0, False)
                with strided(pe, R, B - R, R) as base:
                    for r in range(R):
                        gram(base + r, r, False, False)
                for r in range(R):
                    gram(B - R + r, r, False, r == R - 1)

            @block.vector
            def _(dve):
                ch = Chain(dve, chain)
                ch(nc.vector.tensor_scalar(d[:], k.nsq[:], 1e-24, None, ALU.max))
                nc.vector.tensor_reduce(k.s(NSQ_MAX), k.nsq[:], axis=mybir.AxisListType.XY, op=ALU.max).then_inc(gmax, 1)
                dve.wait_ge(pw, 1)
                ch(nc.vector.reciprocal(rn[:], root[:]))
                ch(nc.vector.tensor_tensor(root[:], rn[:], rn[:], ALU.mult))
                ch(nc.vector.scalar_tensor_tensor(root[:], d[:], -0.5, root[:], ALU.mult, ALU.mult))
                nc.vector.scalar_tensor_tensor(rn[:], root[:], 1.5, rn[:], ALU.add, ALU.mult).then_inc(rn_ready, 1)
                dve.wait_ge(trn, 1)
                nc.vector.tensor_scalar(rnT[:], tp[0:B, :], S_RN, None, ALU.mult).then_inc(rows_ready, 1)

                def units(base, start):
                    for r in range(R):
                        b = base + r
                        dve.wait_ge(rn_in[r], (b // R + 1) * 16 if isinstance(b, int) else (base // R + 1) * 16)
                        if not start:
                            dve.wait_ge(hi_ready, b - R + 1)
                            dve.wait_ge(lo_ready, b - R + 1)
                        nc.vector.tensor_tensor(unit[:, r, :], k.X[:, b, :], rnb[:, r, :], ALU.mult).then_inc(unit_ready, 1)
                    for r in range(R):
                        b = base + r
                        dve.wait_ge(hi_ready, b + 1)
                        if not start:
                            dve.wait_ge(gram_done, b - R + 1)
                        nc.vector.tensor_tensor(lo[:, r, :], unit[:, r, :], hi[:, r, :], ALU.subtract).then_inc(lo_ready, 1)
                units(0, True)
                with strided(dve, R, B, R) as base:
                    units(base, False)

            @block.scalar
            def _(act):
                act.wait_ge(chain, 1)
                nc.scalar.activation(root[:], d[:], ACT.Sqrt).then_inc(pw, 1)

                def split(b, r, start):
                    act.wait_ge(unit_ready, b + 1)
                    if not start:
                        act.wait_ge(gram_done, b - R + 1)
                    nc.scalar.activation(hi[:, r, :], unit[:, r, :], ACT.Copy).then_inc(hi_ready, 1)
                for r in range(R):
                    split(r, r, True)
                with strided(act, R, B, R) as base:
                    for r in range(R):
                        split(base + r, r, False)
    return pair, diag


def neighbours(k, pair, diag, an_h, an_l, wa_h, wa_l):
    nc = k.nc
    copied, tr, simsum, dsum, masked, rounds, taken = (k.sem("copied"), k.sem("tr"), k.sem("sim_sum"), k.sem("diag_added"),
        k.sem("masked"), k.sem("rounds"), k.sem("taken"))
    dd_ready = k.sem("dinv_diag_ready")
    a_ready, deg, deg_c, pw, an_max, an_all, ch_s, ach = (k.sem("a_ready"), k.sem("deg"), k.sem("deg_clamped"), k.sem("deg_pow"),
        k.sem("an_max"), k.sem("an_all"), k.sem("chain"), k.sem("an_hi"))
    SIM = 1.0 / (S_RN * S_RN * B)
    with ExitStack() as ctx:
        raw = k.sb(ctx, "raw", [P, C, N])
        sim = k.sb(ctx, "sim", [P, C, N])
        work = k.sb(ctx, "work", [P, C, N])
        m8 = k.sb(ctx, "m8", [P, C, 8])
        degc = k.sb(ctx, "degc", [P, 2, C])
        degr = k.sb(ctx, "degr", [P, N])
        mxp = k.sb(ctx, "mxp", [P, 1])
        tp = [k.ps(ctx, f"tp{i}") for i in range(2)]
        dr = tp[0]
        dc = tp[1]
        with nc.Block() as block:
            @block.scalar
            def _(act):
                for i in range(C):
                    nc.scalar.activation(raw[:, i, :], pair[i][:], ACT.Copy, scale=SIM).then_inc(copied, 1)
                act.wait_ge(an_all, 2)
                for i in range(C):
                    nc.scalar.activation(an_h[:, i, :], sim[:, i, :], ACT.Copy, scale=k.s(SAN)).then_inc(ach, 1)

            @block.tensor
            def _(pe):
                pe.wait_ge(copied, C)
                for i in range(C):
                    need(pe, simsum, i - 1)
                    for j in range(C):
                        last = nc.tensor.transpose(tp[i % 2][:, j * P:(j + 1) * P], raw[:, j, i * P:(i + 1) * P], k.ident[:])
                    last.then_inc(tr, 1)
                pe.wait_ge(a_ready, C)
                for c in range(C):
                    for i in range(C):
                        last = nc.tensor.matmul(dc[:, c:c + 1], raw[:, i, c * P:(c + 1) * P], k.ones[:, 0:1],
                                                start=(i == 0), stop=(i == C - 1))
                last.then_inc(deg, 1)
                pe.wait_ge(dd_ready, 1)
                nc.tensor.matmul(dr[:], k.ones[:], degr[:], start=True, stop=True).then_inc(deg, 1)

            @block.gpsimd
            def _(pool):
                for i in range(C):
                    pool.wait_ge(dsum, i + 1)
                    where = dict(compare_op=ALU.not_equal, base=i * P, pattern=[[-1, N]], channel_multiplier=1)
                    pool.affine_select(out=work[:, i, :], in_=sim[:, i, :], fill=SENT, **where).then_inc(masked, 1)
                    pool.wait_ge(masked, 2 * i + 1)
                    pool.affine_select(out=sim[:, i, :], in_=sim[:, i, :], fill=0.0, **where).then_inc(masked, 1)
                half = k.s(HALF)
                pool.wait_ge(deg_c, 1)
                pool.tensor_tensor(degc[:, 1, :], degc[:, 1, :], half.broadcast_to([P, C]), ALU.pow).then_inc(pw, 1)
                pool.tensor_tensor(k.s(TMP_A), k.s(TMP_A), half, ALU.pow).then_inc(pw, 1)
                pool.wait_ge(an_max, 1)
                pool.partition_all_reduce(mxp[:], mxp[:], P, ABSMAX).then_inc(an_all, 1)

            @block.vector
            def _(dve):
                ch = Chain(dve, ch_s)
                for i in range(C):
                    dve.wait_ge(tr, i + 1)
                    nc.vector.tensor_tensor(sim[:, i, :], raw[:, i, :], tp[i % 2][:], ALU.add).then_inc(simsum, 1)
                    dve.wait_ge(simsum, i + 1)
                    blk = slice(i * P, (i + 1) * P)
                    nc.vector.scalar_tensor_tensor(sim[:, i, blk], diag[:, blk], SIM, sim[:, i, blk], ALU.mult,
                                                   ALU.add).then_inc(dsum, 1)
                ch(nc.vector.tensor_scalar(wa_h[:], k.adj[:], k.s(W_ADJ), None, ALU.mult))
                ch(nc.vector.scalar_tensor_tensor(wa_l[:], k.adj[:], k.s(W_ADJ), wa_h[:], ALU.mult, ALU.subtract))
                dve.wait_ge(masked, 2 * C)

                def round_of_eight(t):
                    for i in range(C):
                        if not (isinstance(t, int) and t == 0):
                            settle(dve, rounds, (t - 1) * 2 * C + C + i + 1, k.idle["dve"])
                        nc.vector.max(m8[:, i, :], work[:, i, :]).then_inc(rounds, 1)
                    for i in range(C):
                        settle(dve, rounds, t * 2 * C + i + 1, k.idle["dve"])
                        nc.vector.match_replace(work[:, i, :], m8[:, i, :], work[:, i, :], SENT).then_inc(rounds, 1)
                round_of_eight(0)
                with dve.Fori(1, ROUNDS) as t:
                    round_of_eight(t)
                done = ROUNDS * 2 * C
                for i in range(C):
                    dve.wait_ge(rounds, done - C + i + 1)
                    nc.vector.max(m8[:, i, :], work[:, i, :]).then_inc(rounds, 1)
                for i in range(C):
                    dve.wait_ge(rounds, done + i + 1)
                    nc.vector.memset(m8[:, i, 1:8], SENT).then_inc(rounds, 1)
                for i in range(C):
                    dve.wait_ge(rounds, done + C + i + 1)
                    nc.vector.match_replace(work[:, i, :], m8[:, i, :], work[:, i, :], SENT).then_inc(rounds, 1)
                for i in range(C):
                    dve.wait_ge(rounds, done + 2 * C + i + 1)
                    nc.vector.scalar_tensor_tensor(raw[:, i, :], work[:, i, :], SENT, sim[:, i, :], ALU.is_equal,
                                                   ALU.mult).then_inc(a_ready, 1)
                dve.wait_ge(deg, 1)
                ch(nc.vector.tensor_copy(degc[:, 0, :], dc[:, 0:C]))
                ch(nc.vector.tensor_scalar(k.s(TMP_A), k.s(NSQ_MAX), 1e-30, None, ALU.max))
                nc.vector.tensor_scalar(degc[:, 1, :], dc[:, 0:C], 1e-37, None, ALU.max).then_inc(deg_c, 1)
                dve.wait_ge(pw, 2)
                ch(nc.vector.scalar_tensor_tensor(degc[:, 0, :], degc[:, 0, :], 0.0, degc[:, 1, :], ALU.is_gt, ALU.mult))
                nc.vector.tensor_tensor(grouped(degr[:]), over(k.ident[:], C), spread(degc[:, 0, :], P),
                                        ALU.mult).then_inc(dd_ready, 1)
                dve.wait_ge(deg, 2)
                for i in range(C):
                    ch(nc.vector.scalar_tensor_tensor(sim[:, i, :], raw[:, i, :], degc[:, 0, i:i + 1], dr[:],
                                                      ALU.mult, ALU.mult))
                nc.vector.tensor_reduce(mxp[:], sim[:], axis=mybir.AxisListType.XY, op=ALU.max,
                                        apply_absolute_value=True).then_inc(an_max, 1)
                ch(nc.vector.tensor_scalar(k.s(SX), k.s(TMP_A), S_COL, None, ALU.mult))
                dve.wait_ge(an_all, 1)
                ch(nc.vector.tensor_scalar(k.s(TMP_B), mxp[:], 1e-18, 1.0 / S_AN, ALU.max, ALU.mult))
                nc.vector.reciprocal(k.s(SAN), k.s(TMP_B)).then_inc(an_all, 1)
                dve.wait_ge(an_all, 2)
                ch(nc.vector.tensor_scalar(k.s(TMP_A), k.s(SX), k.s(W_ADJ), S_EVAC, ALU.mult, ALU.mult))
                ch(nc.vector.reciprocal(k.s(TMP_C), k.s(TMP_A)))
                ch(nc.vector.tensor_scalar(k.s(F_B), k.s(TMP_C), k.s(TMP_B), None, ALU.mult))
                for i in range(C):
                    dve.wait_ge(ach, i + 1)
                    ch(nc.vector.scalar_tensor_tensor(an_l[:, i, :], sim[:, i, :], k.s(SAN), an_h[:, i, :], ALU.mult,
                                                      ALU.subtract))


def propagate(k, an_h, an_l, wa_h, wa_l, bias, b1, out):
    nc = k.nc
    second = b1 is not None
    (xh_r, xl_r, xw_d, wh_r, wl_r, o_d, t_r, add_r, st_r, ag_r, rs_r, nm_r, ln_r, yh_r, yl_r, m_d, pb_r, add2_r, st2_r,
     ag2_r, rs2_r, nm2_r, ln2_r) = (k.sem(n) for n in (
         "x_hi", "x_lo", "xw_done", "xw_hi", "xw_lo", "out_done", "out_biased", "added", "stats", "moments", "rstd",
         "shift", "normed", "y_hi", "y_lo", "mix_done", "y_biased", "added2", "stats2", "moments2", "rstd2", "shift2",
         "normed2"))
    b1_in, w2_r, ch_s, dummy = k.sem("b1_in"), k.sem("w2_ready"), k.sem("chain"), k.sem("eps_set")
    stored = [k.sem(f"stored{i}") for i in range(4)]
    with ExitStack() as ctx:
        xh, xl = (k.sb(ctx, n, [P, 2, N], F16) for n in ("xh", "xl"))
        wh, wl = (k.sb(ctx, n, [P, 2, N], F16) for n in ("xwh", "xwl"))
        t = k.sb(ctx, "t", [P, 2, N])
        bn = k.sb(ctx, "bn", [P, 2, 6])
        mv = k.sb(ctx, "mv", [P, 4, 2])
        rstd = k.sb(ctx, "rstd", [P, 4, 2])
        if second:
            yh, yl = (k.sb(ctx, n, [P, 2, N], F16) for n in ("yh", "yl"))
            w2 = k.sb(ctx, "w2", [P, P])
            w2h, w2l = (k.sb(ctx, n, [P, P], F16) for n in ("w2h", "w2l"))
            b1b = k.sb(ctx, "b1_bcast", [P, N])
            bn2 = k.sb(ctx, "bn2", [P, 2, 6])
            mv2 = k.sb(ctx, "mv2", [P, 4, 2])
            rstd2 = k.sb(ctx, "rstd2", [P, 4, 2])
            pm = [k.ps(ctx, f"pm{i}") for i in range(2)]
        px = [k.ps(ctx, f"px{i}") for i in range(2)]
        po = [k.ps(ctx, f"po{i}") for i in range(2)]
        depth = 9 if second else 6
        R = 4
        X = k.X
        with nc.Block() as block:
            @block.sync
            def _(sp):
                if second:
                    sp.dma_start(b1b[:], b1.partition_broadcast(P)).then_inc(b1_in, 16)
                    sp.wait_ge(b1_in, 16)
                else:
                    for r in range(4):
                        sp.wait_ge(ln_r, r + 1)
                        sp.dma_start(out[r], X[:, r, :]).then_inc(stored[r], 16)
                    with strided(sp, 4, B, 4) as base:
                        for r in range(4):
                            settle(sp, stored[r], base * 4, k.idle["sp"])
                            settle(sp, ln_r, base + r + 1, k.idle["sp"])
                            sp.dma_start(out[base + r], X[:, base + r, :]).then_inc(stored[r], 16)
                    for r in range(4):
                        sp.wait_ge(stored[r], 16 * B // 4)

            @block.scalar
            def _(act):
                def step(s):
                    if s.live(0):
                        b, r = s.at(0), s.slot(0)
                        settle(act, xw_d, b - 1, k.idle["act"])
                        nc.scalar.activation(xh[:, r, :], X[:, b, :], ACT.Copy, scale=k.s(SX)).then_inc(xh_r, 1)
                    if s.live(2):
                        b, r = s.at(2), s.slot(2)
                        act.wait_ge(xw_d, b + 1)
                        need(act, o_d, b - 1)
                        nc.scalar.activation(wh[:, r, :], px[r][:], ACT.Copy, scale=S_EVAC).then_inc(wh_r, 1)
                    if s.live(4):
                        b, r = s.at(4), s.slot(4)
                        act.wait_ge(o_d, b + 1)
                        need(act, add_r, b - 1)
                        nc.scalar.activation(t[:, r, :], po[r][:], ACT.Identity, scale=k.s(F_B), bias=bias[:]).then_inc(t_r, 1)
                    if s.live(6):
                        b, r = s.at(6), s.slot(6, 4)
                        settle(act, nm_r, b + 1, k.idle["act"])
                        nc.scalar.activation(X[:, b, :], X[:, b, :], ACT.Identity, scale=rstd[:, r, 0:1],
                                             bias=rstd[:, r, 1:2]).then_inc(ln_r, 1)
                        if second:
                            act.wait_ge(ln_r, b + 1)
                            settle(act, m_d, b - 1, k.idle["act"])
                            nc.scalar.activation(yh[:, s.slot(6), :], X[:, b, :], ACT.Copy, scale=S_LN).then_inc(yh_r, 1)
                    if second and s.live(9):
                        b, r = s.at(9), s.slot(9, 4)
                        settle(act, nm2_r, b + 1, k.idle["act"])
                        nc.scalar.activation(X[:, b, :], X[:, b, :], ACT.Identity, scale=rstd2[:, r, 0:1],
                                             bias=rstd2[:, r, 1:2]).then_inc(ln2_r, 1)
                pipeline(act, B, depth, R, step)

            @block.vector
            def _(dve):
                if second:
                    ch = Chain(dve, ch_s)
                    ch(nc.vector.tensor_tensor(w2[:], k.adj[:], k.adj[:], ALU.mult))
                    ch(nc.vector.tensor_scalar(w2h[:], w2[:], k.s(W_SQ), None, ALU.mult))
                    nc.vector.scalar_tensor_tensor(w2l[:], w2[:], k.s(W_SQ), w2h[:], ALU.mult,
                                                   ALU.subtract).then_inc(w2_r, 1)

                idle = k.idle["dve"]

                def step(s):
                    if s.live(0):
                        b, r = s.at(0), s.slot(0)
                        dve.wait_ge(xh_r, b + 1)
                        need(dve, xw_d, b - 1)
                        nc.vector.scalar_tensor_tensor(xl[:, r, :], X[:, b, :], k.s(SX), xh[:, r, :], ALU.mult,
                                                       ALU.subtract).then_inc(xl_r, 1)
                    if s.live(2):
                        b, r = s.at(2), s.slot(2)
                        dve.wait_ge(wh_r, b + 1)
                        need(dve, o_d, b - 1)
                        nc.vector.scalar_tensor_tensor(wl[:, r, :], px[r][:], S_EVAC, wh[:, r, :], ALU.mult,
                                                       ALU.subtract).then_inc(wl_r, 1)
                    if s.live(5):
                        b, r, q = s.at(5), s.slot(5), s.slot(5, 4)
                        dve.wait_ge(t_r, b + 1)
                        nc.vector.tensor_tensor(X[:, b, :], X[:, b, :], t[:, r, :], ALU.add).then_inc(add_r, 1)
                        settle(dve, add_r, b + 1, idle)
                        nc.vector.bn_stats(bn[:, r, :], X[:, b, :]).then_inc(st_r, 1)
                        settle(dve, st_r, b + 1, idle)
                        settle(dve, nm_r, b - 3, idle)
                        nc.vector.bn_aggr(mv[:, q, :], bn[:, r, :]).then_inc(ag_r, 1)
                    if second and s.live(6):
                        b, r = s.at(6), s.slot(6)
                        dve.wait_ge(yh_r, b + 1)
                        need(dve, m_d, b - 1)
                        nc.vector.scalar_tensor_tensor(yl[:, r, :], X[:, b, :], S_LN, yh[:, r, :], ALU.mult,
                                                       ALU.subtract).then_inc(yl_r, 1)
                    if second and s.live(8):
                        b, r, q = s.at(8), s.slot(8), s.slot(8, 4)
                        dve.wait_ge(m_d, b + 1)
                        dve.wait_ge(pb_r, b + 1)
                        nc.vector.scalar_tensor_tensor(X[:, b, :], pm[r][:], k.s(F_L1), X[:, b, :], ALU.mult,
                                                       ALU.add).then_inc(add2_r, 1)
                        settle(dve, add2_r, b + 1, idle)
                        nc.vector.bn_stats(bn2[:, r, :], X[:, b, :]).then_inc(st2_r, 1)
                        settle(dve, st2_r, b + 1, idle)
                        settle(dve, nm2_r, b - 3, idle)
                        nc.vector.bn_aggr(mv2[:, q, :], bn2[:, r, :]).then_inc(ag2_r, 1)
                pipeline(dve, B, depth, R, step)

            @block.gpsimd
            def _(pool):
                def moments(b, q, mvt, rst, aggr, rsem, nsem, lns):
                    need(pool, lns, b - 3)
                    settle(pool, aggr, b + 1, k.idle["pool"])
                    pool.tensor_scalar(rst[:, q, 1:2], mvt[:, q, 1:2], LN_EPS, None, ALU.add).then_inc(rsem, 1)
                    pool.wait_ge(rsem, 2 * b + 1)
                    pool.tensor_tensor(rst[:, q, 0:1], rst[:, q, 1:2], k.s(HALF), ALU.pow).then_inc(rsem, 1)
                    settle(pool, rsem, 2 * b + 2, k.idle["pool"])
                    pool.tensor_scalar(rst[:, q, 1:2], mvt[:, q, 0:1], rst[:, q, 0:1], -1.0, ALU.mult,
                                       ALU.mult).then_inc(nsem, 1)

                if second:
                    pool.wait_ge(b1_in, 16)

                def step(s):
                    if s.live(5):
                        moments(s.at(5), s.slot(5, 4), mv, rstd, ag_r, rs_r, nm_r, ln_r)
                    if second and s.live(7):
                        b = s.at(7)
                        pool.wait_ge(yl_r, b + 1)
                        pool.wait_ge(yh_r, b + 1)
                        pool.tensor_tensor(X[:, b, :], X[:, b, :], b1b[:], ALU.add).then_inc(pb_r, 1)
                    if second and s.live(8):
                        moments(s.at(8), s.slot(8, 4), mv2, rstd2, ag2_r, rs2_r, nm2_r, ln2_r)
                pipeline(pool, B, depth, R, step)

            @block.tensor
            def _(pe):
                if second:
                    pe.wait_ge(w2_r, 1)

                def step(s):
                    if s.live(1):
                        b, r = s.at(1), s.slot(1)
                        pe.wait_ge(xl_r, b + 1)
                        need(pe, wl_r, b - 1)
                        for c in range(C):
                            cs = slice(c * P, (c + 1) * P)
                            nc.tensor.matmul(px[r][:, cs], xh[:, r, cs], wa_h[:], start=True, stop=False)
                            nc.tensor.matmul(px[r][:, cs], xh[:, r, cs], wa_l[:], start=False, stop=False)
                            last = nc.tensor.matmul(px[r][:, cs], xl[:, r, cs], wa_h[:], start=False, stop=True)
                        last.then_inc(xw_d, 1)
                    if s.live(3):
                        b, r = s.at(3), s.slot(3)
                        pe.wait_ge(wl_r, b + 1)
                        need(pe, t_r, b - 1)
                        for c in range(C):
                            cs = slice(c * P, (c + 1) * P)
                            nc.tensor.matmul(po[r][:], wh[:, r, cs], an_h[:, c, :], start=(c == 0), stop=False)
                            nc.tensor.matmul(po[r][:], wh[:, r, cs], an_l[:, c, :], start=False, stop=False)
                            last = nc.tensor.matmul(po[r][:], wl[:, r, cs], an_h[:, c, :], start=False, stop=(c == C - 1))
                        last.then_inc(o_d, 1)
                    if second and s.live(7):
                        b, r = s.at(7), s.slot(7)
                        pe.wait_ge(yl_r, b + 1)
                        need(pe, add2_r, b - 1)
                        nc.tensor.matmul(pm[r][:], w2h[:], yh[:, r, :], start=True, stop=False)
                        nc.tensor.matmul(pm[r][:], w2h[:], yl[:, r, :], start=False, stop=False)
                        nc.tensor.matmul(pm[r][:], w2l[:], yh[:, r, :], start=False, stop=True).then_inc(m_d, 1)
                pipeline(pe, B, depth, R, step)


def adaptive_layer(k, bias, b1, out):
    with ExitStack() as banks:
        pair, diag = similarity(k, banks, None)
        with ExitStack() as ctx:
            an_h, an_l = (k.sb(ctx, n, [P, C, N], F16) for n in ("an_h", "an_l"))
            wa_h, wa_l = (k.sb(ctx, n, [P, P], F16) for n in ("wa_h", "wa_l"))
            neighbours(k, pair, diag, an_h, an_l, wa_h, wa_l)
            banks.close()
            propagate(k, an_h, an_l, wa_h, wa_l, bias, b1, out)


def kernel_mix(k, w):
    nc, X, idle = k.nc, k.X, k.idle["dve"]
    (st_in, t_d, h_h, h_l, zl_d, zl_h, zl_l, zg_d, zg_h, zg_l, gl_d, gg_d, relu_r, mask_r, diag_r, dd_r, bc_d, bc_u, u_r, e_r,
     em_r, k_r, kt_d, kt_h, kt_l, v_d, v_h, v_l, o_d, o_u, bn_r, mv_r, rs_r, nm_r, ln_r, sq_r, ns_d, ns_u, ksm, msk_r, diag_pow) = (
        k.sem(n) for n in (
            "stage_in", "xT_done", "xT_hi", "xT_lo", "zl_done", "zl_hi", "zl_lo", "zg_done", "zg_hi", "zg_lo", "gram_l_done",
            "gram_g_done", "relu_ready", "masked_l", "diag_chain", "diag_ready", "bcast_done", "bcast_used", "u_ready",
            "exp_ready", "masked_g", "k_ready", "kT_done", "kT_hi", "kT_lo", "v_done", "v_hi", "v_lo", "out_done",
            "out_added", "stats", "moments", "rstd", "shift", "normed", "sq_ready", "sums_done", "sums_used", "k_chain",
            "mask_ready", "length_pow"))
    with ExitStack() as ctx:
        stage = k.sb(ctx, "stage", [P, G, N])
        xT_h, xT_l, zl_hi, zl_lo, zg_hi, zg_lo, v_hi, v_lo = (
            k.sb(ctx, n, [P, C, N], F16) for n in ("xT_h", "xT_l", "zl_h", "zl_l", "zg_h", "zg_l", "v_h", "v_l"))
        kT_hi, kT_lo = (k.sb(ctx, n, [P, N], F16) for n in ("kT_h", "kT_l"))
        dl, dg, gs, es = (k.sb(ctx, n, [P, N]) for n in ("dl", "dg", "gs", "es"))
        sq = k.sb(ctx, "sq", [P, N])
        mask = k.sb(ctx, "mask", [P, P])
        dia = k.sb(ctx, "dia", [P, 2, G])
        rn = k.sb(ctx, "rnl", [P, G])
        hs = k.sb(ctx, "half_sq", [P, G])
        sm = k.sb(ctx, "small", [P, 4, G])
        bn = k.sb(ctx, "bn", [P, G, 6])
        mv = k.sb(ctx, "mv", [P, G, 2])
        rs = k.sb(ctx, "rs", [P, 2, G])
        work = [k.ps(ctx, f"work{i}") for i in range(4)]
        pgl, pgg, pbc, pkt = (k.ps(ctx, n) for n in ("gram_l", "gram_g", "bcast", "kT"))
        with nc.Block() as block:
            @block.sync
            def _(sp):
                def load(g):
                    sp.dma_start(stage[:], X[:, bass.ds(g * G, G), :]).then_inc(st_in, 16)
                load(0)
                with sp.Fori(1, NG) as g:
                    settle(sp, t_d, g * C, k.idle["sp"])
                    load(g)

            @block.tensor
            def _(pe):
                def transposes(g):
                    pe.wait_ge(st_in, (g + 1) * 16)
                    for d in range(C):
                        need(pe, v_l, (g - 1) * G + d + 1)
                        for j in range(G):
                            last = nc.tensor.transpose(work[d][:, j * P:(j + 1) * P], stage[:, j, d * P:(d + 1) * P],
                                                       k.ident[:])
                        last.then_inc(t_d, 1)

                def project(g, w_h, w_l, free, done):
                    for e in range(C):
                        pe.wait_ge(free, g * C + e + 1)
                        if e == 0:
                            pe.wait_ge(h_l, g * C + C)
                        es_ = slice(e * P, (e + 1) * P)
                        for d in range(C):
                            nc.tensor.matmul(work[e][:], w_h[:, d, es_], xT_h[:, d, :], start=(d == 0), stop=False)
                            nc.tensor.matmul(work[e][:], w_h[:, d, es_], xT_l[:, d, :], start=False, stop=False)
                            last = nc.tensor.matmul(work[e][:], w_l[:, d, es_], xT_h[:, d, :], start=False,
                                                    stop=(d == C - 1))
                        last.then_inc(done, 1)

                def gram(bank, z_h, z_l, done):
                    for j in range(G):
                        js = slice(j * P, (j + 1) * P)
                        for e in range(C):
                            nc.tensor.matmul(bank[:, js], z_h[:, e, js], z_h[:, e, js], start=(e == 0), stop=False)
                            nc.tensor.matmul(bank[:, js], z_h[:, e, js], z_l[:, e, js], start=False, stop=False)
                            last = nc.tensor.matmul(bank[:, js], z_l[:, e, js], z_h[:, e, js], start=False,
                                                    stop=(e == C - 1))
                    last.then_inc(done, 1)

                def norm_sums(s, j):
                    g, bcast = s.at(2), s.live(1)
                    b = g * G + j
                    pe.wait_ge(sq_r, b + 1)
                    if j == 0 and bcast:
                        pe.wait_ge(bc_u, g + 2)
                    if j == 0 and not bcast:
                        need(pe, ns_u, g)
                    for c in range(C):
                        last = nc.tensor.matmul(pbc[:, j * C + c:j * C + c + 1], sq[:, c * P:(c + 1) * P], k.ones[:, 0:1],
                                                start=True, stop=True)
                    last.then_inc(ns_d, 1)

                def step(s):
                    if s.live(0):
                        transposes(s.at(0))
                    if s.live(1):
                        g = s.at(1)
                        pe.wait_ge(dd_r, 2 * g + 2)
                        need(pe, ns_u, g - 1)
                        nc.tensor.matmul(pbc[:], k.ones[:], dl[:], start=True, stop=True)
                        nc.tensor.matmul(pgg[:], k.ones[:], dg[:], start=False, stop=True,
                                         skip_group_check=True).then_inc(bc_d, 1)
                    if s.live(0):
                        project(s.at(0), w["wl_h"], w["wl_l"], h_l, zl_d)
                    if s.live(1):
                        g = s.at(1)
                        pe.wait_ge(k_r, g + 1)
                        need(pe, kt_l, g)
                        for j in range(G):
                            last = nc.tensor.transpose(pkt[:, j * P:(j + 1) * P], gs[:, j * P:(j + 1) * P], k.ident[:])
                        last.then_inc(kt_d, 1)
                    if s.live(2):
                        norm_sums(s, 0)
                    if s.live(0):
                        project(s.at(0), w["wg_h"], w["wg_l"], zl_l, zg_d)
                    if s.live(2):
                        norm_sums(s, 1)
                    if s.live(0):
                        g = s.at(0)
                        pe.wait_ge(zl_l, (g + 1) * C)
                        need(pe, relu_r, g)
                        gram(pgl, zl_hi, zl_lo, gl_d)
                        pe.wait_ge(zg_l, (g + 1) * C)
                        need(pe, u_r, g)
                        gram(pgg, zg_hi, zg_lo, gg_d)
                    if s.live(2):
                        norm_sums(s, 2)
                    if s.live(1):
                        g = s.at(1)
                        pe.wait_ge(kt_l, g + 1)
                        pe.wait_ge(v_l, (g + 1) * G)
                        for j in range(G):
                            js = slice(j * P, (j + 1) * P)
                            if not isinstance(s.i, int) or s.i < NG:
                                pe.wait_ge(zg_l, (g + 1) * C + j + 1)
                            nc.tensor.matmul(work[j][:], kT_hi[:, js], v_hi[:, j, :], start=True, stop=False)
                            nc.tensor.matmul(work[j][:], kT_hi[:, js], v_lo[:, j, :], start=False, stop=False)
                            nc.tensor.matmul(work[j][:], kT_lo[:, js], v_hi[:, j, :], start=False,
                                             stop=True).then_inc(o_d, 1)
                    if s.live(0):
                        g = s.at(0)
                        for j in range(G):
                            js = slice(j * P, (j + 1) * P)
                            need(pe, o_u, (g - 1) * G + j + 1)
                            for d in range(C):
                                nc.tensor.matmul(work[j][:], xT_h[:, d, js], w["m_h"][:, d, :], start=(d == 0), stop=False)
                                nc.tensor.matmul(work[j][:], xT_h[:, d, js], w["m_l"][:, d, :], start=False, stop=False)
                                last = nc.tensor.matmul(work[j][:], xT_l[:, d, js], w["m_h"][:, d, :], start=False,
                                                        stop=(d == C - 1))
                            last.then_inc(v_d, 1)
                    if s.live(2):
                        norm_sums(s, 3)
                pipeline(pe, NG, 2, 1, step)

            @block.scalar
            def _(act):
                def square(g, j):
                    b = g * G + j
                    need(act, ns_d, b)
                    settle(act, ln_r, b + 1, k.idle["act"])
                    nc.scalar.activation(sq[:], X[:, b, :], ACT.Square).then_inc(sq_r, 1)

                def step(s):
                    if s.live(0):
                        g = s.at(0)
                        need(act, v_d, g * G)
                        for d in range(C):
                            act.wait_ge(t_d, g * C + d + 1)
                            nc.scalar.activation(xT_h[:, d, :], work[d][:], ACT.Copy, scale=S_LN).then_inc(h_h, 1)
                    if s.live(2):
                        g = s.at(2)
                        for j in range(G):
                            b = g * G + j
                            settle(act, nm_r, b + 1, k.idle["act"])
                            nc.scalar.activation(X[:, b, :], X[:, b, :], ACT.Identity, scale=rs[:, 0, j:j + 1],
                                                 bias=rs[:, 1, j:j + 1]).then_inc(ln_r, 1)
                        square(g, 0)
                    if s.live(1):
                        g = s.at(1)
                        act.wait_ge(u_r, g + 1)
                        nc.scalar.activation(es[:], es[:], ACT.Exp, scale=k.s(K_G)).then_inc(e_r, 1)
                    if s.live(0):
                        g = s.at(0)
                        need(act, gl_d, g)
                        for e in range(C):
                            act.wait_ge(zl_d, g * C + e + 1)
                            nc.scalar.activation(zl_hi[:, e, :], work[e][:], ACT.Copy, scale=S_EVAC).then_inc(zl_h, 1)
                    if s.live(2):
                        square(s.at(2), 1)
                    if s.live(1):
                        g = s.at(1)
                        act.wait_ge(kt_d, g + 1)
                        need(act, o_d, g * G)
                        nc.scalar.activation(kT_hi[:], pkt[:], ACT.Copy, scale=S_K).then_inc(kt_h, 1)
                    if s.live(0):
                        g = s.at(0)
                        need(act, gg_d, g)
                        for e in range(C):
                            act.wait_ge(zg_d, g * C + e + 1)
                            nc.scalar.activation(zg_hi[:, e, :], work[e][:], ACT.Copy, scale=S_EVAC).then_inc(zg_h, 1)
                    if s.live(2):
                        square(s.at(2), 2)
                    if s.live(0):
                        g = s.at(0)
                        act.wait_ge(gl_d, g + 1)
                        need(act, kt_d, g)
                        nc.scalar.activation(gs[:], pgl[:], ACT.Relu).then_inc(relu_r, 1)
                        need(act, o_d, g * G)
                        for j in range(G):
                            act.wait_ge(v_d, g * G + j + 1)
                            nc.scalar.activation(v_hi[:, j, :], work[j][:], ACT.Copy, scale=S_EVAC).then_inc(v_h, 1)
                    if s.live(2):
                        square(s.at(2), 3)
                pipeline(act, NG, 2, 1, step)

            @block.vector
            def _(dve):
                nc.vector.tensor_scalar(mask[:], k.ident[:], -1.0, 1.0, ALU.mult, ALU.add).then_inc(msk_r, 1)
                dve.wait_ge(msk_r, 1)
                nc.vector.tensor_tensor(mask[:], mask[:], k.adj[:], ALU.mult).then_inc(msk_r, 1)

                def lo(dst, src, hi, scale, hi_sem, n, done):
                    dve.wait_ge(hi_sem, n)
                    nc.vector.scalar_tensor_tensor(dst, src, scale, hi, ALU.mult, ALU.subtract).then_inc(done, 1)

                def counted(sem, per, g):
                    n = [0]

                    def run(ins, wait=True):
                        n[0] += 1
                        assert n[0] <= per
                        ins.then_inc(sem, 1)
                        if wait:
                            settle(dve, sem, g * per + n[0], idle)
                    return run

                def step(s):
                    if s.live(0):
                        g = s.at(0)
                        for d in range(C):
                            lo(xT_l[:, d, :], work[d][:], xT_h[:, d, :], S_LN, h_h, g * C + d + 1, h_l)
                    if s.live(1):
                        g = s.at(1)
                        dve.wait_ge(bc_d, g + 1)
                        for j in range(G):
                            js = slice(j * P, (j + 1) * P)
                            ins = nc.vector.tensor_scalar(es[:, js], pgg[:, js], hs[:, j:j + 1], 0.0, ALU.add, ALU.min)
                        ins.then_inc(u_r, 1)
                        dve.wait_ge(mask_r, g + 1)
                        nc.vector.tensor_tensor(gs[:], gs[:], pbc[:], ALU.mult).then_inc(bc_u, 1)
                        settle(dve, bc_u, g + 1, idle)
                        run = counted(ksm, 14, g)
                        run(nc.vector.tensor_reduce(sm[:, 0, :], grouped(gs[:], G), axis=AX_X, op=ALU.add))
                        run(nc.vector.tensor_tensor(sm[:, 0, :], sm[:, 0, :], rn[:], ALU.mult))
                        run(nc.vector.tensor_scalar(sm[:, 0, :], sm[:, 0, :], 1e-8, None, ALU.max))
                        run(nc.vector.reciprocal(sm[:, 1, :], sm[:, 0, :]))
                        run(nc.vector.tensor_tensor(sm[:, 1, :], sm[:, 1, :], rn[:], ALU.mult))
                        run(nc.vector.tensor_scalar(sm[:, 1, :], sm[:, 1, :], k.s(GATE), None, ALU.mult))
                    if s.live(0):
                        for e in range(2):
                            lo(zl_lo[:, e, :], work[e][:], zl_hi[:, e, :], S_EVAC, zl_h, s.at(0) * C + e + 1, zl_l)
                    if s.live(1):
                        dve.wait_ge(em_r, g + 1)
                        run(nc.vector.tensor_reduce(sm[:, 2, :], grouped(es[:], G), axis=AX_X, op=ALU.add))
                        run(nc.vector.tensor_scalar(sm[:, 2, :], sm[:, 2, :], 1e-8, None, ALU.max))
                        run(nc.vector.reciprocal(sm[:, 3, :], sm[:, 2, :]))
                        run(nc.vector.tensor_scalar(sm[:, 3, :], sm[:, 3, :], k.s(UNGATE), None, ALU.mult))
                        for j in range(G):
                            js = slice(j * P, (j + 1) * P)
                            run(nc.vector.tensor_scalar(gs[:, js], gs[:, js], sm[:, 1, j:j + 1], None, ALU.mult),
                                wait=(j == G - 1))
                        for j in range(G):
                            js = slice(j * P, (j + 1) * P)
                            ins = nc.vector.scalar_tensor_tensor(gs[:, js], es[:, js], sm[:, 3, j:j + 1], gs[:, js],
                                                                 ALU.mult, ALU.add)
                        ins.then_inc(k_r, 1)
                    if s.live(0):
                        for e in range(2, C):
                            lo(zl_lo[:, e, :], work[e][:], zl_hi[:, e, :], S_EVAC, zl_h, s.at(0) * C + e + 1, zl_l)
                    if s.live(1):
                        lo(kT_lo[:], pkt[:], kT_hi[:], S_K, kt_h, s.at(1) + 1, kt_l)
                    if s.live(0):
                        for e in range(C):
                            lo(zg_lo[:, e, :], work[e][:], zg_hi[:, e, :], S_EVAC, zg_h, s.at(0) * C + e + 1, zg_l)
                    if s.live(1):
                        for j in range(G):
                            b = s.at(1) * G + j
                            dve.wait_ge(o_d, b + 1)
                            nc.vector.scalar_tensor_tensor(X[:, b, :], work[j][:], k.s(F_OUT2), X[:, b, :], ALU.mult,
                                                           ALU.add).then_inc(o_u, 1)
                    if s.live(0):
                        g = s.at(0)
                        dve.wait_ge(relu_r, g + 1)
                        run2 = counted(diag_r, 6, g)
                        run2(nc.vector.tensor_tensor(grouped(dl[:]), grouped(pgl[:]), over(k.ident[:], G), ALU.mult))
                        run2(nc.vector.tensor_reduce(dia[:, 0, :], grouped(dl[:]), axis=AX_X, op=ALU.add))
                        dve.wait_ge(gg_d, g + 1)
                        run2(nc.vector.tensor_tensor(grouped(dg[:]), grouped(pgg[:]), over(k.ident[:], G), ALU.mult))
                        run2(nc.vector.tensor_reduce(dia[:, 1, :], grouped(dg[:]), axis=AX_X, op=ALU.add))
                        run2(nc.vector.tensor_scalar(hs[:], dia[:, 1, :], -0.5, None, ALU.mult))
                        nc.vector.tensor_tensor(grouped(dg[:]), over(k.ident[:], G), spread(hs[:], P),
                                                ALU.mult).then_inc(dd_r, 1)
                        run2(nc.vector.tensor_scalar(rn[:], dia[:, 0, :], k.s(EPS_L), None, ALU.max))
                    if s.live(1):
                        for j in range(G):
                            b = s.at(1) * G + j
                            settle(dve, o_u, b + 1, idle)
                            nc.vector.bn_stats(bn[:, j, :], X[:, b, :]).then_inc(bn_r, 1)
                            settle(dve, bn_r, b + 1, idle)
                            if j == 0:
                                settle(dve, nm_r, s.at(1) * G, idle)
                            nc.vector.bn_aggr(mv[:, j, :], bn[:, j, :]).then_inc(mv_r, 1)
                    if s.live(0):
                        g = s.at(0)
                        dve.wait_ge(diag_pow, g + 1)
                        nc.vector.tensor_tensor(grouped(dl[:]), over(k.ident[:], G), spread(rn[:], P),
                                                ALU.mult).then_inc(dd_r, 1)
                        for j in range(G):
                            lo(v_lo[:, j, :], work[j][:], v_hi[:, j, :], S_EVAC, v_h, g * G + j + 1, v_l)
                    if s.live(2):
                        g = s.at(2)
                        dve.wait_ge(ns_d, (g + 1) * G)
                        nc.vector.tensor_copy(k.nsq[:, :, bass.ds(g * G, G)].rearrange("p c b -> p b c"),
                                              pbc[:, 0:G * C].rearrange("p (b c) -> p b c", b=G)).then_inc(ns_u, 1)
                pipeline(dve, NG, 2, 1, step)

            @block.gpsimd
            def _(pool):
                pool.wait_ge(msk_r, 2)
                half = k.s(HALF)

                def step(s):
                    if s.live(1):
                        pool.wait_ge(e_r, s.at(1) + 1)
                        pool.tensor_tensor(grouped(es[:], G), grouped(es[:], G), over(mask[:], G), ALU.mult).then_inc(em_r, 1)
                    if s.live(0):
                        g = s.at(0)
                        pool.wait_ge(relu_r, g + 1)
                        pool.tensor_tensor(grouped(gs[:], G), grouped(gs[:], G), over(mask[:], G), ALU.mult).then_inc(mask_r, 1)
                        pool.wait_ge(diag_r, (g + 1) * 6)
                        pool.tensor_tensor(rn[:], rn[:], half.broadcast_to([P, G]), ALU.pow).then_inc(diag_pow, 1)
                    if s.live(1):
                        g = s.at(1)
                        pool.wait_ge(mv_r, (g + 1) * G)
                        need(pool, ln_r, g * G)
                        settle(pool, mv_r, (g + 1) * G, k.idle["pool"])
                        pool.tensor_scalar(rs[:, 1, :], mv[:, :, 1], LN_EPS, None, ALU.add).then_inc(rs_r, 1)
                        settle(pool, rs_r, 3 * g + 1, k.idle["pool"])
                        pool.tensor_tensor(rs[:, 0, :], rs[:, 1, :], half.broadcast_to([P, G]), ALU.pow).then_inc(rs_r, 1)
                        settle(pool, rs_r, 3 * g + 2, k.idle["pool"])
                        pool.tensor_tensor(rs[:, 1, :], mv[:, :, 0], rs[:, 0, :], ALU.mult).then_inc(rs_r, 1)
                        settle(pool, rs_r, 3 * g + 3, k.idle["pool"])
                        pool.tensor_scalar(rs[:, 1, :], rs[:, 1, :], -1.0, None, ALU.mult).then_inc(nm_r, G)
                pipeline(pool, NG, 2, 1, step)


def build(nc, x, adj, b0, b1, wl, wg, wv, wo, gate, logsig, b3, out):
    with ExitStack() as ctx:
        k = Chip(nc, ctx)
        with ExitStack() as weights:
            w = {f"{n}_{h}": k.sb(weights, f"{n}_{h}", [P, C, N], F16) for n in ("wl", "wg", "m") for h in "hl"}
            x_in = prepare(k, w, x, adj, b0, b1, b3, wl, wg, wv, wo, gate, logsig)
            first_norms(k, x_in)
            k.release_semaphores()
            adaptive_layer(k, k.bias0, b1, None)
            k.release_semaphores()
            kernel_mix(k, w)
            k.release_semaphores()
        adaptive_layer(k, k.bias3, None, out)


_INS = ['x', 'adj', 'L0_gnn_bias', 'L1_gnn_bias', 'L2_gnn_W_lang', 'L2_gnn_W_grav', 'L2_gnn_W_V', 'L2_gnn_W_O',
        'L2_gnn_gate_logit', 'L2_gnn_log_sigma', 'L3_gnn_bias']


def kernel(**inputs):
    import numpy as _np
    import concourse.bacc as _bacc
    from concourse import mybir as _mybir
    from concourse.bass_utils import run_bass_kernel_spmd as _run

    nc = _bacc.Bacc("TRN2", target_bir_lowering=False, num_devices=1)
    arrays, args = {}, []
    for name in _INS:
        a = _np.ascontiguousarray(inputs[name])
        if a.ndim == 0:
            a = a.reshape(1)
        arrays[f"in_{name}_dram"] = a
        args.append(nc.dram_tensor(f"in_{name}_dram", a.shape, _mybir.dt.from_np(a.dtype), kind="ExternalInput").ap())
    args.append(nc.dram_tensor("out_0_dram", (B, P, N), F32, kind="ExternalOutput").ap())
    build(nc, *args)
    r = _run(nc, [arrays], core_ids=[0])
    return r.results[0]["out_0_dram"]
```

```python
import concourse.bass as bass
from concourse import mybir
from contextlib import ExitStack, contextmanager

F32 = mybir.dt.float32
F16 = mybir.dt.float16
ALU = mybir.AluOpType
ACT = mybir.ActivationFunctionType
AX_X = mybir.AxisListType.X
ABSMAX = bass.bass_isa.ReduceOp.absmax
RMAX = bass.bass_isa.ReduceOp.max

B, P, N = 64, 128, 512
C = N // P
G = 4
NG = B // G
TOPK = int(N * 0.3)
ROUNDS = TOPK // 8
assert TOPK == 8 * ROUNDS + 1
SEARCH = 8
LN_EPS = 1e-5
SENT = -3.0e38

S_RN = 2.0 ** 14
S_COL = 2.0 ** 15
S_W = 2.0 ** 13
S_AN = 2.0 ** 14
S_SQ = 2.0 ** 6
S_F = 2.0 ** 15
S_LN = 2.0 ** 10
S_K = 2.0 ** 14
S_EVAC = 2.0 ** -17

(M_ADJ, M_WL, M_WG, M_M, W_ADJ, W_WL, W_WG, W_M, W_SQ, EPS_L, K_G, GATE, UNGATE, F_OUT2, F_L1, SIG,
 NSQ_MAX, SX, SAN, F_B, TMP_A, TMP_B, HALF, TMP_C, PLUS_HALF) = range(25)
NSCAL = 25


def need(eng, sem, value):
    if isinstance(value, int) and value <= 0:
        return
    eng.wait_ge(sem, value)


@contextmanager
def strided(eng, start, end, step):
    with eng.Fori(start // step, end // step) as u:
        yield u * step


def settle(eng, sem, value, idle):
    if isinstance(value, int):
        return need(eng, sem, value)
    eng.wait_ge(sem, value)
    eng.sem_inc(idle, 1)


class Step:

    def __init__(self, i, rem, total):
        self.i, self.rem, self.total = i, rem, total

    def live(self, lag):
        return not isinstance(self.i, int) or 0 <= self.i - lag < self.total

    def at(self, lag):
        return self.i - lag

    def slot(self, lag, ring=2):
        return (self.rem - lag) % ring


def pipeline(eng, total, depth, ring, step):
    head = -(-(depth + ring) // ring) * ring
    for i in range(head):
        step(Step(i, i % ring, total))
    with strided(eng, head, total, ring) as base:
        for j in range(ring):
            step(Step(base + j, j % ring, total))
    for i in range(total, total + depth):
        step(Step(i, i % ring, total))


def over(t, reps):
    return t.rearrange("p (o n) -> p o n", o=1).broadcast_to([t.shape[0], reps, t.shape[1]])


def spread(t, width):
    return t.rearrange("p (n o) -> p n o", o=1).broadcast_to([t.shape[0], t.shape[1], width])


def grouped(t, parts=C):
    return t.rearrange("p (a b) -> p a b", a=parts)


class Chip:

    def __init__(self, nc, ctx):
        self.nc, self.ctx = nc, ctx
        self.n = 0
        self.taken = []
        self.X = self.sb(ctx, "x_all", [P, B, N])
        self.ident = self.sb(ctx, "ident", [P, P])
        self.ones = self.sb(ctx, "ones", [P, P])
        self.adj = self.sb(ctx, "adj", [P, P])
        self.sc = self.sb(ctx, "scalars", [P, NSCAL])
        self.bias0 = self.sb(ctx, "bias0", [P, 1])
        self.bias3 = self.sb(ctx, "bias3", [P, 1])
        self.idle = {e: nc.alloc_semaphore(name=f"idle_{e}") for e in ("sp", "dve", "pool", "act")}
        self.nsq_rows = nc.dram_tensor("nsq_rows", (B, N), F32, kind="Internal").ap()
        self.rn_rows = nc.dram_tensor("rn_rows", (B, N), F32, kind="Internal").ap()

    def sb(self, ctx, name, shape, dt=F32):
        self.n += 1
        return ctx.enter_context(self.nc.sbuf_tensor(f"{name}_{self.n}", shape, dt))

    def ps(self, ctx, name, shape=(P, N), dt=F32):
        self.n += 1
        return ctx.enter_context(self.nc.psum_tensor(f"{name}_{self.n}", list(shape), dt))

    def sem(self, name):
        self.n += 1
        self.taken.append(self.nc.alloc_semaphore(name=f"{name}_{self.n}"))
        return self.taken[-1]

    def release_semaphores(self):
        self.nc.clear_and_free_semaphores(self.taken)
        self.taken = []
        self.nc.all_engine_barrier()

    def s(self, k):
        return self.sc[:, k:k + 1]


class Chain:

    def __init__(self, eng, sem):
        self.eng, self.sem, self.n = eng, sem, 0

    def __call__(self, ins):
        self.n += 1
        ins.then_inc(self.sem, 1)
        self.eng.wait_ge(self.sem, self.n)


def upper(d):
    return slice(d * P, N)


def load_x(k, x, adj, b0, b3, gate, logsig):
    nc = k.nc
    PARTS, RS = 8, 4
    x_in = [k.sem(f"x_in{q}") for q in range(PARTS)]
    small_in, consts, zeroed = k.sem("small_in"), k.sem("consts_set"), k.sem("ident_zeroed")
    mx, mxall, chain = k.sem("adj_max"), k.sem("adj_max_all"), k.sem("dve_chain")
    sq_ready, sums, row_ready = k.sem("sq_ready"), k.sem("sums"), k.sem("row_ready")
    rows_out = k.sem("rows_out")
    per = B // PARTS
    with ExitStack() as ctx:
        sq = k.sb(ctx, "sq", [P, RS, N])
        row = k.sb(ctx, "row", [P, NG, N])
        ps = [k.ps(ctx, f"sum{i}") for i in range(2)]
        with nc.Block() as block:
            @block.sync
            def _(sp):
                column = lambda t: t.rearrange("(p o) -> p o", o=1)
                single = lambda t: t.rearrange("(a b) -> a b", a=1).broadcast_to([P, 1])
                for q in range(2 * PARTS):
                    sp.dma_start(k.X[:, per // 2 * q:per // 2 * (q + 1), :],
                                 x[per // 2 * q:per // 2 * (q + 1)].rearrange("b l n -> l b n")).then_inc(x_in[q // 2], 16)
                    if q == 0:
                        sp.dma_start(k.adj[:], adj).then_inc(small_in, 16)
                        sp.dma_start(k.bias0[:], column(b0)).then_inc(small_in, 16)
                        sp.dma_start(k.bias3[:], column(b3)).then_inc(small_in, 16)
                        sp.dma_start(k.s(GATE), single(gate)).then_inc(small_in, 16)
                        sp.dma_start(k.s(SIG), single(logsig)).then_inc(small_in, 16)
                for n in range(2):
                    half = slice(n * NG // 2, (n + 1) * NG // 2)
                    sp.wait_ge(row_ready, (n + 1) * NG // 2)
                    sp.dma_start(k.nsq_rows.rearrange("(g j) n -> j g n", j=G)[:, half],
                                 row[0:P:P // G, half, :]).then_inc(rows_out, 16)
                sp.wait_ge(rows_out, 32)

            @block.gpsimd
            def _(pool):
                pool.memset(k.ones[:], 1.0).then_inc(consts, 1)
                pool.memset(k.ident[:], 0.0).then_inc(zeroed, 1)
                pool.memset(k.s(HALF), -0.5).then_inc(consts, 1)
                pool.memset(k.s(PLUS_HALF), 0.5).then_inc(consts, 1)
                pool.wait_ge(zeroed, 1)
                pool.affine_select(out=k.ident[:], in_=k.ident[:], compare_op=ALU.not_equal, fill=1.0, base=0,
                                   pattern=[[-1, P]], channel_multiplier=1).then_inc(consts, 1)
                pool.wait_ge(mx, 1)
                pool.partition_all_reduce(k.s(M_ADJ), k.s(M_ADJ), P, ABSMAX).then_inc(mxall, 1)

            @block.scalar
            def _(act):
                act.wait_ge(small_in, 80)
                nc.scalar.activation(k.s(SIG), k.s(SIG), ACT.Exp, scale=-2.0)
                nc.scalar.activation(k.s(GATE), k.s(GATE), ACT.Exp, scale=-1.0)
                for q in range(PARTS):
                    act.wait_ge(x_in[q], 32)
                    for i in range(per):
                        b = q * per + i
                        need(act, sums, b - RS + 1)
                        nc.scalar.activation(sq[:, b % RS, :], k.X[:, b, :], ACT.Square).then_inc(sq_ready, 1)

            @block.tensor
            def _(pe):
                pe.wait_ge(consts, 4)

                def group(g, slot):
                    need(pe, row_ready, g - 1)
                    for j in range(G):
                        pe.wait_ge(sq_ready, g * G + j + 1)
                        nc.tensor.matmul(ps[slot][j * P // G:(j + 1) * P // G, :], k.ones[:, 0:P // G], sq[:, j, :],
                                         start=True, stop=True).then_inc(sums, 1)
                group(0, 0)
                group(1, 1)
                with strided(pe, 2, NG, 2) as g:
                    group(g, 0)
                    group(g + 1, 1)

            @block.vector
            def _(dve):
                ch = Chain(dve, chain)
                dve.wait_ge(small_in, 80)
                nc.vector.tensor_reduce(k.s(M_ADJ), k.adj[:], axis=AX_X, op=ALU.max,
                                        apply_absolute_value=True).then_inc(mx, 1)
                dve.wait_ge(mxall, 1)
                ch(nc.vector.tensor_scalar(k.s(M_ADJ), k.s(M_ADJ), 1e-18, 1.0 / S_W, ALU.max, ALU.mult))
                ch(nc.vector.reciprocal(k.s(W_ADJ), k.s(M_ADJ)))

                with strided(dve, 0, NG, 2) as g:
                    for j in range(2):
                        dve.wait_ge(sums, (g + j + 1) * G)
                        nc.vector.tensor_copy(row[:, g + j, :], ps[j][:]).then_inc(row_ready, 1)


class MixWeights:

    def __init__(self, k, ctx, w, wl, wg, wv, wo):
        self.k, self.w = k, w
        self.a, self.b = (k.sb(ctx, n, [P, C, N]) for n in ("weights_a", "weights_b"))
        self.sources = {"wl": wl, "wg": wg, "wv": wv, "wo": wo}
        self.win = {n: k.sem(f"{n}_in") for n in self.sources}
        self.part = k.sb(ctx, "part_sq", [P, 3, C])
        self.fro = k.sb(ctx, "fro", [P, 3])
        self.half = k.sb(ctx, "half_scale", [P, 3])
        (self.prod, self.sq, self.sum, self.fro_in, self.pool_ch, self.scale_r, self.tmp_r, self.hi_r, self.lo_r,
         self.woT_d, self.woT_c) = (k.sem(n) for n in (
             "product_done", "squares", "square_sum", "fro_copied", "scale_chain", "scale_ready", "scaled", "w_hi",
             "w_lo", "woT_done", "woT_copied"))
        self.mats = [("wl", self.a, W_WL, M_WL), ("wg", self.b, W_WG, M_WG), ("m", self.b, W_M, M_M)]

    def load(self, sp, name, buf):
        sp.dma_start(buf[:], self.sources[name].rearrange("(c p) n -> p c n", p=P)).then_inc(self.win[name], 16)

    def early_loads(self, sp):
        self.load(sp, "wl", self.a)
        self.load(sp, "wg", self.b)

    def late_loads(self, sp):
        sp.wait_ge(self.lo_r, C)
        self.load(sp, "wo", self.a)
        sp.wait_ge(self.lo_r, 2 * C)
        self.load(sp, "wv", self.b)
        for name in ("wo", "wv"):
            sp.wait_ge(self.win[name], 16)

    @staticmethod
    def cols(name, d):
        return slice(0, N) if name == "m" else upper(d)

    def on_tensor(self, pe, bank, sum_bank):
        nc, k, a, b = self.k.nc, self.k, self.a, self.b

        def product(n, left, right):
            for d in range(C):
                cs = self.cols(self.mats[n][0], d)
                for e in range(C):
                    last = nc.tensor.matmul(bank[d][:, cs], left[:, e, d * P:(d + 1) * P], right[:, e, cs],
                                            start=(e == 0), stop=(e == C - 1))
                last.then_inc(self.prod, 1)
            pe.wait_ge(self.sq, (n + 1) * C)
            for d in range(C):
                last = nc.tensor.matmul(sum_bank[:, n:n + 1], k.ones[:], self.part[:, n, d:d + 1], start=(d == 0),
                                        stop=(d == C - 1))
            last.then_inc(self.sum, 1)
        pe.wait_ge(self.win["wl"], 16)
        product(0, a, a)
        pe.wait_ge(self.win["wg"], 16)
        pe.wait_ge(self.tmp_r, C)
        product(1, b, b)
        pe.wait_ge(self.win["wo"], 16)
        pe.wait_ge(self.tmp_r, 2 * C)
        for c in range(C):
            for r in range(C):
                last = nc.tensor.transpose(bank[c][:, r * P:(r + 1) * P], a[:, r, c * P:(c + 1) * P], k.ident[:])
            last.then_inc(self.woT_d, 1)
        pe.wait_ge(self.win["wv"], 16)
        pe.wait_ge(self.woT_c, C)
        product(2, b, a)

    def on_scalar(self, act, bank, sum_bank):
        nc, k = self.k.nc, self.k
        for n, (name, buf, scale, _) in enumerate(self.mats):
            if name == "m":
                act.wait_ge(self.woT_d, C)
                for c in range(C):
                    nc.scalar.activation(self.a[:, c, :], bank[c][:], ACT.Copy).then_inc(self.woT_c, 1)
            act.wait_ge(self.prod, (n + 1) * C)
            for d in range(C):
                cs = self.cols(name, d)
                nc.scalar.activation(buf[:, d, cs], bank[d][:, cs], ACT.Square,
                                     accum_out=self.part[:, n, d:d + 1]).then_inc(self.sq, 1)
            act.wait_ge(self.sum, n + 1)
            nc.scalar.activation(self.fro[:, n:n + 1], sum_bank[:, n:n + 1], ACT.Copy,
                                 scale=1.0 / (S_F * S_F)).then_inc(self.fro_in, 1)
            act.wait_ge(self.scale_r, n + 1)
            for d in range(C):
                cs, rest = self.cols(name, d), self.cols(name, d)
                if name != "m":
                    ds_, rest = slice(d * P, (d + 1) * P), slice((d + 1) * P, N)
                    last = nc.scalar.activation(buf[:, d, ds_], bank[d][:, ds_], ACT.Copy, scale=self.half[:, n:n + 1])
                if name == "m" or d < C - 1:
                    last = nc.scalar.activation(buf[:, d, rest], bank[d][:, rest], ACT.Copy, scale=k.s(scale))
                last.then_inc(self.tmp_r, 1)
            for d in range(C):
                cs = self.cols(name, d)
                act.wait_ge(self.tmp_r, n * C + d + 1)
                nc.scalar.activation(self.w[f"{name}_h"][:, d, cs], buf[:, d, cs], ACT.Copy).then_inc(self.hi_r, 1)

    def on_gpsimd(self, pool):
        k = self.k
        for n, (name, buf, scale, inverse) in enumerate(self.mats):
            q = self.fro[:, n:n + 1]
            pool.wait_ge(self.fro_in, n + 1)
            pool.tensor_scalar(q, q, 1e-36, None, ALU.max).then_inc(self.pool_ch, 1)
            pool.wait_ge(self.pool_ch, 4 * n + 1)
            pool.tensor_tensor(k.s(scale), q, k.s(HALF), ALU.pow).then_inc(self.pool_ch, 1)
            pool.tensor_tensor(k.s(inverse), q, k.s(PLUS_HALF), ALU.pow).then_inc(self.pool_ch, 1)
            pool.wait_ge(self.pool_ch, 4 * n + 3)
            pool.tensor_scalar(self.half[:, n:n + 1], k.s(scale), 0.5, None, ALU.mult).then_inc(self.pool_ch, 1)
            pool.wait_ge(self.pool_ch, 4 * n + 4)
            pool.sem_inc(self.scale_r, 1)
            for d in range(C):
                cs = MixWeights.cols(name, d)
                pool.wait_ge(self.hi_r, n * C + d + 1)
                pool.tensor_tensor(self.w[f"{name}_l"][:, d, cs], buf[:, d, cs], self.w[f"{name}_h"][:, d, cs],
                                   ALU.subtract).then_inc(self.lo_r, 1)


def similarity(k, ctx_out, rows_bank, weights):
    nc = k.nc
    pair = [k.ps(ctx_out, f"pair{i}") for i in range(C)]
    diag = k.ps(ctx_out, "diag")
    R = 4
    chain, root_ready, rows_ready, rows_out, gmax, gmax_all, nsq_in = (k.sem("rn_chain"), k.sem("root_ready"),
        k.sem("rn_rows_ready"), k.sem("rn_rows_out"), k.sem("gmax"), k.sem("gmax_all"), k.sem("nsq_in"))
    rn_in = [k.sem(f"rn_in{r}") for r in range(R)]
    unit_ready, hi_ready, lo_ready, gram_done = k.sem("unit_ready"), k.sem("hi_ready"), k.sem("lo_ready"), k.sem("gram_done")
    with ExitStack() as ctx:
        shape = [B, N] if rows_bank is not None else [P, B * N // P]
        rn, d, root = (k.sb(ctx, n, shape) for n in ("rn", "clamped_sq", "root"))
        rnb = k.sb(ctx, "rn_bcast", [P, R, N])
        unit = k.sb(ctx, "unit", [P, R, N])
        hi = k.sb(ctx, "unit_hi", [P, R, N], F16)
        lo = k.sb(ctx, "unit_lo", [P, R, N], F16)
        as_tile = lambda rows: rows.rearrange("b (h n) -> (b h) n", n=shape[1])
        with nc.Block() as block:
            @block.sync
            def _(sp):
                if rows_bank is None:
                    sp.dma_start(d[:], as_tile(k.nsq_rows)).then_inc(nsq_in, 16)
                if weights:
                    weights.early_loads(sp)
                sp.wait_ge(rows_ready, 1)
                sp.dma_start(as_tile(k.rn_rows), rn[:]).then_inc(rows_out, 16)
                sp.wait_ge(rows_out, 16)

                def load(b, r):
                    if not isinstance(b, int) or b >= R:
                        settle(sp, unit_ready, b - R + 1, k.idle["sp"])
                    row = b if rows_bank is None else B - 1 - b
                    sp.dma_start(rnb[:, r, :], k.rn_rows[row].partition_broadcast(P)).then_inc(rn_in[r], 16)
                for r in range(R):
                    load(r, r)
                with strided(sp, R, B, R) as base:
                    for r in range(R):
                        load(base + r, r)

            @block.gpsimd
            def _(pool):
                pool.memset(k.s(NSQ_MAX), 0.0).then_inc(gmax, 1)
                pool.wait_ge(gmax, 2)
                pool.partition_all_reduce(k.s(NSQ_MAX), k.s(NSQ_MAX), P, RMAX).then_inc(gmax_all, 1)

            @block.tensor
            def _(pe):
                def gram(b, r, first, final):
                    pe.wait_ge(lo_ready, b + 1)
                    pe.wait_ge(hi_ready, b + 1)
                    for i in range(C):
                        stat = hi[:, r, i * P:(i + 1) * P]
                        nc.tensor.matmul(pair[i][:], stat, lo[:, r, :], start=first, stop=False, skip_group_check=True)
                        if i < C - 1:
                            nc.tensor.matmul(pair[i][:, (i + 1) * P:], stat, hi[:, r, (i + 1) * P:], start=False,
                                             stop=final, skip_group_check=True)
                        last = nc.tensor.matmul(diag[:, i * P:(i + 1) * P], stat, stat, start=(first and i == 0),
                                                stop=final, skip_group_check=True)
                    last.then_inc(gram_done, 1)
                for r in range(R):
                    gram(r, r, r == 0, False)
                with strided(pe, R, B - R, R) as base:
                    for r in range(R):
                        gram(base + r, r, False, False)
                for r in range(R):
                    gram(B - R + r, r, False, r == R - 1)

            @block.vector
            def _(dve):
                ch = Chain(dve, chain)
                if rows_bank is None:
                    dve.wait_ge(nsq_in, 16)
                    ch(nc.vector.tensor_scalar(d[:], d[:], 1e-24, None, ALU.max))
                else:
                    ch(nc.vector.tensor_scalar(d[:], rows_bank[0:B, :], 1.0 / S_SQ, 1e-24, ALU.mult, ALU.max))
                dve.wait_ge(gmax, 1)
                nc.vector.tensor_reduce(k.sc[0:shape[0], NSQ_MAX:NSQ_MAX + 1], d[:], axis=AX_X,
                                        op=ALU.max).then_inc(gmax, 1)
                dve.wait_ge(root_ready, 1)
                ch(nc.vector.reciprocal(rn[:], root[:]))
                ch(nc.vector.tensor_tensor(root[:], rn[:], rn[:], ALU.mult))
                ch(nc.vector.scalar_tensor_tensor(root[:], d[:], -0.5 * S_RN, root[:], ALU.mult, ALU.mult))
                nc.vector.scalar_tensor_tensor(rn[:], root[:], 1.5 * S_RN, rn[:], ALU.add, ALU.mult).then_inc(rows_ready, 1)

                def units(base, start):
                    for r in range(R):
                        b = base + r
                        dve.wait_ge(rn_in[r], (b // R + 1) * 16 if isinstance(b, int) else (base // R + 1) * 16)
                        if not start:
                            dve.wait_ge(hi_ready, b - R + 1)
                            dve.wait_ge(lo_ready, b - R + 1)
                        nc.vector.tensor_tensor(unit[:, r, :], k.X[:, b, :], rnb[:, r, :], ALU.mult).then_inc(unit_ready, 1)
                    for r in range(R):
                        b = base + r
                        dve.wait_ge(hi_ready, b + 1)
                        if not start:
                            dve.wait_ge(gram_done, b - R + 1)
                        nc.vector.tensor_tensor(lo[:, r, :], unit[:, r, :], hi[:, r, :], ALU.subtract).then_inc(lo_ready, 1)
                units(0, True)
                with strided(dve, R, B, R) as base:
                    units(base, False)

            @block.scalar
            def _(act):
                act.wait_ge(chain, 1)
                nc.scalar.activation(root[:], d[:], ACT.Sqrt).then_inc(root_ready, 1)

                def split(b, r, start):
                    act.wait_ge(unit_ready, b + 1)
                    if not start:
                        act.wait_ge(gram_done, b - R + 1)
                    nc.scalar.activation(hi[:, r, :], unit[:, r, :], ACT.Copy).then_inc(hi_ready, 1)
                for r in range(R):
                    split(r, r, True)
                with strided(act, R, B, R) as base:
                    for r in range(R):
                        split(base + r, r, False)
    return pair, diag


def neighbours(k, pair, diag, an_h, an_l, wa_h, wa_l, weights):
    nc = k.nc
    copied, tr, simsum, dsum, masked, rounds = (k.sem("copied"), k.sem("tr"), k.sem("sim_sum"), k.sem("diag_added"),
        k.sem("masked"), k.sem("rounds"))
    dd_ready = k.sem("dinv_diag_ready")
    a_ready, deg, deg_c, pw, an_max, an_all, ch_s, ach = (k.sem("a_ready"), k.sem("deg"), k.sem("deg_clamped"), k.sem("deg_pow"),
        k.sem("an_max"), k.sem("an_all"), k.sem("chain"), k.sem("an_hi"))
    SIM = 1.0 / (S_RN * S_RN * B)
    st, sd_r, search, cnt_b, bad_in, bad_all, pick = (k.sem("stats"), k.sem("deviation"), k.sem("search"), k.sem("counts_b"),
        k.sem("worst_row"), k.sem("worst_of_all"), k.sem("pick"))
    STEPS = 9
    HALF_C = C // 2
    with ExitStack() as ctx:
        raw = k.sb(ctx, "raw", [P, C, N])
        sim = k.sb(ctx, "sim", [P, C, N])
        work = k.sb(ctx, "work", [P, C, N])
        m8, sel = (k.sb(ctx, n, [P, C, 8]) for n in ("m8", "sel"))
        ranks = k.sb(ctx, "ranks", [P, 8])
        bns = k.sb(ctx, "bns", [P, C, 6])
        mvs = k.sb(ctx, "mvs", [P, C, 2])
        thr, delta, cnt, left = (k.sb(ctx, n, [P, C]) for n in ("threshold", "delta", "count", "left"))
        move = k.sb(ctx, "move", [P, 2, C])
        worst = k.sb(ctx, "worst", [P, 1])
        flag = k.sb(ctx, "flag", [P, 1], mybir.dt.int32)
        degc = k.sb(ctx, "degc", [P, 2, C])
        degr = k.sb(ctx, "degr", [P, N])
        mxp = k.sb(ctx, "mxp", [P, 1])
        tp = [k.ps(ctx, f"tp{i}") for i in range(2)]
        dr = tp[0]
        dc = tp[1]
        with nc.Block() as block:
            @block.sync
            def _(sp):
                if weights:
                    weights.late_loads(sp)

            @block.scalar
            def _(act):
                for i in range(C):
                    nc.scalar.activation(raw[:, i, :], pair[i][:], ACT.Copy, scale=SIM).then_inc(copied, 1)

                def count_b(it):
                    act.wait_ge(search, it * STEPS + 1)
                    for i in range(HALF_C, C):
                        nc.scalar.activation(raw[:, i, :], work[:, i, :], ACT.Sign, scale=-1.0, bias=thr[:, i:i + 1],
                                             accum_out=cnt[:, i:i + 1]).then_inc(cnt_b, 1)
                with act.Fori(0, SEARCH) as it:
                    count_b(it)
                if weights:
                    weights.on_scalar(act, pair, diag)
                act.wait_ge(an_all, 2)
                for i in range(C):
                    nc.scalar.activation(an_h[:, i, :], sim[:, i, :], ACT.Copy, scale=k.s(SAN)).then_inc(ach, 1)

            @block.tensor
            def _(pe):
                pe.wait_ge(copied, C)
                for i in range(C):
                    need(pe, simsum, i - 1)
                    for j in range(C):
                        last = nc.tensor.transpose(tp[i % 2][:, j * P:(j + 1) * P], raw[:, j, i * P:(i + 1) * P], k.ident[:])
                    last.then_inc(tr, 1)
                if weights:
                    pe.wait_ge(dsum, C)
                    weights.on_tensor(pe, pair, diag)
                pe.wait_ge(a_ready, C)
                for c in range(C):
                    for i in range(C):
                        last = nc.tensor.matmul(dc[:, c:c + 1], raw[:, i, c * P:(c + 1) * P], k.ones[:, 0:1],
                                                start=(i == 0), stop=(i == C - 1))
                last.then_inc(deg, 1)
                pe.wait_ge(dd_ready, 1)
                nc.tensor.matmul(dr[:], k.ones[:], degr[:], start=True, stop=True).then_inc(deg, 1)

            @block.gpsimd
            def _(pool):
                for i in range(C):
                    pool.wait_ge(dsum, i + 1)
                    where = dict(compare_op=ALU.not_equal, base=i * P, pattern=[[-1, N]], channel_multiplier=1)
                    pool.affine_select(out=work[:, i, :], in_=sim[:, i, :], fill=SENT, **where).then_inc(masked, 1)
                    pool.wait_ge(masked, 2 * i + 1)
                    pool.affine_select(out=sim[:, i, :], in_=sim[:, i, :], fill=0.0, **where).then_inc(masked, 1)
                for j in range(8):
                    pool.memset(ranks[:, j:j + 1], float(j)).then_inc(masked, 1)
                pool.wait_ge(st, 2 * C)
                pool.tensor_tensor(delta[:], mvs[:, :, 1], k.s(PLUS_HALF).broadcast_to([P, C]), ALU.pow).then_inc(sd_r, 1)
                pool.wait_ge(bad_in, 1)
                pool.partition_all_reduce(worst[:], worst[:], P, RMAX).then_inc(bad_all, 1)
                if weights:
                    weights.on_gpsimd(pool)
                half = k.s(HALF)
                pool.wait_ge(deg_c, 1)
                pool.tensor_tensor(degc[:, 1, :], degc[:, 1, :], half.broadcast_to([P, C]), ALU.pow).then_inc(pw, 1)
                pool.tensor_tensor(k.s(TMP_A), k.s(TMP_A), half, ALU.pow).then_inc(pw, 1)
                pool.wait_ge(an_max, 1)
                pool.partition_all_reduce(mxp[:], mxp[:], P, ABSMAX).then_inc(an_all, 1)

            @block.vector
            def _(dve):
                ch = Chain(dve, ch_s)
                for i in range(C):
                    dve.wait_ge(tr, i + 1)
                    nc.vector.tensor_tensor(sim[:, i, :], raw[:, i, :], tp[i % 2][:], ALU.add).then_inc(simsum, 1)
                    dve.wait_ge(simsum, i + 1)
                    blk = slice(i * P, (i + 1) * P)
                    nc.vector.scalar_tensor_tensor(sim[:, i, blk], diag[:, blk], SIM, sim[:, i, blk], ALU.mult,
                                                   ALU.add).then_inc(dsum, 1)
                ch(nc.vector.tensor_scalar(wa_h[:], k.adj[:], k.s(W_ADJ), None, ALU.mult))
                ch(nc.vector.scalar_tensor_tensor(wa_l[:], k.adj[:], k.s(W_ADJ), wa_h[:], ALU.mult, ALU.subtract))
                dve.wait_ge(masked, 2 * C + 8)
                for i in range(C):
                    nc.vector.bn_stats(bns[:, i, :], sim[:, i, :]).then_inc(st, 1)
                for i in range(C):
                    dve.wait_ge(st, i + 1)
                    nc.vector.bn_aggr(mvs[:, i, :], bns[:, i, :]).then_inc(st, 1)
                dve.wait_ge(sd_r, 1)
                ch(nc.vector.scalar_tensor_tensor(thr[:], delta[:], 0.5, mvs[:, :, 0], ALU.mult, ALU.add))
                nc.vector.tensor_scalar(delta[:], delta[:], 0.25, None, ALU.mult).then_inc(search, 1)

                def at_or_above(i):
                    return nc.vector.tensor_scalar(raw[:, i, :], work[:, i, :], thr[:, i:i + 1], None, ALU.is_ge, ALU.add,
                                                   accum_out=cnt[:, i:i + 1])

                def search_step(it):
                    base = it * STEPS + 1
                    dve.wait_ge(search, base)
                    for i in range(HALF_C):
                        at_or_above(i).then_inc(search, 1)
                    a, b = slice(0, HALF_C), slice(HALF_C, C)
                    dve.wait_ge(search, base + HALF_C)
                    up, down = (TOPK + 0.5, ALU.is_gt), (TOPK - 8.5, ALU.is_lt)
                    for m, (bound, op) in enumerate((up, down)):
                        nc.vector.scalar_tensor_tensor(move[:, m, a], cnt[:, a], bound, delta[:, a], op,
                                                       ALU.mult).then_inc(search, 1)
                    dve.wait_ge(cnt_b, (it + 1) * HALF_C)
                    up, down = (N - 2 * (TOPK + 0.5), ALU.is_lt), (N - 2 * (TOPK - 8.5), ALU.is_gt)
                    for m, (bound, op) in enumerate((up, down)):
                        nc.vector.scalar_tensor_tensor(move[:, m, b], cnt[:, b], bound, delta[:, b], op,
                                                       ALU.mult).then_inc(search, 1)
                    dve.wait_ge(search, base + HALF_C + 4)
                    nc.vector.tensor_tensor(move[:, 0, :], move[:, 0, :], move[:, 1, :], ALU.subtract).then_inc(search, 1)
                    nc.vector.tensor_scalar(delta[:], delta[:], 0.5, None, ALU.mult).then_inc(search, 1)
                    dve.wait_ge(search, base + HALF_C + 6)
                    nc.vector.tensor_tensor(thr[:], thr[:], move[:, 0, :], ALU.add).then_inc(search, 1)
                with dve.Fori(0, SEARCH) as it:
                    search_step(it)
                dve.wait_ge(search, SEARCH * STEPS + 1)
                dve.wait_ge(cnt_b, SEARCH * HALF_C)
                for i in range(C):
                    at_or_above(i).then_inc(pick, 1)
                dve.wait_ge(pick, C)
                ch(nc.vector.tensor_scalar(left[:], cnt[:], -1.0, float(TOPK - 4), ALU.mult, ALU.add))
                nc.vector.tensor_reduce(worst[:], left[:], axis=AX_X, op=ALU.max,
                                        apply_absolute_value=True).then_inc(bad_in, 1)
                ch(nc.vector.tensor_scalar(left[:], left[:], 4.0, None, ALU.add))
                for i in range(C):
                    nc.vector.scalar_tensor_tensor(raw[:, i, :], raw[:, i, :], SENT, work[:, i, :], ALU.mult,
                                                   ALU.add).then_inc(pick, 1)
                dve.wait_ge(bad_all, 1)
                ch(nc.vector.tensor_scalar(flag[:], worst[:], 4.5, None, ALU.is_gt))
                dve.wait_ge(pick, 2 * C)
                outside = dve.value_load(flag[0:1, 0:1], min_val=0, max_val=1)
                with dve.If(outside > 0):
                    def round_of_eight(t):
                        for i in range(C):
                            if not (isinstance(t, int) and t == 0):
                                settle(dve, rounds, (t - 1) * 2 * C + C + i + 1, k.idle["dve"])
                            nc.vector.max(m8[:, i, :], work[:, i, :]).then_inc(rounds, 1)
                        for i in range(C):
                            settle(dve, rounds, t * 2 * C + i + 1, k.idle["dve"])
                            nc.vector.match_replace(work[:, i, :], m8[:, i, :], work[:, i, :], SENT).then_inc(rounds, 1)
                    round_of_eight(0)
                    with dve.Fori(1, ROUNDS) as t:
                        round_of_eight(t)
                    dve.wait_ge(rounds, ROUNDS * 2 * C)
                    nc.vector.memset(left[:], 1.0).then_inc(rounds, 1)
                    for i in range(C):
                        nc.vector.tensor_copy(raw[:, i, :], work[:, i, :]).then_inc(rounds, 1)
                    dve.wait_ge(rounds, ROUNDS * 2 * C + C + 1)
                for i in range(C):
                    nc.vector.max(m8[:, i, :], raw[:, i, :]).then_inc(pick, 1)
                ch(nc.vector.tensor_tensor(sel[:], over(ranks[:], C), spread(left[:], 8), ALU.is_ge))
                dve.wait_ge(pick, 3 * C)
                ch(nc.vector.scalar_tensor_tensor(m8[:], sel[:], SENT, m8[:], ALU.mult, ALU.add))
                for i in range(C):
                    nc.vector.match_replace(raw[:, i, :], m8[:, i, :], raw[:, i, :], SENT).then_inc(pick, 1)
                for i in range(C):
                    dve.wait_ge(pick, 3 * C + i + 1)
                    nc.vector.scalar_tensor_tensor(raw[:, i, :], raw[:, i, :], SENT, sim[:, i, :], ALU.is_equal,
                                                   ALU.mult).then_inc(a_ready, 1)
                dve.wait_ge(deg, 1)
                ch(nc.vector.tensor_copy(degc[:, 0, :], dc[:, 0:C]))
                ch(nc.vector.tensor_scalar(k.s(TMP_A), k.s(NSQ_MAX), 1e-30, None, ALU.max))
                nc.vector.tensor_scalar(degc[:, 1, :], dc[:, 0:C], 1e-37, None, ALU.max).then_inc(deg_c, 1)
                dve.wait_ge(pw, 2)
                ch(nc.vector.scalar_tensor_tensor(degc[:, 0, :], degc[:, 0, :], 0.0, degc[:, 1, :], ALU.is_gt, ALU.mult))
                nc.vector.tensor_tensor(grouped(degr[:]), over(k.ident[:], C), spread(degc[:, 0, :], P),
                                        ALU.mult).then_inc(dd_ready, 1)
                dve.wait_ge(deg, 2)
                for i in range(C):
                    ch(nc.vector.scalar_tensor_tensor(sim[:, i, :], raw[:, i, :], degc[:, 0, i:i + 1], dr[:],
                                                      ALU.mult, ALU.mult))
                nc.vector.tensor_reduce(mxp[:], sim[:], axis=mybir.AxisListType.XY, op=ALU.max,
                                        apply_absolute_value=True).then_inc(an_max, 1)
                ch(nc.vector.tensor_scalar(k.s(SX), k.s(TMP_A), S_COL, None, ALU.mult))
                dve.wait_ge(an_all, 1)
                ch(nc.vector.tensor_scalar(k.s(TMP_B), mxp[:], 1e-18, 1.0 / S_AN, ALU.max, ALU.mult))
                nc.vector.reciprocal(k.s(SAN), k.s(TMP_B)).then_inc(an_all, 1)
                dve.wait_ge(an_all, 2)
                ch(nc.vector.tensor_scalar(k.s(TMP_A), k.s(SX), k.s(W_ADJ), S_EVAC, ALU.mult, ALU.mult))
                ch(nc.vector.reciprocal(k.s(TMP_C), k.s(TMP_A)))
                ch(nc.vector.tensor_scalar(k.s(F_B), k.s(TMP_C), k.s(TMP_B), None, ALU.mult))
                for i in range(C):
                    dve.wait_ge(ach, i + 1)
                    ch(nc.vector.scalar_tensor_tensor(an_l[:, i, :], sim[:, i, :], k.s(SAN), an_h[:, i, :], ALU.mult,
                                                      ALU.subtract))


def propagate(k, an_h, an_l, wa_h, wa_l, bias, b1, out):
    nc = k.nc
    second = b1 is not None
    (xh_r, xl_r, xw_d, wh_r, wl_r, o_d, t_r, add_r, st_r, ag_r, rs_r, nm_r, ln_r, yh_r, yl_r, m_d, pb_r, add2_r, st2_r,
     ag2_r, rs2_r, nm2_r, ln2_r) = (k.sem(n) for n in (
         "x_hi", "x_lo", "xw_done", "xw_hi", "xw_lo", "out_done", "out_biased", "added", "stats", "moments", "rstd",
         "shift", "normed", "y_hi", "y_lo", "mix_done", "y_biased", "added2", "stats2", "moments2", "rstd2", "shift2",
         "normed2"))
    b1_in, w2_r, ch_s, dummy = k.sem("b1_in"), k.sem("w2_ready"), k.sem("chain"), k.sem("eps_set")
    stored = [k.sem(f"stored{i}") for i in range(4)]
    with ExitStack() as ctx:
        xh, xl = (k.sb(ctx, n, [P, 2, N], F16) for n in ("xh", "xl"))
        wh, wl = (k.sb(ctx, n, [P, 2, N], F16) for n in ("xwh", "xwl"))
        t = k.sb(ctx, "t", [P, 2, N])
        bn = k.sb(ctx, "bn", [P, 2, 6])
        mv = k.sb(ctx, "mv", [P, 4, 2])
        rstd = k.sb(ctx, "rstd", [P, 4, 2])
        if second:
            yh, yl = (k.sb(ctx, n, [P, 2, N], F16) for n in ("yh", "yl"))
            w2 = k.sb(ctx, "w2", [P, P])
            w2h, w2l = (k.sb(ctx, n, [P, P], F16) for n in ("w2h", "w2l"))
            b1b = k.sb(ctx, "b1_bcast", [P, N])
            bn2 = k.sb(ctx, "bn2", [P, 2, 6])
            mv2 = k.sb(ctx, "mv2", [P, 4, 2])
            rstd2 = k.sb(ctx, "rstd2", [P, 4, 2])
            pm = [k.ps(ctx, f"pm{i}") for i in range(2)]
        px = [k.ps(ctx, f"px{i}") for i in range(2)]
        po = [k.ps(ctx, f"po{i}") for i in range(2)]
        depth = 10 if second else 7
        R = 4
        X = k.X
        with nc.Block() as block:
            @block.sync
            def _(sp):
                if second:
                    sp.dma_start(b1b[:], b1.partition_broadcast(P)).then_inc(b1_in, 16)
                    sp.wait_ge(b1_in, 16)
                else:
                    for r in range(4):
                        sp.wait_ge(ln_r, r + 1)
                        sp.dma_start(out[r], X[:, r, :]).then_inc(stored[r], 16)
                    with strided(sp, 4, B, 4) as base:
                        for r in range(4):
                            settle(sp, stored[r], base * 4, k.idle["sp"])
                            settle(sp, ln_r, base + r + 1, k.idle["sp"])
                            sp.dma_start(out[base + r], X[:, base + r, :]).then_inc(stored[r], 16)
                    for r in range(4):
                        sp.wait_ge(stored[r], 16 * B // 4)

            @block.scalar
            def _(act):
                def step(s):
                    if s.live(0):
                        b, r = s.at(0), s.slot(0)
                        settle(act, xw_d, b - 1, k.idle["act"])
                        nc.scalar.activation(xh[:, r, :], X[:, b, :], ACT.Copy, scale=k.s(SX)).then_inc(xh_r, 1)
                    if s.live(2):
                        b, r = s.at(2), s.slot(2)
                        act.wait_ge(xw_d, b + 1)
                        need(act, o_d, b - 1)
                        nc.scalar.activation(wh[:, r, :], px[r][:], ACT.Copy, scale=S_EVAC).then_inc(wh_r, 1)
                    if s.live(4):
                        b, r = s.at(4), s.slot(4)
                        act.wait_ge(o_d, b + 1)
                        need(act, add_r, b - 1)
                        nc.scalar.activation(t[:, r, :], po[r][:], ACT.Identity, scale=k.s(F_B), bias=bias[:]).then_inc(t_r, 1)
                    if s.live(7):
                        b, r = s.at(7), s.slot(7, 4)
                        settle(act, nm_r, b + 1, k.idle["act"])
                        nc.scalar.activation(X[:, b, :], X[:, b, :], ACT.Identity, scale=rstd[:, r, 0:1],
                                             bias=rstd[:, r, 1:2]).then_inc(ln_r, 1)
                        if second:
                            act.wait_ge(ln_r, b + 1)
                            settle(act, m_d, b - 1, k.idle["act"])
                            nc.scalar.activation(yh[:, s.slot(7), :], X[:, b, :], ACT.Copy, scale=S_LN).then_inc(yh_r, 1)
                    if second and s.live(10):
                        b, r = s.at(10), s.slot(10, 4)
                        settle(act, nm2_r, b + 1, k.idle["act"])
                        nc.scalar.activation(X[:, b, :], X[:, b, :], ACT.Identity, scale=rstd2[:, r, 0:1],
                                             bias=rstd2[:, r, 1:2]).then_inc(ln2_r, 1)
                pipeline(act, B, depth, R, step)

            @block.vector
            def _(dve):
                if second:
                    dve.wait_ge(b1_in, 16)
                    ch = Chain(dve, ch_s)
                    ch(nc.vector.tensor_tensor(w2[:], k.adj[:], k.adj[:], ALU.mult))
                    ch(nc.vector.tensor_tensor(w2[:], w2[:], k.ident[:], ALU.add))
                    ch(nc.vector.tensor_scalar(k.s(TMP_A), k.s(M_ADJ), k.s(M_ADJ), S_W * S_W, ALU.mult, ALU.mult))
                    ch(nc.vector.tensor_scalar(k.s(TMP_B), k.s(TMP_A), 1.0, 1.0 / S_W, ALU.add, ALU.mult))
                    ch(nc.vector.reciprocal(k.s(W_SQ), k.s(TMP_B)))
                    ch(nc.vector.tensor_scalar(k.s(F_L1), k.s(TMP_B), 1.0 / S_LN, None, ALU.mult))
                    ch(nc.vector.tensor_scalar(w2h[:], w2[:], k.s(W_SQ), None, ALU.mult))
                    nc.vector.scalar_tensor_tensor(w2l[:], w2[:], k.s(W_SQ), w2h[:], ALU.mult,
                                                   ALU.subtract).then_inc(w2_r, 1)

                idle = k.idle["dve"]

                def step(s):
                    if second and s.live(9):
                        b, r = s.at(9), s.slot(9)
                        dve.wait_ge(m_d, b + 1)
                        nc.vector.scalar_tensor_tensor(X[:, b, :], pm[r][:], k.s(F_L1), b1b[:], ALU.mult,
                                                       ALU.add).then_inc(add2_r, 1)
                    if s.live(6):
                        b, r = s.at(6), s.slot(6)
                        settle(dve, add_r, b + 1, idle)
                        nc.vector.bn_stats(bn[:, r, :], X[:, b, :]).then_inc(st_r, 1)
                    if second and s.live(9):
                        b, r = s.at(9), s.slot(9)
                        settle(dve, add2_r, b + 1, idle)
                        nc.vector.bn_stats(bn2[:, r, :], X[:, b, :]).then_inc(st2_r, 1)
                    if s.live(6):
                        b, r, q = s.at(6), s.slot(6), s.slot(6, 4)
                        settle(dve, nm_r, b - 3, idle)
                        settle(dve, st_r, b + 1, idle)
                        nc.vector.bn_aggr(mv[:, q, :], bn[:, r, :]).then_inc(ag_r, 1)
                    if s.live(0):
                        b, r = s.at(0), s.slot(0)
                        dve.wait_ge(xh_r, b + 1)
                        need(dve, xw_d, b - 1)
                        nc.vector.scalar_tensor_tensor(xl[:, r, :], X[:, b, :], k.s(SX), xh[:, r, :], ALU.mult,
                                                       ALU.subtract).then_inc(xl_r, 1)
                    if second and s.live(9):
                        b, r, q = s.at(9), s.slot(9), s.slot(9, 4)
                        settle(dve, nm2_r, b - 3, idle)
                        settle(dve, st2_r, b + 1, idle)
                        nc.vector.bn_aggr(mv2[:, q, :], bn2[:, r, :]).then_inc(ag2_r, 1)
                    if s.live(2):
                        b, r = s.at(2), s.slot(2)
                        dve.wait_ge(wh_r, b + 1)
                        need(dve, o_d, b - 1)
                        nc.vector.scalar_tensor_tensor(wl[:, r, :], px[r][:], S_EVAC, wh[:, r, :], ALU.mult,
                                                       ALU.subtract).then_inc(wl_r, 1)
                    if second and s.live(7):
                        b, r = s.at(7), s.slot(7)
                        dve.wait_ge(yh_r, b + 1)
                        need(dve, m_d, b - 1)
                        nc.vector.scalar_tensor_tensor(yl[:, r, :], X[:, b, :], S_LN, yh[:, r, :], ALU.mult,
                                                       ALU.subtract).then_inc(yl_r, 1)
                pipeline(dve, B, depth, R, step)

            @block.gpsimd
            def _(pool):
                def moments(b, q, mvt, rst, aggr, rsem, nsem, lns):
                    need(pool, lns, b - 3)
                    settle(pool, aggr, b + 1, k.idle["pool"])
                    pool.tensor_scalar(rst[:, q, 1:2], mvt[:, q, 1:2], LN_EPS, None, ALU.add).then_inc(rsem, 1)
                    pool.wait_ge(rsem, 2 * b + 1)
                    pool.tensor_tensor(rst[:, q, 0:1], rst[:, q, 1:2], k.s(HALF), ALU.pow).then_inc(rsem, 1)
                    settle(pool, rsem, 2 * b + 2, k.idle["pool"])
                    pool.tensor_scalar(rst[:, q, 1:2], mvt[:, q, 0:1], rst[:, q, 0:1], -1.0, ALU.mult,
                                       ALU.mult).then_inc(nsem, 1)

                def step(s):
                    if s.live(5):
                        b, r = s.at(5), s.slot(5)
                        settle(pool, t_r, b + 1, k.idle["pool"])
                        pool.tensor_tensor(X[:, b, :], X[:, b, :], t[:, r, :], ALU.add).then_inc(add_r, 1)
                    if s.live(6):
                        moments(s.at(6), s.slot(6, 4), mv, rstd, ag_r, rs_r, nm_r, ln_r)
                    if second and s.live(9):
                        moments(s.at(9), s.slot(9, 4), mv2, rstd2, ag2_r, rs2_r, nm2_r, ln2_r)
                pipeline(pool, B, depth, R, step)

            @block.tensor
            def _(pe):
                if second:
                    pe.wait_ge(w2_r, 1)

                def step(s):
                    if s.live(1):
                        b, r = s.at(1), s.slot(1)
                        pe.wait_ge(xl_r, b + 1)
                        need(pe, wl_r, b - 1)
                        for c in range(C):
                            cs = slice(c * P, (c + 1) * P)
                            nc.tensor.matmul(px[r][:, cs], xh[:, r, cs], wa_h[:], start=True, stop=False)
                            nc.tensor.matmul(px[r][:, cs], xh[:, r, cs], wa_l[:], start=False, stop=False)
                            last = nc.tensor.matmul(px[r][:, cs], xl[:, r, cs], wa_h[:], start=False, stop=True)
                        last.then_inc(xw_d, 1)
                    if s.live(3):
                        b, r = s.at(3), s.slot(3)
                        pe.wait_ge(wl_r, b + 1)
                        need(pe, t_r, b - 1)
                        for c in range(C):
                            cs = slice(c * P, (c + 1) * P)
                            nc.tensor.matmul(po[r][:], wh[:, r, cs], an_h[:, c, :], start=(c == 0), stop=False)
                            nc.tensor.matmul(po[r][:], wh[:, r, cs], an_l[:, c, :], start=False, stop=False)
                            last = nc.tensor.matmul(po[r][:], wl[:, r, cs], an_h[:, c, :], start=False, stop=(c == C - 1))
                        last.then_inc(o_d, 1)
                    if second and s.live(8):
                        b, r = s.at(8), s.slot(8)
                        pe.wait_ge(yl_r, b + 1)
                        need(pe, add2_r, b - 1)
                        nc.tensor.matmul(pm[r][:], w2h[:], yh[:, r, :], start=True, stop=False)
                        nc.tensor.matmul(pm[r][:], w2h[:], yl[:, r, :], start=False, stop=False)
                        nc.tensor.matmul(pm[r][:], w2l[:], yh[:, r, :], start=False, stop=True).then_inc(m_d, 1)
                pipeline(pe, B, depth, R, step)


def adaptive_layer(k, rows_bank, weights, bias, b1, out):
    with ExitStack() as banks:
        with ExitStack() as ctx:
            an_h, an_l = (k.sb(ctx, n, [P, C, N], F16) for n in ("an_h", "an_l"))
            wa_h, wa_l = (k.sb(ctx, n, [P, P], F16) for n in ("wa_h", "wa_l"))
            with ExitStack() as buffers:
                mix = weights and weights(buffers)
                pair, diag = similarity(k, banks, rows_bank, mix)
                neighbours(k, pair, diag, an_h, an_l, wa_h, wa_l, mix)
            banks.close()
            if weights:
                k.release_semaphores()
            propagate(k, an_h, an_l, wa_h, wa_l, bias, b1, out)


def kernel_mix(k, w, rows_bank):
    nc, X, idle = k.nc, k.X, k.idle["dve"]
    DIAG, SMALL = 5, 15
    (st_in, t_d, h_h, h_l, tl_d, tl_h, tl_l, tg_d, tg_h, tg_l, gl_d, gg_d, tl_c, tg_c, diag_r, dd_r, bc_d, sum_r, mask_r, u_r, e_r,
     k_r, kt_d, kt_h, kt_l, v_d, v_h, v_l, o_d, o_u, bn_r, mv_r, rs_r, nm_r, ln_r, sq_r, sq_h, sq_l, ns_d, ksm, msk_r, consts,
     diag_pow, unit_ready) = (
        k.sem(n) for n in (
            "stage_in", "xT_done", "xT_hi", "xT_lo", "tl_done", "tl_hi", "tl_lo", "tg_done", "tg_hi", "tg_lo", "T_l_done",
            "T_g_done", "T_l_copied", "T_g_shifted", "diag_chain", "diag_ready", "flipped", "G_l_used", "masked_l", "u_ready",
            "exp_ready", "k_ready", "kT_done", "kT_hi", "kT_lo", "v_done", "v_hi", "v_lo", "out_done",
            "out_added", "stats", "moments", "rstd", "shift", "normed", "sq_ready", "sq_hi", "sq_lo", "sums_done", "k_chain",
            "mask_ready", "constants", "length_pow", "unit_col_ready"))
    with ExitStack() as ctx:
        stage = k.sb(ctx, "stage", [P, G, N])
        xT_h, xT_l, tl_hi, tl_lo, tg_hi, tg_lo, v_hi, v_lo = (
            k.sb(ctx, n, [P, C, N], F16) for n in ("xT_h", "xT_l", "tl_h", "tl_l", "tg_h", "tg_l", "v_h", "v_l"))
        kT_hi, kT_lo = (k.sb(ctx, n, [P, N], F16) for n in ("kT_h", "kT_l"))
        dd, gs, es = (k.sb(ctx, n, [P, N]) for n in ("dd", "gs", "es"))
        sq = k.sb(ctx, "sq", [P, N])
        sq_hi, sq_lo = (k.sb(ctx, n, [P, N], F16) for n in ("sq_hi", "sq_lo"))
        unit_col = k.sb(ctx, "unit_col", [P, B - 1 + P], F16)
        mask = k.sb(ctx, "mask", [P, P])
        rn = k.sb(ctx, "rnl", [P, G])
        hs = k.sb(ctx, "half_sq", [P, G])
        sm = k.sb(ctx, "small", [P, 4, G])
        bn = k.sb(ctx, "bn", [P, G, 6])
        mv = k.sb(ctx, "mv", [P, G, 2])
        rs = k.sb(ctx, "rs", [P, 2, G])
        work = [k.ps(ctx, f"work{i}") for i in range(4)]
        pgl, pgg, pbc = (k.ps(ctx, n) for n in ("gram_l", "gram_g", "bcast"))
        pkt = pbc
        with nc.Block() as block:
            @block.sync
            def _(sp):
                def load(g):
                    sp.dma_start(stage[:], X[:, bass.ds(g * G, G), :]).then_inc(st_in, 16)
                load(0)
                with sp.Fori(1, NG) as g:
                    settle(sp, t_d, g * C, k.idle["sp"])
                    load(g)

            @block.tensor
            def _(pe):
                def transposes(g):
                    pe.wait_ge(st_in, (g + 1) * 16)
                    for d in range(C):
                        need(pe, v_l, (g - 1) * G + d + 1)
                        for j in range(G):
                            last = nc.tensor.transpose(work[d][:, j * P:(j + 1) * P], stage[:, j, d * P:(d + 1) * P],
                                                       k.ident[:])
                        last.then_inc(t_d, 1)

                def project(g, w_h, w_l, free, done):
                    for e in range(C):
                        pe.wait_ge(free, g * C + e + 1)
                        if e == 0:
                            pe.wait_ge(h_l, g * C + C)
                        es_ = slice(e * P, (e + 1) * P)
                        for d in range(e + 1):
                            nc.tensor.matmul(work[e][:], w_h[:, d, es_], xT_h[:, d, :], start=(d == 0), stop=False)
                            nc.tensor.matmul(work[e][:], w_h[:, d, es_], xT_l[:, d, :], start=False, stop=False)
                            last = nc.tensor.matmul(work[e][:], w_l[:, d, es_], xT_h[:, d, :], start=False,
                                                    stop=(d == e))
                        last.then_inc(done, 1)

                def gram(bank, t_h, t_l, done):
                    for j in range(G):
                        js = slice(j * P, (j + 1) * P)
                        for e in range(C):
                            nc.tensor.matmul(bank[:, js], t_h[:, e, js], xT_h[:, e, js], start=(e == 0), stop=False)
                            nc.tensor.matmul(bank[:, js], t_h[:, e, js], xT_l[:, e, js], start=False, stop=False)
                            last = nc.tensor.matmul(bank[:, js], t_l[:, e, js], xT_h[:, e, js], start=False,
                                                    stop=(e == C - 1))
                    last.then_inc(done, 1)

                def norm_sums(s, j):
                    g = s.at(2)
                    b = g * G + j
                    first, final = (isinstance(b, int) and b == e for e in (0, B - 1))
                    pick = unit_col[:, bass.ds(b, P)]
                    pe.wait_ge(sq_l, b + 1)
                    nc.tensor.matmul(rows_bank[:], pick, sq_hi[:], start=first, stop=False, skip_group_check=True)
                    nc.tensor.matmul(rows_bank[:], pick, sq_lo[:], start=False, stop=final,
                                     skip_group_check=True).then_inc(ns_d, 1)

                pe.wait_ge(unit_ready, 2)

                def step(s):
                    if s.live(0):
                        transposes(s.at(0))
                    if s.live(1):
                        g = s.at(1)

                        def flip(bank, src):
                            for j in range(G):
                                js = slice(j * P, (j + 1) * P)
                                last = nc.tensor.transpose(bank[:, js], src[:, js], k.ident[:])
                            return last
                        pe.wait_ge(tl_c, g + 1)
                        pe.wait_ge(diag_r, g * DIAG + 1)
                        flip(pgl, gs)
                        need(pe, kt_l, g)
                        pe.wait_ge(dd_r, g + 1)
                        nc.tensor.matmul(pbc[:], k.ones[:], dd[:], start=True, stop=True).then_inc(bc_d, 1)
                        pe.wait_ge(tg_c, g + 1)
                        flip(pgg, es).then_inc(bc_d, 1)
                    if s.live(0):
                        project(s.at(0), w["wl_h"], w["wl_l"], h_l, tl_d)
                    if s.live(2):
                        norm_sums(s, 0)
                    if s.live(0):
                        project(s.at(0), w["wg_h"], w["wg_l"], tl_l, tg_d)
                    if s.live(1):
                        g = s.at(1)
                        pe.wait_ge(k_r, g + 1)
                        for j in range(G):
                            last = nc.tensor.transpose(pkt[:, j * P:(j + 1) * P], gs[:, j * P:(j + 1) * P], k.ident[:])
                        last.then_inc(kt_d, 1)
                    if s.live(2):
                        norm_sums(s, 1)
                    if s.live(0):
                        g = s.at(0)
                        pe.wait_ge(tl_l, (g + 1) * C)
                        gram(pgl, tl_hi, tl_lo, gl_d)
                        pe.wait_ge(tg_l, (g + 1) * C)
                        gram(pgg, tg_hi, tg_lo, gg_d)
                    if s.live(2):
                        norm_sums(s, 2)
                    if s.live(1):
                        g = s.at(1)
                        pe.wait_ge(kt_l, g + 1)
                        pe.wait_ge(v_l, (g + 1) * G)
                        for j in range(G):
                            js = slice(j * P, (j + 1) * P)
                            if not isinstance(s.i, int) or s.i < NG:
                                pe.wait_ge(tg_l, (g + 1) * C + j + 1)
                            nc.tensor.matmul(work[j][:], kT_hi[:, js], v_hi[:, j, :], start=True, stop=False)
                            nc.tensor.matmul(work[j][:], kT_hi[:, js], v_lo[:, j, :], start=False, stop=False)
                            nc.tensor.matmul(work[j][:], kT_lo[:, js], v_hi[:, j, :], start=False,
                                             stop=True).then_inc(o_d, 1)
                    if s.live(0):
                        g = s.at(0)
                        for j in range(G):
                            js = slice(j * P, (j + 1) * P)
                            need(pe, o_u, (g - 1) * G + j + 1)
                            for d in range(C):
                                nc.tensor.matmul(work[j][:], xT_h[:, d, js], w["m_h"][:, d, :], start=(d == 0), stop=False)
                                nc.tensor.matmul(work[j][:], xT_h[:, d, js], w["m_l"][:, d, :], start=False, stop=False)
                                last = nc.tensor.matmul(work[j][:], xT_l[:, d, js], w["m_h"][:, d, :], start=False,
                                                        stop=(d == C - 1))
                            last.then_inc(v_d, 1)
                    if s.live(2):
                        norm_sums(s, 3)
                pipeline(pe, NG, 2, 1, step)

            @block.scalar
            def _(act):
                def square(g, j):
                    b = g * G + j
                    need(act, sq_l, b)
                    settle(act, ln_r, b + 1, k.idle["act"])
                    nc.scalar.activation(sq[:], X[:, b, :], ACT.Square, scale=S_SQ ** 0.5).then_inc(sq_r, 1)
                    need(act, ns_d, b)
                    act.wait_ge(sq_r, b + 1)
                    nc.scalar.activation(sq_hi[:], sq[:], ACT.Copy).then_inc(sq_h, 1)

                def step(s):
                    if s.live(0):
                        g = s.at(0)
                        need(act, v_d, g * G)
                        for d in range(C):
                            act.wait_ge(t_d, g * C + d + 1)
                            nc.scalar.activation(xT_h[:, d, :], work[d][:], ACT.Copy, scale=S_LN).then_inc(h_h, 1)
                    if s.live(2):
                        g = s.at(2)
                        for j in range(G):
                            b = g * G + j
                            settle(act, nm_r, b + 1, k.idle["act"])
                            nc.scalar.activation(X[:, b, :], X[:, b, :], ACT.Identity, scale=rs[:, 0, j:j + 1],
                                                 bias=rs[:, 1, j:j + 1]).then_inc(ln_r, 1)
                        square(g, 0)
                    if s.live(1):
                        g = s.at(1)
                        act.wait_ge(u_r, g + 1)
                        nc.scalar.activation(es[:], es[:], ACT.Exp, scale=k.s(K_G)).then_inc(e_r, 1)
                    if s.live(0):
                        g = s.at(0)
                        need(act, gl_d, g)
                        for e in range(C):
                            act.wait_ge(tl_d, g * C + e + 1)
                            nc.scalar.activation(tl_hi[:, e, :], work[e][:], ACT.Copy, scale=S_EVAC).then_inc(tl_h, 1)
                    if s.live(2):
                        square(s.at(2), 1)
                    if s.live(0):
                        g = s.at(0)
                        need(act, gg_d, g)
                        for e in range(C):
                            act.wait_ge(tg_d, g * C + e + 1)
                            nc.scalar.activation(tg_hi[:, e, :], work[e][:], ACT.Copy, scale=S_EVAC).then_inc(tg_h, 1)
                    if s.live(1):
                        g = s.at(1)
                        act.wait_ge(kt_d, g + 1)
                        need(act, o_d, g * G)
                        nc.scalar.activation(kT_hi[:], pkt[:], ACT.Copy, scale=S_K).then_inc(kt_h, 1)
                    if s.live(2):
                        square(s.at(2), 2)
                    if s.live(0):
                        g = s.at(0)
                        act.wait_ge(gl_d, g + 1)
                        nc.scalar.activation(gs[:], pgl[:], ACT.Copy).then_inc(tl_c, 1)
                        need(act, o_d, g * G)
                        act.wait_ge(v_d, g * G + 1)
                        nc.scalar.activation(v_hi[:, 0, :], work[0][:], ACT.Copy, scale=S_EVAC).then_inc(v_h, 1)
                    if s.live(2):
                        square(s.at(2), 3)
                    if s.live(0):
                        for j in range(1, G):
                            act.wait_ge(v_d, s.at(0) * G + j + 1)
                            nc.scalar.activation(v_hi[:, j, :], work[j][:], ACT.Copy, scale=S_EVAC).then_inc(v_h, 1)
                pipeline(act, NG, 2, 1, step)

            @block.vector
            def _(dve):
                nc.vector.tensor_scalar(mask[:], k.ident[:], -1.0, 1.0, ALU.mult, ALU.add).then_inc(msk_r, 1)
                dve.wait_ge(msk_r, 1)
                nc.vector.tensor_tensor(mask[:], mask[:], k.adj[:], ALU.mult).then_inc(msk_r, 1)
                ch = Chain(dve, consts)
                ch(nc.vector.tensor_scalar(k.s(EPS_L), k.s(W_WL), 1e-16 * S_LN * S_LN * S_EVAC, None, ALU.mult))
                ch(nc.vector.tensor_scalar(k.s(F_OUT2), k.s(M_M), 1.0 / (S_K * S_EVAC * S_LN), None, ALU.mult))
                ch(nc.vector.tensor_scalar(k.s(TMP_A), k.s(M_WG), 1.0 / (S_LN * S_LN * S_EVAC), None, ALU.mult))
                ch(nc.vector.tensor_scalar(k.s(K_G), k.s(TMP_A), k.s(SIG), None, ALU.mult))
                ch(nc.vector.tensor_scalar(k.s(TMP_B), k.s(GATE), 1.0, None, ALU.add))
                ch(nc.vector.reciprocal(k.s(GATE), k.s(TMP_B)))
                ch(nc.vector.tensor_scalar(k.s(UNGATE), k.s(GATE), -1.0, 1.0, ALU.mult, ALU.add))

                def lo(dst, src, hi, scale, hi_sem, n, done):
                    dve.wait_ge(hi_sem, n)
                    nc.vector.scalar_tensor_tensor(dst, src, scale, hi, ALU.mult, ALU.subtract).then_inc(done, 1)

                def counted(sem, per, g):
                    n = [0]

                    def run(ins, wait=True):
                        n[0] += 1
                        assert n[0] <= per
                        ins.then_inc(sem, 1)
                        if wait:
                            settle(dve, sem, g * per + n[0], idle)
                    return run

                def step(s):
                    if s.live(0):
                        g = s.at(0)
                        for d in range(C):
                            lo(xT_l[:, d, :], work[d][:], xT_h[:, d, :], S_LN, h_h, g * C + d + 1, h_l)
                    if s.live(1):
                        g = s.at(1)
                        run = counted(ksm, SMALL, g)
                        dve.wait_ge(bc_d, 2 * g + 2)
                        run(nc.vector.tensor_tensor(gs[:], gs[:], pgl[:], ALU.add), wait=False)
                        nc.vector.tensor_tensor(es[:], es[:], pgg[:], ALU.add).then_inc(u_r, 1)
                        settle(dve, ksm, g * SMALL + 1, idle)
                        nc.vector.scalar_tensor_tensor(gs[:], gs[:], 0.0, pbc[:], ALU.max, ALU.mult).then_inc(sum_r, 1)
                    if s.live(0):
                        for e in range(2):
                            lo(tl_lo[:, e, :], work[e][:], tl_hi[:, e, :], S_EVAC, tl_h, s.at(0) * C + e + 1, tl_l)
                    if s.live(1):
                        dve.wait_ge(e_r, g + 1)
                        run(nc.vector.scalar_tensor_tensor(grouped(es[:], G), grouped(es[:], G), 1.0, over(mask[:], G),
                                                           ALU.min, ALU.mult), wait=False)
                    if s.live(0):
                        lo(tl_lo[:, 2, :], work[2][:], tl_hi[:, 2, :], S_EVAC, tl_h, s.at(0) * C + 3, tl_l)
                    if s.live(1):
                        dve.wait_ge(mask_r, g + 1)
                        run(nc.vector.tensor_reduce(sm[:, 0, :], grouped(gs[:], G), axis=AX_X, op=ALU.add), wait=False)
                        settle(dve, ksm, g * SMALL + 2, idle)
                        run(nc.vector.tensor_reduce(sm[:, 2, :], grouped(es[:], G), axis=AX_X, op=ALU.add), wait=False)
                    if s.live(0):
                        lo(tl_lo[:, 3, :], work[3][:], tl_hi[:, 3, :], S_EVAC, tl_h, s.at(0) * C + 4, tl_l)
                    if s.live(1):
                        settle(dve, ksm, g * SMALL + 3, idle)
                        run(nc.vector.tensor_tensor(sm[:, 0, :], sm[:, 0, :], rn[:], ALU.mult))
                        run(nc.vector.tensor_scalar(sm[:, 0, :], sm[:, 0, :], 1e-8, None, ALU.max))
                        run(nc.vector.reciprocal(sm[:, 1, :], sm[:, 0, :]), wait=False)
                        run(nc.vector.tensor_scalar(sm[:, 2, :], sm[:, 2, :], 1e-8, None, ALU.max))
                        run(nc.vector.reciprocal(sm[:, 3, :], sm[:, 2, :]), wait=False)
                        run(nc.vector.scalar_tensor_tensor(sm[:, 1, :], sm[:, 1, :], k.s(GATE), rn[:], ALU.mult, ALU.mult))
                        run(nc.vector.tensor_scalar(sm[:, 3, :], sm[:, 3, :], k.s(UNGATE), None, ALU.mult))
                    if s.live(1):
                        for j in range(G):
                            js = slice(j * P, (j + 1) * P)
                            run(nc.vector.tensor_scalar(gs[:, js], gs[:, js], sm[:, 1, j:j + 1], None, ALU.mult),
                                wait=False)
                        for j in range(G):
                            js = slice(j * P, (j + 1) * P)
                            settle(dve, ksm, g * SMALL + SMALL - G + 1 + j, idle)
                            ins = nc.vector.scalar_tensor_tensor(gs[:, js], es[:, js], sm[:, 3, j:j + 1], gs[:, js],
                                                                 ALU.mult, ALU.add)
                        ins.then_inc(k_r, 1)
                    if s.live(0):
                        for e in range(C):
                            lo(tg_lo[:, e, :], work[e][:], tg_hi[:, e, :], S_EVAC, tg_h, s.at(0) * C + e + 1, tg_l)
                    if s.live(1):
                        lo(kT_lo[:], pkt[:], kT_hi[:], S_K, kt_h, s.at(1) + 1, kt_l)
                    if s.live(1):
                        for j in range(G):
                            b = s.at(1) * G + j
                            dve.wait_ge(o_d, b + 1)
                            nc.vector.scalar_tensor_tensor(X[:, b, :], work[j][:], k.s(F_OUT2), X[:, b, :], ALU.mult,
                                                           ALU.add).then_inc(o_u, 1)
                    if s.live(0):
                        g = s.at(0)
                        dve.wait_ge(tl_c, g + 1)
                        run2 = counted(diag_r, DIAG, g)
                        run2(nc.vector.tensor_tensor(grouped(dd[:]), grouped(pgl[:]), over(k.ident[:], G), ALU.mult))
                        run2(nc.vector.tensor_reduce(rn[:], grouped(dd[:]), axis=AX_X, op=ALU.add))
                        dve.wait_ge(gg_d, g + 1)
                        run2(nc.vector.tensor_tensor(grouped(dd[:]), grouped(pgg[:]), over(k.ident[:], G), ALU.mult))
                        run2(nc.vector.tensor_reduce(hs[:], grouped(dd[:]), axis=AX_X, op=ALU.add), wait=False)
                        run2(nc.vector.tensor_scalar(rn[:], rn[:], 2.0, k.s(EPS_L), ALU.mult, ALU.max), wait=False)
                        settle(dve, diag_r, g * DIAG + 4, idle)
                        for j in range(G):
                            js = slice(j * P, (j + 1) * P)
                            ins = nc.vector.tensor_scalar(es[:, js], pgg[:, js], hs[:, j:j + 1], None, ALU.subtract)
                        ins.then_inc(tg_c, 1)
                    if s.live(1):
                        for j in range(G):
                            b = s.at(1) * G + j
                            settle(dve, o_u, b + 1, idle)
                            nc.vector.bn_stats(bn[:, j, :], X[:, b, :]).then_inc(bn_r, 1)
                            settle(dve, bn_r, b + 1, idle)
                            if j == 0:
                                settle(dve, nm_r, s.at(1) * G, idle)
                            nc.vector.bn_aggr(mv[:, j, :], bn[:, j, :]).then_inc(mv_r, 1)
                    if s.live(0):
                        g = s.at(0)
                        dve.wait_ge(diag_pow, g + 1)
                        nc.vector.tensor_tensor(grouped(dd[:]), over(k.ident[:], G), spread(rn[:], P),
                                                ALU.mult).then_inc(dd_r, 1)
                        for j in range(G):
                            lo(v_lo[:, j, :], work[j][:], v_hi[:, j, :], S_EVAC, v_h, g * G + j + 1, v_l)
                pipeline(dve, NG, 2, 1, step)

            @block.gpsimd
            def _(pool):
                pool.memset(unit_col[:], 0.0).then_inc(unit_ready, 1)
                pool.wait_ge(unit_ready, 1)
                pool.memset(unit_col[:, B - 1:B], 1.0).then_inc(unit_ready, 1)
                pool.wait_ge(msk_r, 2)
                half = k.s(HALF)

                def square_lo(s, j):
                    b = s.at(2) * G + j
                    need(pool, ns_d, b)
                    pool.wait_ge(sq_h, b + 1)
                    pool.tensor_tensor(sq_lo[:], sq[:], sq_hi[:], ALU.subtract).then_inc(sq_l, 1)

                def step(s):
                    if s.live(2):
                        square_lo(s, 0)
                    if s.live(1):
                        pool.wait_ge(sum_r, s.at(1) + 1)
                        pool.tensor_tensor(grouped(gs[:], G), grouped(gs[:], G), over(mask[:], G), ALU.mult).then_inc(mask_r, 1)
                    if s.live(2):
                        square_lo(s, 1)
                        square_lo(s, 2)
                    if s.live(0):
                        g = s.at(0)
                        pool.wait_ge(diag_r, (g + 1) * DIAG)
                        pool.tensor_tensor(rn[:], rn[:], half.broadcast_to([P, G]), ALU.pow).then_inc(diag_pow, 1)
                    if s.live(2):
                        square_lo(s, 3)
                    if s.live(1):
                        g = s.at(1)
                        pool.wait_ge(mv_r, (g + 1) * G)
                        need(pool, ln_r, g * G)
                        settle(pool, mv_r, (g + 1) * G, k.idle["pool"])
                        pool.tensor_scalar(rs[:, 1, :], mv[:, :, 1], LN_EPS, None, ALU.add).then_inc(rs_r, 1)
                        settle(pool, rs_r, 3 * g + 1, k.idle["pool"])
                        pool.tensor_tensor(rs[:, 0, :], rs[:, 1, :], half.broadcast_to([P, G]), ALU.pow).then_inc(rs_r, 1)
                        settle(pool, rs_r, 3 * g + 2, k.idle["pool"])
                        pool.tensor_tensor(rs[:, 1, :], mv[:, :, 0], rs[:, 0, :], ALU.mult).then_inc(rs_r, 1)
                        settle(pool, rs_r, 3 * g + 3, k.idle["pool"])
                        pool.tensor_scalar(rs[:, 1, :], rs[:, 1, :], -1.0, None, ALU.mult).then_inc(nm_r, G)
                pipeline(pool, NG, 2, 1, step)


def build(nc, x, adj, b0, b1, wl, wg, wv, wo, gate, logsig, b3, out):
    with ExitStack() as ctx:
        k = Chip(nc, ctx)
        rows_bank = None
        with ExitStack() as parts:
            w = {f"{n}_{h}": k.sb(parts, f"{n}_{h}", [P, C, N], F16) for n in ("wl", "wg", "m") for h in "hl"}
            load_x(k, x, adj, b0, b3, gate, logsig)
            k.release_semaphores()
            adaptive_layer(k, None, lambda buffers: MixWeights(k, buffers, w, wl, wg, wv, wo), k.bias0, b1, None)
            k.release_semaphores()
            rows_bank = k.ps(ctx, "rows_bank")
            kernel_mix(k, w, rows_bank)
            k.release_semaphores()
        adaptive_layer(k, rows_bank, None, k.bias3, None, out)


_INS = ['x', 'adj', 'L0_gnn_bias', 'L1_gnn_bias', 'L2_gnn_W_lang', 'L2_gnn_W_grav', 'L2_gnn_W_V', 'L2_gnn_W_O',
        'L2_gnn_gate_logit', 'L2_gnn_log_sigma', 'L3_gnn_bias']


def kernel(**inputs):
    import numpy as _np
    import concourse.bacc as _bacc
    from concourse import mybir as _mybir
    from concourse.bass_utils import run_bass_kernel_spmd as _run

    nc = _bacc.Bacc("TRN2", target_bir_lowering=False, num_devices=1)
    arrays, args = {}, []
    for name in _INS:
        a = _np.ascontiguousarray(inputs[name])
        if a.ndim == 0:
            a = a.reshape(1)
        arrays[f"in_{name}_dram"] = a
        args.append(nc.dram_tensor(f"in_{name}_dram", a.shape, _mybir.dt.from_np(a.dtype), kind="ExternalInput").ap())
    args.append(nc.dram_tensor("out_0_dram", (B, P, N), F32, kind="ExternalOutput").ap())
    build(nc, *args)
    r = _run(nc, [arrays], core_ids=[0])
    return r.results[0]["out_0_dram"]
```

```python
import concourse.bass as bass
from concourse import mybir
from contextlib import ExitStack, contextmanager

F32 = mybir.dt.float32
F16 = mybir.dt.float16
ALU = mybir.AluOpType
ACT = mybir.ActivationFunctionType
AX_X = mybir.AxisListType.X
ABSMAX = bass.bass_isa.ReduceOp.absmax
RMAX = bass.bass_isa.ReduceOp.max

B, P, N = 64, 128, 512
C = N // P
RUN, BAND = 16, 32
G = 4
NG = B // G
TOPK = int(N * 0.3)
ROUNDS = TOPK // 8
assert TOPK == 8 * ROUNDS + 1
SEARCH = 7
LN_EPS = 1e-5
SENT = -3.0e38

S_RN = 2.0 ** 14
S_COL = 2.0 ** 15
S_W = 2.0 ** 13
S_AN = 2.0 ** 14
S_SQ = 2.0 ** 6
S_F = 2.0 ** 15
S_LN = 2.0 ** 10
S_K = 2.0 ** 14
S_EVAC = 2.0 ** -17

(M_ADJ, M_WL, M_WG, M_M, W_ADJ, W_WL, W_WG, W_M, W_SQ, EPS_L, K_G, GATE, UNGATE, F_OUT2, F_L1, SIG,
 NSQ_MAX, SX, SAN, F_B, TMP_A, TMP_B, HALF, TMP_C, PLUS_HALF) = range(25)
NSCAL = 25


def need(eng, sem, value):
    if isinstance(value, int) and value <= 0:
        return
    eng.wait_ge(sem, value)


@contextmanager
def strided(eng, start, end, step):
    with eng.Fori(start // step, end // step) as u:
        yield u * step


def settle(eng, sem, value, idle):
    if isinstance(value, int):
        return need(eng, sem, value)
    eng.wait_ge(sem, value)
    eng.sem_inc(idle, 1)


class Step:

    def __init__(self, i, rem, total):
        self.i, self.rem, self.total = i, rem, total

    def live(self, lag):
        return not isinstance(self.i, int) or 0 <= self.i - lag < self.total

    def at(self, lag):
        return self.i - lag

    def slot(self, lag, ring=2):
        return (self.rem - lag) % ring


def pipeline(eng, total, depth, ring, step, ahead=0):
    head = -(-(depth + ring) // ring) * ring
    for i in range(-ahead, head):
        step(Step(i, i % ring, total))
    with strided(eng, head, total - ahead, ring) as base:
        for j in range(ring):
            step(Step(base + j, j % ring, total))
    for i in range(total - ahead, total + depth):
        step(Step(i, i % ring, total))


def over(t, reps):
    return t.rearrange("p (o n) -> p o n", o=1).broadcast_to([t.shape[0], reps, t.shape[1]])


def spread(t, width):
    return t.rearrange("p (n o) -> p n o", o=1).broadcast_to([t.shape[0], t.shape[1], width])


def grouped(t, parts=C):
    return t.rearrange("p (a b) -> p a b", a=parts)


class Chip:

    def __init__(self, nc, ctx):
        self.nc, self.ctx = nc, ctx
        self.n = 0
        self.taken = []
        self.X = self.sb(ctx, "x_all", [P, B, N])
        self.ident = self.sb(ctx, "ident", [P, P])
        self.ones = self.sb(ctx, "ones", [P, P])
        self.adj = self.sb(ctx, "adj", [P, P])
        self.sc = self.sb(ctx, "scalars", [P, NSCAL])
        self.bias0 = self.sb(ctx, "bias0", [P, 1])
        self.bias3 = self.sb(ctx, "bias3", [P, 1])
        self.idle = {e: nc.alloc_semaphore(name=f"idle_{e}") for e in ("sp", "dve", "pool", "act")}
        self.rn_rows = nc.dram_tensor("rn_rows", (B, N), F32, kind="Internal").ap()

    def sb(self, ctx, name, shape, dt=F32):
        self.n += 1
        return ctx.enter_context(self.nc.sbuf_tensor(f"{name}_{self.n}", shape, dt))

    def ps(self, ctx, name, shape=(P, N), dt=F32):
        self.n += 1
        return ctx.enter_context(self.nc.psum_tensor(f"{name}_{self.n}", list(shape), dt))

    def sem(self, name):
        self.n += 1
        self.taken.append(self.nc.alloc_semaphore(name=f"{name}_{self.n}"))
        return self.taken[-1]

    def release_semaphores(self):
        self.nc.clear_and_free_semaphores(self.taken)
        self.taken = []
        self.nc.all_engine_barrier()

    def s(self, k):
        return self.sc[:, k:k + 1]


class Chain:

    def __init__(self, eng, sem):
        self.eng, self.sem, self.n = eng, sem, 0

    def __call__(self, ins):
        self.n += 1
        ins.then_inc(self.sem, 1)
        self.eng.wait_ge(self.sem, self.n)


def upper(d):
    return slice(d * P, N)


class ColumnScales:

    def __init__(self, k, rows_bank, scale, banded, early, tiles):
        self.k, self.scale, self.banded = k, scale, banded
        count = B if banded else B // 2
        first = (0 if early else count) if banded else (count if early else 0)
        self.rows = slice(first, first + count)
        self.src = rows_bank[self.rows, :]
        self.d, self.root, self.rn = (t[self.rows, :] for t in tiles)
        self.runs = [(self.rn[j * BAND:j * BAND + RUN, :], (first // BAND + j) * RUN) for j in range(count // BAND)] \
            if banded else [(self.rn, first)]
        self.chain, self.clamped, self.root_r, self.ready, self.stored, self.top = (k.sem(n) for n in (
            "rn_chain", "clamped", "root_ready", "rn_ready", "rn_stored", "nsq_top"))

    def clamp(self, dve):
        k = self.k
        k.nc.vector.tensor_scalar(self.d, self.src, 1.0 / self.scale, 1e-24, ALU.mult, ALU.max).then_inc(self.clamped, 1)
        dve.wait_ge(self.clamped, 1)
        k.nc.vector.tensor_reduce(k.sc[self.rows, NSQ_MAX:NSQ_MAX + 1], self.d, axis=AX_X, op=ALU.max).then_inc(self.top, 1)

    def take_root(self, act):
        act.wait_ge(self.clamped, 1)
        self.k.nc.scalar.activation(self.root, self.d, ACT.Sqrt).then_inc(self.root_r, 1)

    def invert(self, dve):
        dve.wait_ge(self.root_r, 1)
        self.k.nc.vector.reciprocal(self.rn, self.root).then_inc(self.chain, 1)

    def refine(self, dve):
        nc, d, root, rn = self.k.nc, self.d, self.root, self.rn
        dve.wait_ge(self.chain, 1)
        nc.vector.tensor_tensor(root, rn, rn, ALU.mult).then_inc(self.chain, 1)
        dve.wait_ge(self.chain, 2)
        nc.vector.scalar_tensor_tensor(root, d, -0.5 * S_RN, root, ALU.mult, ALU.mult).then_inc(self.chain, 1)
        dve.wait_ge(self.chain, 3)
        nc.vector.scalar_tensor_tensor(rn, root, 1.5 * S_RN, rn, ALU.add, ALU.mult).then_inc(self.ready, 1)

    def store(self, queue):
        queue.wait_ge(self.ready, 1)
        for rows, at in self.runs:
            queue.dma_start(self.k.rn_rows[at:at + rows.shape[0]], rows).then_inc(self.stored, 16)

    def all_stored(self, eng):
        eng.wait_ge(self.stored, 16 * len(self.runs))


class Operand:

    def __init__(self, k, mix, n, name, regions, sum_col):
        self.k, self.name, self.regions, self.sum_col = k, name, regions, sum_col
        self.scale_col, self.inverse_col = {"wl": (W_WL, M_WL), "wg": (W_WG, M_WG), "m": (W_M, M_M)}[name]
        self.hi, self.lo = mix.w[f"{name}_h"], mix.w[f"{name}_l"]
        self.part, self.q, self.half = mix.part[:, n, :], mix.fro[:, n:n + 1], mix.half[:, n:n + 1]
        self.prod, self.sq, self.sum, self.q_in, self.chain, self.scale_r, self.tmp_r, self.hi_r, self.lo_r = (
            k.sem(f"{name}_{n}") for n in ("product", "squares", "square_sum", "norm_in", "scale_chain", "scale_ready",
                                           "scaled", "hi", "lo"))

    def cols(self, d):
        return slice(0, N) if self.name == "m" else upper(d)

    def multiply(self, d, left, right):
        for e in range(C):
            last = self.k.nc.tensor.matmul(self.regions[d], left[:, e, d * P:(d + 1) * P], right[:, e, self.cols(d)],
                                           start=(e == 0), stop=(e == C - 1))
        last.then_inc(self.prod, 1)

    def square(self, act, scratch):
        act.wait_ge(self.prod, C)
        for d in range(C):
            need(act, self.sq, d)
            self.k.nc.scalar.activation(scratch[:, d, self.cols(d)], self.regions[d], ACT.Square,
                                        accum_out=self.part[:, d:d + 1]).then_inc(self.sq, 1)

    def sum_squares(self, pe):
        pe.wait_ge(self.sq, C)
        for d in range(C):
            last = self.k.nc.tensor.matmul(self.sum_col, self.k.ones[:], self.part[:, d:d + 1], start=(d == 0),
                                           stop=(d == C - 1))
        last.then_inc(self.sum, 1)

    def norm_out(self, act):
        act.wait_ge(self.sum, 1)
        self.k.nc.scalar.activation(self.q, self.sum_col, ACT.Copy, scale=1.0 / (S_F * S_F)).then_inc(self.q_in, 1)

    def scales(self, pool):
        k = self.k
        pool.wait_ge(self.q_in, 1)
        pool.tensor_scalar(self.q, self.q, 1e-36, None, ALU.max).then_inc(self.chain, 1)
        pool.wait_ge(self.chain, 1)
        pool.tensor_tensor(k.s(self.scale_col), self.q, k.s(HALF), ALU.pow).then_inc(self.chain, 1)
        pool.tensor_tensor(k.s(self.inverse_col), self.q, k.s(PLUS_HALF), ALU.pow).then_inc(self.chain, 1)
        pool.wait_ge(self.chain, 3)
        pool.tensor_scalar(self.half, k.s(self.scale_col), 0.5, None, ALU.mult).then_inc(self.scale_r, 1)

    def scaled_pieces(self, d):
        scale = self.k.s(self.scale_col)
        if self.name == "m":
            return [(slice(0, N), self.regions[d], scale)]
        pieces = [(slice(d * P, (d + 1) * P), self.regions[d][:, 0:P], self.half)]
        if d < C - 1:
            pieces.append((slice((d + 1) * P, N), self.regions[d][:, P:], scale))
        return pieces

    def scale_and_hi(self, act, buf):
        act.wait_ge(self.scale_r, 1)
        for d in range(C):
            for cs, src, scale in self.scaled_pieces(d):
                last = self.k.nc.scalar.activation(buf[:, d, cs], src, ACT.Copy, scale=scale)
            last.then_inc(self.tmp_r, 1)
        for d in range(C):
            act.wait_ge(self.tmp_r, d + 1)
            self.k.nc.scalar.activation(self.hi[:, d, self.cols(d)], buf[:, d, self.cols(d)],
                                        ACT.Copy).then_inc(self.hi_r, 1)

    def scale_and_hi_on_vector(self, dve, buf):
        nc = self.k.nc
        dve.wait_ge(self.scale_r, 1)
        for d in range(C):
            for cs, src, scale in self.scaled_pieces(d):
                last = nc.vector.tensor_scalar(buf[:, d, cs], src, scale, None, ALU.mult)
            last.then_inc(self.tmp_r, 1)
        for d in range(C):
            dve.wait_ge(self.tmp_r, d + 1)
            nc.vector.tensor_copy(self.hi[:, d, self.cols(d)], buf[:, d, self.cols(d)]).then_inc(self.hi_r, 1)

    def lo_part(self, pool, buf):
        for d in range(C):
            pool.wait_ge(self.hi_r, d + 1)
            pool.tensor_tensor(self.lo[:, d, self.cols(d)], buf[:, d, self.cols(d)], self.hi[:, d, self.cols(d)],
                               ALU.subtract).then_inc(self.lo_r, 1)

    def hi_direct(self, act):
        act.wait_ge(self.scale_r, 1)
        for d in range(C):
            for cs, src, scale in self.scaled_pieces(d):
                last = self.k.nc.scalar.activation(self.hi[:, d, cs], src, ACT.Copy, scale=scale)
            last.then_inc(self.hi_r, 1)

    def lo_direct(self, dve):
        dve.wait_ge(self.hi_r, C)
        for d in range(C):
            for cs, src, scale in self.scaled_pieces(d):
                self.k.nc.vector.scalar_tensor_tensor(self.lo[:, d, cs], src, scale, self.hi[:, d, cs], ALU.mult,
                                                      ALU.subtract).then_inc(self.lo_r, 1)


def packed(banks):
    return [banks[0][:, 0:N], banks[1][:, 0:N - P], banks[2][:, 0:N - 2 * P], banks[1][:, N - P:N]], banks[2][:, N - 1:N]


class MixWeights:

    def __init__(self, k, ctx, w, wl, wg, wv, wo):
        self.k, self.w = k, w
        self.a, self.b = (k.sb(ctx, n, [P, C, N]) for n in ("weights_a", "weights_b"))
        self.sources = {"wl": wl, "wg": wg, "wv": wv, "wo": wo}
        self.win = {}
        self.part = k.sb(ctx, "part_sq", [P, 3, C])
        self.fro, self.half = (k.sb(ctx, n, [P, 3]) for n in ("squared_norm", "half_scale"))

    def load(self, sp, name, buf):
        sp.dma_start(buf[:], self.sources[name].rearrange("(c p) n -> p c n", p=P)).then_inc(self.win[name], 16)

    def arrive(self, *names):
        self.win = {n: self.k.sem(f"{n}_in") for n in names}

    def during_load(self, ctx):
        self.arrive("wl")
        self.lang = Operand(self.k, self, 0, "wl", *packed([self.k.ps(ctx, f"u{i}") for i in range(3)]))

    def during_topk(self, pair, diag, spare, tp0, tp1):
        regions, _ = packed([diag, spare, tp1])
        self.grav = Operand(self.k, self, 1, "wg", regions, tp1[:, N - 1:N])
        self.m = Operand(self.k, self, 2, "m", [bank[:] for bank in pair], tp0[:, N - 1:N])
        self.woT_d, self.woT_c = self.k.sem("woT_done"), self.k.sem("woT_copied")


def load_x(k, x, adj, b0, b3, gate, logsig, mix, rows_bank, tiles):
    nc = k.nc
    PARTS, RS = 16, 4
    x_in = [k.sem(f"x_in{q}") for q in range(PARTS)]
    small_in, consts, zeroed = k.sem("small_in"), k.sem("consts_set"), k.sem("ident_zeroed")
    mx, mxall, chain = k.sem("adj_max"), k.sem("adj_max_all"), k.sem("dve_chain")
    sq_ready, sums = k.sem("sq_ready"), k.sem("sums")
    per = B // PARTS
    with ExitStack() as ctx:
        sq = k.sb(ctx, "sq", [P, RS, N])
        unit_col = k.sb(ctx, "unit_col", [P, RUN - 1 + BAND])
        mix.during_load(ctx)
        early = ColumnScales(k, rows_bank, 1.0, True, True, tiles)
        with nc.Block() as block:
            @block.sync
            def _(sp):
                column = lambda t: t.rearrange("(p o) -> p o", o=1)
                single = lambda t: t.rearrange("(a b) -> a b", a=1).broadcast_to([P, 1])
                for q in range(PARTS):
                    sp.dma_start(k.X[:, per * q:per * (q + 1), :],
                                 x[per * q:per * (q + 1)].rearrange("b l n -> l b n")).then_inc(x_in[q], 16)
                    if q == 1:
                        mix.load(sp, "wl", mix.a)
                    if q == 0:
                        sp.dma_start(k.adj[:], adj).then_inc(small_in, 16)
                        sp.dma_start(k.bias0[:], column(b0)).then_inc(small_in, 16)
                        sp.dma_start(k.bias3[:], column(b3)).then_inc(small_in, 16)
                        sp.dma_start(k.s(GATE), single(gate)).then_inc(small_in, 16)
                        sp.dma_start(k.s(SIG), single(logsig)).then_inc(small_in, 16)
                early.store(sp)
                early.all_stored(sp)

            @block.gpsimd
            def _(pool):
                pool.memset(unit_col[:], 0.0).then_inc(zeroed, 1)
                pool.wait_ge(zeroed, 1)
                pool.memset(unit_col[:, RUN - 1:RUN], 1.0).then_inc(consts, 1)
                pool.memset(k.ones[:], 1.0).then_inc(consts, 1)
                pool.memset(k.ident[:], 0.0).then_inc(zeroed, 1)
                pool.memset(k.s(HALF), -0.5).then_inc(consts, 1)
                pool.memset(k.s(PLUS_HALF), 0.5).then_inc(consts, 1)
                pool.wait_ge(zeroed, 2)
                pool.affine_select(out=k.ident[:], in_=k.ident[:], compare_op=ALU.not_equal, fill=1.0, base=0,
                                   pattern=[[-1, P]], channel_multiplier=1).then_inc(consts, 1)
                pool.wait_ge(mx, 1)
                pool.partition_all_reduce(k.s(M_ADJ), k.s(M_ADJ), P, ABSMAX).then_inc(mxall, 1)
                mix.lang.scales(pool)
                mix.lang.lo_part(pool, mix.a)

            @block.scalar
            def _(act):
                act.wait_ge(small_in, 80)
                nc.scalar.activation(k.s(SIG), k.s(SIG), ACT.Exp, scale=-2.0)
                nc.scalar.activation(k.s(GATE), k.s(GATE), ACT.Exp, scale=-1.0)
                for q in range(PARTS):
                    if q == 6:
                        mix.lang.square(act, mix.a)
                    if q == 8:
                        mix.lang.norm_out(act)
                    if q == PARTS // 2 + 2:
                        early.take_root(act)
                    act.wait_ge(x_in[q], 16)
                    for i in range(per):
                        b = q * per + i
                        need(act, sums, b - RS + 1)
                        nc.scalar.activation(sq[:, b % RS, :], k.X[:, b, :], ACT.Square).then_inc(sq_ready, 1)

            @block.tensor
            def _(pe):
                pe.wait_ge(consts, 5)
                for b in range(B):
                    j, i = b // RUN, b % RUN
                    if b == B // 2:
                        pe.wait_ge(early.clamped, 1)
                    pe.wait_ge(sq_ready, b + 1)
                    nc.tensor.matmul(rows_bank[j * BAND:(j + 1) * BAND, :], unit_col[:, RUN - 1 - i:RUN - 1 - i + BAND],
                                     sq[:, b % RS, :], start=(i == 0), stop=(i == RUN - 1),
                                     skip_group_check=True).then_inc(sums, 1)
                    if b == 7:
                        pe.wait_ge(mix.win["wl"], 16)
                    if b in (7, 11, 15, 19):
                        mix.lang.multiply((b - 7) // 4, mix.a, mix.a)
                    if b == 27:
                        mix.lang.sum_squares(pe)

            @block.vector
            def _(dve):
                ch = Chain(dve, chain)
                dve.wait_ge(small_in, 80)
                nc.vector.tensor_reduce(k.s(M_ADJ), k.adj[:], axis=AX_X, op=ALU.max,
                                        apply_absolute_value=True).then_inc(mx, 1)
                dve.wait_ge(mxall, 1)
                ch(nc.vector.tensor_scalar(k.s(M_ADJ), k.s(M_ADJ), 1e-18, 1.0 / S_W, ALU.max, ALU.mult))
                ch(nc.vector.reciprocal(k.s(W_ADJ), k.s(M_ADJ)))
                dve.wait_ge(sums, B // 2)
                early.clamp(dve)
                early.invert(dve)
                early.refine(dve)
                mix.lang.scale_and_hi_on_vector(dve, mix.a)


def similarity(k, ctx_out, rows_bank, scale, banded, mix, ops):
    nc = k.nc
    if mix:
        mix.arrive("wg", "wo", "wv")
    pair = [k.ps(ctx_out, f"pair{i}") for i in range(C)]
    diag = k.ps(ctx_out, "diag")
    R = 4
    gmax_all = k.sem("gmax_all")
    late = ColumnScales(k, rows_bank, scale, banded, False, scratch_tiles(ops))
    rn_in = [k.sem(f"rn_in{r}") for r in range(R)]
    unit_ready, hi_ready, lo_ready, gram_done = k.sem("unit_ready"), k.sem("hi_ready"), k.sem("lo_ready"), k.sem("gram_done")
    with ExitStack() as ctx:
        rnb, unit = ops.sim, ops.kept
        hi = k.sb(ctx, "unit_hi", [P, R, N], F16)
        lo = k.sb(ctx, "unit_lo", [P, R, N], F16)
        with nc.Block() as block:
            @block.sync
            def _(sp):
                def load(b, r):
                    if not isinstance(b, int) or b >= R:
                        settle(sp, unit_ready, b - R + 1, k.idle["sp"])
                    row = b if banded else B - 1 - b
                    sp.dma_start(rnb[:, r, :], k.rn_rows[row].partition_broadcast(P)).then_inc(rn_in[r], 16)
                for r in range(R):
                    load(r, r)
                if mix:
                    mix.load(sp, "wg", mix.b)
                    mix.load(sp, "wo", mix.a)
                with strided(sp, R, B // 2, R) as base:
                    for r in range(R):
                        load(base + r, r)
                late.all_stored(sp)
                with strided(sp, B // 2, B, R) as base:
                    for r in range(R):
                        load(base + r, r)

            @block.gpsimd
            def _(pool):
                late.store(pool)
                pool.wait_ge(late.top, 1)
                pool.partition_all_reduce(k.s(NSQ_MAX), k.s(NSQ_MAX), P, RMAX).then_inc(gmax_all, 1)

            @block.tensor
            def _(pe):
                def gram(b, r, first, final):
                    pe.wait_ge(lo_ready, b + 1)
                    pe.wait_ge(hi_ready, b + 1)
                    for i in range(C):
                        stat = hi[:, r, i * P:(i + 1) * P]
                        nc.tensor.matmul(pair[i][:], stat, lo[:, r, :], start=first, stop=False, skip_group_check=True)
                        if i < C - 1:
                            nc.tensor.matmul(pair[i][:, (i + 1) * P:], stat, hi[:, r, (i + 1) * P:], start=False,
                                             stop=final, skip_group_check=True)
                        last = nc.tensor.matmul(diag[:, i * P:(i + 1) * P], stat, stat, start=(first and i == 0),
                                                stop=final, skip_group_check=True)
                    last.then_inc(gram_done, 1)
                for r in range(R):
                    gram(r, r, r == 0, False)
                with strided(pe, R, B - R, R) as base:
                    for r in range(R):
                        gram(base + r, r, False, False)
                for r in range(R):
                    gram(B - R + r, r, False, r == R - 1)

            @block.vector
            def _(dve):
                def units(base, start):
                    for r in range(R):
                        b = base + r
                        dve.wait_ge(rn_in[r], (b // R + 1) * 16 if isinstance(b, int) else (base // R + 1) * 16)
                        if not start:
                            dve.wait_ge(hi_ready, b - R + 1)
                            dve.wait_ge(lo_ready, b - R + 1)
                        nc.vector.tensor_tensor(unit[:, r, :], k.X[:, b, :], rnb[:, r, :], ALU.mult).then_inc(unit_ready, 1)
                    for r in range(R):
                        b = base + r
                        dve.wait_ge(hi_ready, b + 1)
                        if not start:
                            dve.wait_ge(gram_done, b - R + 1)
                        nc.vector.tensor_tensor(lo[:, r, :], unit[:, r, :], hi[:, r, :], ALU.subtract).then_inc(lo_ready, 1)
                units(0, True)
                late.clamp(dve)
                units(R, False)
                late.invert(dve)
                units(2 * R, False)
                late.refine(dve)
                with strided(dve, 3 * R, B, R) as base:
                    units(base, False)

            @block.scalar
            def _(act):
                def split(b, r, start):
                    act.wait_ge(unit_ready, b + 1)
                    if not start:
                        act.wait_ge(gram_done, b - R + 1)
                    nc.scalar.activation(hi[:, r, :], unit[:, r, :], ACT.Copy).then_inc(hi_ready, 1)
                for r in range(R):
                    split(r, r, True)
                late.take_root(act)
                with strided(act, R, B, R) as base:
                    for r in range(R):
                        split(base + r, r, False)
    return pair, diag


def neighbours(k, pair, diag, spare, ops, mix):
    nc = k.nc
    ranks_set, copied, tr, simsum, dsum, masked, rounds, a_ready, top_r, ch_s = (k.sem(n) for n in (
        "ranks_set", "copied", "transposed", "sim_sum", "diag_added", "masked", "rounds", "a_ready", "top_ready", "chain"))
    SIM = 1.0 / (S_RN * S_RN * B)
    st, sd_r, search, cnt_b, bad_in, bad_all, pick = (k.sem("stats"), k.sem("deviation"), k.sem("search"), k.sem("counts_b"),
        k.sem("worst_row"), k.sem("worst_of_all"), k.sem("pick"))
    STEPS = 11
    HALF_C = C // 2
    with ExitStack() as ctx:
        raw, sim, wa_h, wa_l = ops.kept, ops.sim, ops.wa_h, ops.wa_l
        work = k.sb(ctx, "work", [P, C, N])
        m8, sel = (k.sb(ctx, n, [P, C, 8]) for n in ("m8", "sel"))
        ranks = k.sb(ctx, "ranks", [P, 8])
        bns = k.sb(ctx, "bns", [P, C, 6])
        mvs = k.sb(ctx, "mvs", [P, C, 2])
        thr, delta, cnt, left = (k.sb(ctx, n, [P, C]) for n in ("threshold", "delta", "count", "left"))
        move = k.sb(ctx, "move", [P, 2, C])
        worst = k.sb(ctx, "worst", [P, 1])
        flag = k.sb(ctx, "flag", [P, 1], mybir.dt.int32)
        junk = k.sb(ctx, "junk", [P, N])
        tp = [ops.degrees, k.ps(ctx, "tp")]
        dr = tp[0]
        if mix:
            mix.during_topk(pair, diag, spare, *tp)
        with nc.Block() as block:
            @block.sync
            def _(sp):
                if mix:
                    sp.wait_ge(mix.grav.prod, C)
                    mix.load(sp, "wv", mix.b)
                    sp.wait_ge(mix.win["wv"], 16)

            @block.scalar
            def _(act):
                for i in range(C // 2):
                    nc.scalar.activation(raw[:, i, :], pair[i][:], ACT.Copy, scale=SIM).then_inc(copied, 1)
                if mix:
                    for c in range(C):
                        act.wait_ge(mix.woT_d, c + 1)
                        if c == 0:
                            act.wait_ge(mix.woT_d, C)
                        nc.scalar.activation(mix.a[:, c, :], pair[c][:], ACT.Copy).then_inc(mix.woT_c, 1)

                def count_b():
                    for i in range(HALF_C, C):
                        nc.scalar.activation(raw[:, i, :], work[:, i, :], ACT.Sign, scale=-1.0, bias=thr[:, i:i + 1],
                                             accum_out=cnt[:, i:i + 1]).then_inc(cnt_b, 1)
                act.wait_ge(search, 1)
                count_b()
                with act.Fori(1, SEARCH) as it:
                    act.wait_ge(search, it * STEPS)
                    count_b()
                if mix:
                    mix.grav.square(act, over(junk[:], C))
                    mix.grav.norm_out(act)
                    mix.grav.hi_direct(act)
                    mix.m.square(act, mix.b)
                    mix.m.norm_out(act)
                    mix.m.scale_and_hi(act, mix.b)

            @block.tensor
            def _(pe):
                pe.wait_ge(copied, C)
                for i in range(C):
                    need(pe, simsum, i - 1)
                    for j in range(C):
                        last = nc.tensor.transpose(tp[i % 2][:, j * P:(j + 1) * P], raw[:, j, i * P:(i + 1) * P], k.ident[:])
                    last.then_inc(tr, 1)
                if mix:
                    pe.wait_ge(mix.win["wo"], 16)
                    for c in range(C):
                        for r in range(C):
                            last = nc.tensor.transpose(pair[c][:, r * P:(r + 1) * P], mix.a[:, r, c * P:(c + 1) * P],
                                                       k.ident[:])
                        last.then_inc(mix.woT_d, 1)
                    pe.wait_ge(mix.win["wg"], 16)
                    pe.wait_ge(dsum, C)
                    for d in range(C):
                        mix.grav.multiply(d, mix.b, mix.b)
                    pe.wait_ge(mix.woT_c, C)
                    pe.wait_ge(mix.win["wv"], 16)
                    for d in range(C):
                        if d == C - 1:
                            mix.grav.sum_squares(pe)
                        mix.m.multiply(d, mix.b, mix.a)
                    mix.m.sum_squares(pe)
                    pe.wait_ge(mix.m.q_in, 1)
                for i in range(C):
                    pe.wait_ge(a_ready, i + 1)
                    nc.tensor.matmul(dr[:], k.ones[:], raw[:, i, :], start=(i == 0), stop=(i == C - 1))

            @block.gpsimd
            def _(pool):
                for j in range(8):
                    pool.memset(ranks[:, j:j + 1], float(j)).then_inc(ranks_set, 1)
                for i in range(C):
                    pool.wait_ge(dsum, i + 1)
                    where = dict(compare_op=ALU.not_equal, base=i * P, pattern=[[-1, N]], channel_multiplier=1)
                    pool.affine_select(out=sim[:, i, :], in_=sim[:, i, :], fill=0.0, **where).then_inc(masked, 1)
                    pool.wait_ge(masked, 2 * i + 1)
                    pool.affine_select(out=work[:, i, :], in_=sim[:, i, :], fill=SENT, **where).then_inc(masked, 1)
                pool.wait_ge(top_r, 1)
                pool.tensor_tensor(k.s(TMP_A), k.s(TMP_A), k.s(HALF), ALU.pow).then_inc(sd_r, 1)
                pool.wait_ge(st, 2 * C)
                pool.tensor_tensor(delta[:], mvs[:, :, 1], k.s(PLUS_HALF).broadcast_to([P, C]), ALU.pow).then_inc(sd_r, 1)
                pool.wait_ge(bad_in, 1)
                pool.partition_all_reduce(worst[:], worst[:], P, RMAX).then_inc(bad_all, 1)
                if mix:
                    mix.grav.scales(pool)
                    mix.m.scales(pool)
                    mix.m.lo_part(pool, mix.b)

            @block.vector
            def _(dve):
                ch = Chain(dve, ch_s)
                for i in range(C // 2, C):
                    nc.vector.tensor_scalar(raw[:, i, :], pair[i][:], SIM, None, ALU.mult).then_inc(copied, 1)
                for i in range(C):
                    if i == 0:
                        dve.wait_ge(copied, C)
                    dve.wait_ge(tr, i + 1)
                    nc.vector.tensor_tensor(sim[:, i, :], raw[:, i, :], tp[i % 2][:], ALU.add).then_inc(simsum, 1)
                    dve.wait_ge(simsum, i + 1)
                    blk = slice(i * P, (i + 1) * P)
                    nc.vector.scalar_tensor_tensor(sim[:, i, blk], diag[:, blk], SIM, sim[:, i, blk], ALU.mult,
                                                   ALU.add).then_inc(dsum, 1)
                ch(nc.vector.tensor_scalar(wa_h[:], k.adj[:], k.s(W_ADJ), None, ALU.mult))
                ch(nc.vector.scalar_tensor_tensor(wa_l[:], k.adj[:], k.s(W_ADJ), wa_h[:], ALU.mult, ALU.subtract))
                nc.vector.tensor_scalar(k.s(TMP_A), k.s(NSQ_MAX), 1e-30, None, ALU.max).then_inc(top_r, 1)
                for i in range(C):
                    dve.wait_ge(masked, 2 * i + 1)
                    nc.vector.bn_stats(bns[:, i, :], sim[:, i, :]).then_inc(st, 1)
                for i in range(C):
                    dve.wait_ge(st, i + 1)
                    nc.vector.bn_aggr(mvs[:, i, :], bns[:, i, :]).then_inc(st, 1)
                dve.wait_ge(sd_r, 2)
                ch(nc.vector.tensor_scalar(k.s(SX), k.s(TMP_A), S_COL, None, ALU.mult))
                ch(nc.vector.scalar_tensor_tensor(thr[:], delta[:], 0.5, mvs[:, :, 0], ALU.mult, ALU.add))
                nc.vector.tensor_scalar(delta[:], delta[:], 0.25, None, ALU.mult).then_inc(search, 1)

                dve.wait_ge(masked, 2 * C)
                dve.wait_ge(ranks_set, 8)

                def at_or_above(i):
                    return nc.vector.tensor_scalar(raw[:, i, :], work[:, i, :], thr[:, i:i + 1], None, ALU.is_ge, ALU.add,
                                                   accum_out=cnt[:, i:i + 1])

                def search_step(it):
                    base = it * STEPS + 1
                    dve.wait_ge(search, base)
                    for i in range(HALF_C):
                        at_or_above(i).then_inc(search, 1)
                    def moves(part, bounds):
                        for m, (bound, op) in enumerate(bounds):
                            nc.vector.scalar_tensor_tensor(move[:, m, part], cnt[:, part], bound, delta[:, part], op,
                                                           ALU.mult).then_inc(search, 1)
                    a, b = slice(0, HALF_C), slice(HALF_C, C)
                    dve.wait_ge(cnt_b, (it + 1) * HALF_C)
                    moves(b, ((N - 2 * (TOPK + 0.5), ALU.is_lt), (N - 2 * (TOPK - 8.5), ALU.is_gt)))
                    dve.wait_ge(search, base + HALF_C)
                    moves(a, ((TOPK + 0.5, ALU.is_gt), (TOPK - 8.5, ALU.is_lt)))
                    dve.wait_ge(search, base + HALF_C + 2)
                    nc.vector.tensor_tensor(thr[:, b], thr[:, b], move[:, 0, b], ALU.add).then_inc(search, 1)
                    dve.wait_ge(search, base + HALF_C + 4)
                    nc.vector.tensor_tensor(thr[:, a], thr[:, a], move[:, 0, a], ALU.add).then_inc(search, 1)
                    nc.vector.tensor_scalar(delta[:], delta[:], 0.5, None, ALU.mult).then_inc(search, 1)
                    dve.wait_ge(search, base + HALF_C + 5)
                    nc.vector.tensor_tensor(thr[:, b], thr[:, b], move[:, 1, b], ALU.subtract).then_inc(search, 1)
                    dve.wait_ge(search, base + HALF_C + 6)
                    nc.vector.tensor_tensor(thr[:, a], thr[:, a], move[:, 1, a], ALU.subtract).then_inc(search, 1)
                with dve.Fori(0, SEARCH) as it:
                    search_step(it)
                dve.wait_ge(search, SEARCH * STEPS + 1)
                dve.wait_ge(cnt_b, SEARCH * HALF_C)
                for i in range(C):
                    at_or_above(i).then_inc(pick, 1)
                dve.wait_ge(pick, C)
                ch(nc.vector.tensor_scalar(left[:], cnt[:], -1.0, float(TOPK - 4), ALU.mult, ALU.add))
                nc.vector.tensor_reduce(worst[:], left[:], axis=AX_X, op=ALU.max,
                                        apply_absolute_value=True).then_inc(bad_in, 1)
                ch(nc.vector.tensor_scalar(left[:], left[:], 4.0, None, ALU.add))
                for i in range(C):
                    nc.vector.scalar_tensor_tensor(raw[:, i, :], raw[:, i, :], SENT, work[:, i, :], ALU.mult,
                                                   ALU.add).then_inc(pick, 1)
                dve.wait_ge(bad_all, 1)
                ch(nc.vector.tensor_scalar(flag[:], worst[:], 4.5, None, ALU.is_gt))
                dve.wait_ge(pick, 2 * C)
                outside = dve.value_load(flag[0:1, 0:1], min_val=0, max_val=1)
                with dve.If(outside > 0):
                    def round_of_eight(t):
                        for i in range(C):
                            if not (isinstance(t, int) and t == 0):
                                settle(dve, rounds, (t - 1) * 2 * C + C + i + 1, k.idle["dve"])
                            nc.vector.max(m8[:, i, :], work[:, i, :]).then_inc(rounds, 1)
                        for i in range(C):
                            settle(dve, rounds, t * 2 * C + i + 1, k.idle["dve"])
                            nc.vector.match_replace(work[:, i, :], m8[:, i, :], work[:, i, :], SENT).then_inc(rounds, 1)
                    round_of_eight(0)
                    with dve.Fori(1, ROUNDS) as t:
                        round_of_eight(t)
                    dve.wait_ge(rounds, ROUNDS * 2 * C)
                    nc.vector.memset(left[:], 1.0).then_inc(rounds, 1)
                    for i in range(C):
                        nc.vector.tensor_copy(raw[:, i, :], work[:, i, :]).then_inc(rounds, 1)
                    dve.wait_ge(rounds, ROUNDS * 2 * C + C + 1)
                for i in range(C):
                    nc.vector.max(m8[:, i, :], raw[:, i, :]).then_inc(pick, 1)
                ch(nc.vector.tensor_tensor(sel[:], over(ranks[:], C), spread(left[:], 8), ALU.is_ge))
                dve.wait_ge(pick, 3 * C)
                ch(nc.vector.scalar_tensor_tensor(m8[:], sel[:], SENT, m8[:], ALU.mult, ALU.add))
                for i in range(C):
                    nc.vector.match_replace(raw[:, i, :], m8[:, i, :], raw[:, i, :], SENT).then_inc(pick, 1)
                for i in range(C):
                    dve.wait_ge(pick, 3 * C + i + 1)
                    nc.vector.scalar_tensor_tensor(raw[:, i, :], raw[:, i, :], SENT, sim[:, i, :], ALU.is_equal,
                                                   ALU.mult).then_inc(a_ready, 1)
                if mix:
                    mix.grav.lo_direct(dve)


def propagate(k, ops, bias, b1, out):
    nc = k.nc
    second = b1 is not None
    (xh_r, xl_r, xw_d, wh_r, wl_r, o_d, t_r, add_r, st_r, ag_r, rs_r, nm_r, ln_r, yh_r, yl_r, m_d, pb_r, add2_r, st2_r,
     ag2_r, rs2_r, nm2_r, ln2_r) = (k.sem(n) for n in (
         "x_hi", "x_lo", "xw_done", "xw_hi", "xw_lo", "out_done", "out_biased", "added", "stats", "moments", "rstd",
         "shift", "normed", "y_hi", "y_lo", "mix_done", "y_biased", "added2", "stats2", "moments2", "rstd2", "shift2",
         "normed2"))
    b1_in, w2_r, ch_s = k.sem("b1_in"), k.sem("w2_ready"), k.sem("chain")
    deg_c, deg_pw, dd_ready, deg_b, an_max, an_all, an_hi, an_lo = (k.sem(n) for n in (
        "degree_clamped", "degree_pow", "diag_ready", "row_factors", "an_max", "an_scale", "an_hi", "an_lo"))
    an_h, an_l, wa_h, wa_l, kept, sim, dr = ops.an_h, ops.an_l, ops.wa_h, ops.wa_l, ops.kept, ops.sim, ops.degrees
    stored = [k.sem(f"stored{i}") for i in range(4)]
    with ExitStack() as ctx:
        xh, xl = (k.sb(ctx, n, [P, 2, N], F16) for n in ("xh", "xl"))
        wh, wl = (k.sb(ctx, n, [P, 2, N], F16) for n in ("xwh", "xwl"))
        t = k.sb(ctx, "t", [P, 2, N])
        degc = k.sb(ctx, "degc", [P, 2, C])
        degr = k.sb(ctx, "degr", [P, N])
        mxp = k.sb(ctx, "mxp", [P, 1])
        bn = k.sb(ctx, "bn", [P, 2, 6])
        mv = k.sb(ctx, "mv", [P, 4, 2])
        rstd = k.sb(ctx, "rstd", [P, 4, 2])
        if second:
            yh, yl = (k.sb(ctx, n, [P, 2, N], F16) for n in ("yh", "yl"))
            w2 = k.sb(ctx, "w2", [P, P])
            w2h, w2l = (k.sb(ctx, n, [P, P], F16) for n in ("w2h", "w2l"))
            b1b = k.sb(ctx, "b1_bcast", [P, N])
            bn2 = k.sb(ctx, "bn2", [P, 2, 6])
            mv2 = k.sb(ctx, "mv2", [P, 4, 2])
            rstd2 = k.sb(ctx, "rstd2", [P, 4, 2])
            pm = [k.ps(ctx, f"pm{i}") for i in range(2)]
        px = [k.ps(ctx, f"px{i}") for i in range(2)]
        po = [k.ps(ctx, f"po{i}") for i in range(2)]
        depth = 10 if second else 7
        R = 4
        X = k.X
        with nc.Block() as block:
            @block.sync
            def _(sp):
                if second:
                    sp.dma_start(b1b[:], b1.partition_broadcast(P)).then_inc(b1_in, 16)
                    sp.wait_ge(b1_in, 16)
                else:
                    for r in range(4):
                        sp.wait_ge(ln_r, r + 1)
                        sp.dma_start(out[r], X[:, r, :]).then_inc(stored[r], 16)
                    with strided(sp, 4, B, 4) as base:
                        for r in range(4):
                            settle(sp, stored[r], base * 4, k.idle["sp"])
                            settle(sp, ln_r, base + r + 1, k.idle["sp"])
                            sp.dma_start(out[base + r], X[:, base + r, :]).then_inc(stored[r], 16)
                    for r in range(4):
                        sp.wait_ge(stored[r], 16 * B // 4)

            @block.scalar
            def _(act):
                def adjacency_hi():
                    act.wait_ge(an_all, 2)
                    for i in range(C):
                        nc.scalar.activation(an_h[:, i, :], sim[:, i, :], ACT.Copy, scale=k.s(SAN)).then_inc(an_hi, 1)

                def step(s):
                    if isinstance(s.i, int) and s.i == 3:
                        adjacency_hi()
                    if isinstance(s.i, int) and s.i == 4:
                        act.wait_ge(an_lo, C)
                    if s.live(0):
                        b, r = s.at(0), s.slot(0)
                        settle(act, xw_d, b - 1, k.idle["act"])
                        nc.scalar.activation(xh[:, r, :], X[:, b, :], ACT.Copy, scale=k.s(SX)).then_inc(xh_r, 1)
                    if s.live(2):
                        b, r = s.at(2), s.slot(2)
                        act.wait_ge(xw_d, b + 1)
                        need(act, o_d, b - 1)
                        nc.scalar.activation(wh[:, r, :], px[r][:], ACT.Copy, scale=S_EVAC).then_inc(wh_r, 1)
                    if s.live(4):
                        b, r = s.at(4), s.slot(4)
                        act.wait_ge(o_d, b + 1)
                        need(act, add_r, b - 1)
                        nc.scalar.activation(t[:, r, :], po[r][:], ACT.Identity, scale=k.s(F_B), bias=bias[:]).then_inc(t_r, 1)
                    if s.live(7):
                        b, r = s.at(7), s.slot(7, 4)
                        settle(act, nm_r, b + 1, k.idle["act"])
                        nc.scalar.activation(X[:, b, :], X[:, b, :], ACT.Identity, scale=rstd[:, r, 0:1],
                                             bias=rstd[:, r, 1:2]).then_inc(ln_r, 1)
                        if second:
                            act.wait_ge(ln_r, b + 1)
                            settle(act, m_d, b - 1, k.idle["act"])
                            nc.scalar.activation(yh[:, s.slot(7), :], X[:, b, :], ACT.Copy, scale=S_LN).then_inc(yh_r, 1)
                    if second and s.live(10):
                        b, r = s.at(10), s.slot(10, 4)
                        settle(act, nm2_r, b + 1, k.idle["act"])
                        nc.scalar.activation(X[:, b, :], X[:, b, :], ACT.Identity, scale=rstd2[:, r, 0:1],
                                             bias=rstd2[:, r, 1:2]).then_inc(ln2_r, 1)
                pipeline(act, B, depth, R, step)

            @block.vector
            def _(dve):
                ch = Chain(dve, ch_s)
                ch(nc.vector.tensor_tensor(grouped(degr[:]), grouped(dr[:]), over(k.ident[:], C), ALU.mult))
                ch(nc.vector.tensor_reduce(degc[:, 0, :], grouped(degr[:]), axis=AX_X, op=ALU.add))
                nc.vector.tensor_scalar(degc[:, 1, :], degc[:, 0, :], 1e-37, None, ALU.max).then_inc(deg_c, 1)
                if second:
                    ch(nc.vector.tensor_tensor(w2[:], k.adj[:], k.adj[:], ALU.mult))
                    ch(nc.vector.tensor_tensor(w2[:], w2[:], k.ident[:], ALU.add))
                    ch(nc.vector.tensor_scalar(k.s(TMP_A), k.s(M_ADJ), k.s(M_ADJ), S_W * S_W, ALU.mult, ALU.mult))
                    ch(nc.vector.tensor_scalar(k.s(TMP_B), k.s(TMP_A), 1.0, 1.0 / S_W, ALU.add, ALU.mult))
                    ch(nc.vector.reciprocal(k.s(W_SQ), k.s(TMP_B)))
                    ch(nc.vector.tensor_scalar(k.s(F_L1), k.s(TMP_B), 1.0 / S_LN, None, ALU.mult))
                    ch(nc.vector.tensor_scalar(w2h[:], w2[:], k.s(W_SQ), None, ALU.mult))
                    nc.vector.scalar_tensor_tensor(w2l[:], w2[:], k.s(W_SQ), w2h[:], ALU.mult,
                                                   ALU.subtract).then_inc(w2_r, 1)

                idle = k.idle["dve"]

                def row_factors():
                    dve.wait_ge(deg_pw, 1)
                    ch(nc.vector.scalar_tensor_tensor(degc[:, 0, :], degc[:, 0, :], 0.0, degc[:, 1, :], ALU.is_gt,
                                                      ALU.mult))
                    nc.vector.tensor_tensor(grouped(degr[:]), over(k.ident[:], C), spread(degc[:, 0, :], P),
                                            ALU.mult).then_inc(dd_ready, 1)

                def normalise():
                    dve.wait_ge(deg_b, 1)
                    for i in range(C):
                        ch(nc.vector.scalar_tensor_tensor(sim[:, i, :], kept[:, i, :], degc[:, 0, i:i + 1], dr[:],
                                                          ALU.mult, ALU.mult))
                    nc.vector.tensor_reduce(mxp[:], sim[:], axis=mybir.AxisListType.XY, op=ALU.max,
                                            apply_absolute_value=True).then_inc(an_max, 1)
                    ch(nc.vector.tensor_scalar(k.s(TMP_A), k.s(SX), k.s(W_ADJ), S_EVAC, ALU.mult, ALU.mult))
                    ch(nc.vector.reciprocal(k.s(TMP_C), k.s(TMP_A)))
                    dve.wait_ge(an_all, 1)
                    ch(nc.vector.tensor_scalar(k.s(TMP_B), mxp[:], 1e-18, 1.0 / S_AN, ALU.max, ALU.mult))
                    nc.vector.reciprocal(k.s(SAN), k.s(TMP_B)).then_inc(an_all, 1)
                    ch(nc.vector.tensor_scalar(k.s(F_B), k.s(TMP_C), k.s(TMP_B), None, ALU.mult))

                def adjacency_lo():
                    for i in range(C):
                        dve.wait_ge(an_hi, i + 1)
                        nc.vector.scalar_tensor_tensor(an_l[:, i, :], sim[:, i, :], k.s(SAN), an_h[:, i, :], ALU.mult,
                                                       ALU.subtract).then_inc(an_lo, 1)
                    if second:
                        dve.wait_ge(b1_in, 16)

                def step(s):
                    for position, stage in enumerate((None, row_factors, normalise, adjacency_lo)):
                        if stage and isinstance(s.i, int) and s.i == position:
                            stage()
                    if second and s.live(9):
                        b, r = s.at(9), s.slot(9)
                        dve.wait_ge(m_d, b + 1)
                        nc.vector.scalar_tensor_tensor(X[:, b, :], pm[r][:], k.s(F_L1), b1b[:], ALU.mult,
                                                       ALU.add).then_inc(add2_r, 1)
                    if s.live(6):
                        b, r = s.at(6), s.slot(6)
                        settle(dve, add_r, b + 1, idle)
                        nc.vector.bn_stats(bn[:, r, :], X[:, b, :]).then_inc(st_r, 1)
                    if second and s.live(9):
                        b, r = s.at(9), s.slot(9)
                        settle(dve, add2_r, b + 1, idle)
                        nc.vector.bn_stats(bn2[:, r, :], X[:, b, :]).then_inc(st2_r, 1)
                    if s.live(6):
                        b, r, q = s.at(6), s.slot(6), s.slot(6, 4)
                        settle(dve, nm_r, b - 3, idle)
                        settle(dve, st_r, b + 1, idle)
                        nc.vector.bn_aggr(mv[:, q, :], bn[:, r, :]).then_inc(ag_r, 1)
                    if s.live(0):
                        b, r = s.at(0), s.slot(0)
                        dve.wait_ge(xh_r, b + 1)
                        need(dve, xw_d, b - 1)
                        nc.vector.scalar_tensor_tensor(xl[:, r, :], X[:, b, :], k.s(SX), xh[:, r, :], ALU.mult,
                                                       ALU.subtract).then_inc(xl_r, 1)
                    if second and s.live(9):
                        b, r, q = s.at(9), s.slot(9), s.slot(9, 4)
                        settle(dve, nm2_r, b - 3, idle)
                        settle(dve, st2_r, b + 1, idle)
                        nc.vector.bn_aggr(mv2[:, q, :], bn2[:, r, :]).then_inc(ag2_r, 1)
                    if s.live(2):
                        b, r = s.at(2), s.slot(2)
                        dve.wait_ge(wh_r, b + 1)
                        need(dve, o_d, b - 1)
                        nc.vector.scalar_tensor_tensor(wl[:, r, :], px[r][:], S_EVAC, wh[:, r, :], ALU.mult,
                                                       ALU.subtract).then_inc(wl_r, 1)
                    if second and s.live(7):
                        b, r = s.at(7), s.slot(7)
                        dve.wait_ge(yh_r, b + 1)
                        need(dve, m_d, b - 1)
                        nc.vector.scalar_tensor_tensor(yl[:, r, :], X[:, b, :], S_LN, yh[:, r, :], ALU.mult,
                                                       ALU.subtract).then_inc(yl_r, 1)
                pipeline(dve, B, depth, R, step)

            @block.gpsimd
            def _(pool):
                def moments(b, q, mvt, rst, aggr, rsem, nsem, lns):
                    need(pool, lns, b - 3)
                    settle(pool, aggr, b + 1, k.idle["pool"])
                    pool.tensor_scalar(rst[:, q, 1:2], mvt[:, q, 1:2], LN_EPS, None, ALU.add).then_inc(rsem, 1)
                    pool.wait_ge(rsem, 2 * b + 1)
                    pool.tensor_tensor(rst[:, q, 0:1], rst[:, q, 1:2], k.s(HALF), ALU.pow).then_inc(rsem, 1)
                    settle(pool, rsem, 2 * b + 2, k.idle["pool"])
                    pool.tensor_scalar(rst[:, q, 1:2], mvt[:, q, 0:1], rst[:, q, 0:1], -1.0, ALU.mult,
                                       ALU.mult).then_inc(nsem, 1)

                pool.wait_ge(deg_c, 1)
                pool.tensor_tensor(degc[:, 1, :], degc[:, 1, :], k.s(HALF).broadcast_to([P, C]), ALU.pow).then_inc(deg_pw, 1)
                pool.wait_ge(an_max, 1)
                pool.partition_all_reduce(mxp[:], mxp[:], P, ABSMAX).then_inc(an_all, 1)

                def step(s):
                    if s.live(5):
                        b, r = s.at(5), s.slot(5)
                        settle(pool, t_r, b + 1, k.idle["pool"])
                        pool.tensor_tensor(X[:, b, :], X[:, b, :], t[:, r, :], ALU.add).then_inc(add_r, 1)
                    if s.live(6):
                        moments(s.at(6), s.slot(6, 4), mv, rstd, ag_r, rs_r, nm_r, ln_r)
                    if second and s.live(9):
                        moments(s.at(9), s.slot(9, 4), mv2, rstd2, ag2_r, rs2_r, nm2_r, ln2_r)
                pipeline(pool, B, depth, R, step)

            @block.tensor
            def _(pe):
                def step(s):
                    if isinstance(s.i, int) and s.i == 2:
                        pe.wait_ge(dd_ready, 1)
                        nc.tensor.matmul(dr[:], k.ones[:], degr[:], start=True, stop=True).then_inc(deg_b, 1)
                    if isinstance(s.i, int) and s.i == 3:
                        pe.wait_ge(an_lo, C)
                        if second:
                            pe.wait_ge(w2_r, 1)
                    if s.live(1):
                        b, r = s.at(1), s.slot(1)
                        pe.wait_ge(xl_r, b + 1)
                        need(pe, wl_r, b - 1)
                        for c in range(C):
                            cs = slice(c * P, (c + 1) * P)
                            nc.tensor.matmul(px[r][:, cs], xh[:, r, cs], wa_h[:], start=True, stop=False)
                            nc.tensor.matmul(px[r][:, cs], xh[:, r, cs], wa_l[:], start=False, stop=False)
                            last = nc.tensor.matmul(px[r][:, cs], xl[:, r, cs], wa_h[:], start=False, stop=True)
                        last.then_inc(xw_d, 1)
                    if s.live(3):
                        b, r = s.at(3), s.slot(3)
                        pe.wait_ge(wl_r, b + 1)
                        need(pe, t_r, b - 1)
                        for c in range(C):
                            cs = slice(c * P, (c + 1) * P)
                            nc.tensor.matmul(po[r][:], wh[:, r, cs], an_h[:, c, :], start=(c == 0), stop=False)
                            nc.tensor.matmul(po[r][:], wh[:, r, cs], an_l[:, c, :], start=False, stop=False)
                            last = nc.tensor.matmul(po[r][:], wl[:, r, cs], an_h[:, c, :], start=False, stop=(c == C - 1))
                        last.then_inc(o_d, 1)
                    if second and s.live(8):
                        b, r = s.at(8), s.slot(8)
                        pe.wait_ge(yl_r, b + 1)
                        need(pe, add2_r, b - 1)
                        nc.tensor.matmul(pm[r][:], w2h[:], yh[:, r, :], start=True, stop=False)
                        nc.tensor.matmul(pm[r][:], w2h[:], yl[:, r, :], start=False, stop=False)
                        nc.tensor.matmul(pm[r][:], w2l[:], yh[:, r, :], start=False, stop=True).then_inc(m_d, 1)
                pipeline(pe, B, depth, R, step)


class GraphOperands:

    def __init__(self, k, ctx):
        self.an_h, self.an_l = (k.sb(ctx, n, [P, C, N], F16) for n in ("an_h", "an_l"))
        self.wa_h, self.wa_l = (k.sb(ctx, n, [P, P], F16) for n in ("wa_h", "wa_l"))
        self.kept, self.sim = (k.sb(ctx, n, [P, C, N]) for n in ("kept", "sim"))
        self.degrees = k.ps(ctx, "degrees")


def scratch_tiles(ops):
    h, l = (t[:].rearrange("p c n -> p (c n)").bitcast(F32) for t in (ops.an_h, ops.an_l))
    return h[:, 0:N], h[:, N:2 * N], l[:, 0:N]


def select_neighbours(k, rows_bank, scale, banded, mix, ops):
    with ExitStack() as banks:
        pair, diag = similarity(k, banks, rows_bank, scale, banded, mix, ops)
        neighbours(k, pair, diag, rows_bank, ops, mix)


def kernel_mix(k, w, rows_bank):
    nc, X, idle = k.nc, k.X, k.idle["dve"]
    DIAG, SMALL = 5, 15
    (xs_hi, xs_lo, t_d, xt_a, xt_v, tl_d, tl_h, tl_l, tg_d, tg_h, tg_l, gl_d, gg_d, tl_c, tg_c, diag_r, dd_r, bc_d, sum_r, mask_r, u_r, e_r,
     k_r, kt_d, kt_h, kt_l, v_d, v_h, v_l, o_d, o_u, bn_r, mv_r, rs_r, nm_r, ln_r, sq_r, sq_h, sq_l, ns_d, ksm, msk_r, consts,
     diag_pow, unit_ready, cleared) = (
        k.sem(n) for n in (
            "x_hi", "x_lo", "xT_done", "xT_copied_act", "xT_copied_dve", "tl_done", "tl_hi", "tl_lo", "tg_done", "tg_hi", "tg_lo", "T_l_done",
            "T_g_done", "T_l_copied", "T_g_shifted", "diag_chain", "diag_ready", "flipped", "G_l_used", "masked_l", "u_ready",
            "exp_ready", "k_ready", "kT_done", "kT_hi", "kT_lo", "v_done", "v_hi", "v_lo", "out_done",
            "out_added", "stats", "moments", "rstd", "shift", "normed", "sq_ready", "sq_hi", "sq_lo", "sums_done", "k_chain",
            "mask_ready", "constants", "length_pow", "unit_col_ready", "top_cleared"))
    with ExitStack() as ctx:
        xs = k.sb(ctx, "xs", [P, 2, G, N], F16)
        ident16 = k.sb(ctx, "ident16", [P, P], F16)
        xT = k.sb(ctx, "xT", [P, C, 2, N], F16)
        xT_h, xT_l = xT[:, :, 0, :], xT[:, :, 1, :]
        tl_hi, tl_lo, tg_hi, tg_lo, v_hi, v_lo = (
            k.sb(ctx, n, [P, C, N], F16) for n in ("tl_h", "tl_l", "tg_h", "tg_l", "v_h", "v_l"))
        kT_hi, kT_lo = (k.sb(ctx, n, [P, N], F16) for n in ("kT_h", "kT_l"))
        dd, gs, es = (k.sb(ctx, n, [P, N]) for n in ("dd", "gs", "es"))
        sq = k.sb(ctx, "sq", [P, N])
        sq_hi, sq_lo = (k.sb(ctx, n, [P, N], F16) for n in ("sq_hi", "sq_lo"))
        unit_col = k.sb(ctx, "unit_col", [P, B - 1 + P], F16)
        mask = k.sb(ctx, "mask", [P, P])
        rn = k.sb(ctx, "rnl", [P, G])
        hs = k.sb(ctx, "half_sq", [P, G])
        sm = k.sb(ctx, "small", [P, 4, G])
        bn = k.sb(ctx, "bn", [P, G, 6])
        mv = k.sb(ctx, "mv", [P, G, 2])
        rs = k.sb(ctx, "rs", [P, 2, G])
        work = [k.ps(ctx, f"work{i}") for i in range(4)]

        def square_tiles(b):
            if not isinstance(b, int) or b < B - G:
                return sq[:], sq_hi[:], sq_lo[:]
            j = b - (B - G)
            wide = (tl_hi, tg_hi)[j // 2][:].rearrange("p c n -> p (c n)").bitcast(F32)
            return wide[:, j % 2 * N:(j % 2 + 1) * N], tl_lo[:, j, :], tg_lo[:, j, :]

        def last_group(b):
            return isinstance(b, int) and b >= B - G
        pgl, pgg, pbc = (k.ps(ctx, n) for n in ("gram_l", "gram_g", "bcast"))
        tiles = xs[:].rearrange("p h g n -> p (h g n)").bitcast(F32)
        early = ColumnScales(k, rows_bank, S_SQ, False, True, [tiles[:, i * N:(i + 1) * N] for i in range(3)])
        pkt = pbc
        with nc.Block() as block:
            @block.sync
            def _(sp):
                early.store(sp)
                early.all_stored(sp)

            @block.tensor
            def _(pe):
                def transposes(g):
                    pe.wait_ge(xs_lo, (g + 1) * G)
                    for d in range(C):
                        need(pe, v_l, (g - 1) * G + d + 1)
                        bank = work[d][:].bitcast(F16)
                        for h in range(2):
                            for j in range(G):
                                last = nc.tensor.transpose(bank[:, h * N + j * P:h * N + (j + 1) * P],
                                                           xs[:, h, j, d * P:(d + 1) * P], ident16[:])
                        last.then_inc(t_d, 1)

                def project(g, w_h, w_l, free, done):
                    for e in range(C):
                        if free:
                            pe.wait_ge(free, g * C + e + 1)
                        elif e == 0:
                            pe.wait_ge(xt_a, (g + 1) * C // 2)
                            pe.wait_ge(xt_v, (g + 1) * C // 2)
                        es_ = slice(e * P, (e + 1) * P)
                        for d in range(e + 1):
                            nc.tensor.matmul(work[e][:], w_h[:, d, es_], xT_h[:, d, :], start=(d == 0), stop=False)
                            nc.tensor.matmul(work[e][:], w_h[:, d, es_], xT_l[:, d, :], start=False, stop=False)
                            last = nc.tensor.matmul(work[e][:], w_l[:, d, es_], xT_h[:, d, :], start=False,
                                                    stop=(d == e))
                        last.then_inc(done, 1)

                def gram(bank, t_h, t_l, done):
                    for j in range(G):
                        js = slice(j * P, (j + 1) * P)
                        for e in range(C):
                            nc.tensor.matmul(bank[:, js], t_h[:, e, js], xT_h[:, e, js], start=(e == 0), stop=False)
                            nc.tensor.matmul(bank[:, js], t_h[:, e, js], xT_l[:, e, js], start=False, stop=False)
                            last = nc.tensor.matmul(bank[:, js], t_l[:, e, js], xT_h[:, e, js], start=False,
                                                    stop=(e == C - 1))
                    last.then_inc(done, 1)

                def norm_sums(s, j):
                    g = s.at(2)
                    b = g * G + j
                    if isinstance(g, int) and g == NG - 1 and j == 0:
                        pe.wait_ge(early.clamped, 1)
                    first, final = (isinstance(b, int) and b == e for e in (0, B - 1))
                    pick = unit_col[:, bass.ds(b, P)]
                    pe.wait_ge(sq_l, b + 1)
                    _, hi, low = square_tiles(b)
                    nc.tensor.matmul(rows_bank[:], pick, hi, start=first, stop=False, skip_group_check=True)
                    nc.tensor.matmul(rows_bank[:], pick, low, start=False, stop=final,
                                     skip_group_check=True).then_inc(ns_d, 1)

                pe.wait_ge(unit_ready, 2)
                pe.wait_ge(msk_r, 3)

                def step(s):
                    if s.live(0):
                        transposes(s.at(0))
                    if s.live(1):
                        g = s.at(1)

                        def flip(bank, src):
                            for j in range(G):
                                js = slice(j * P, (j + 1) * P)
                                last = nc.tensor.transpose(bank[:, js], src[:, js], k.ident[:])
                            return last
                        pe.wait_ge(tl_c, g + 1)
                        pe.wait_ge(diag_r, g * DIAG + 1)
                        flip(pgl, gs)
                        need(pe, kt_l, g)
                        pe.wait_ge(dd_r, g + 1)
                        nc.tensor.matmul(pbc[:], k.ones[:], dd[:], start=True, stop=True).then_inc(bc_d, 1)
                        pe.wait_ge(tg_c, g + 1)
                        flip(pgg, es).then_inc(bc_d, 1)
                    if s.live(0):
                        project(s.at(0), w["wl_h"], w["wl_l"], None, tl_d)
                    if s.live(2):
                        norm_sums(s, 0)
                    if s.live(0):
                        project(s.at(0), w["wg_h"], w["wg_l"], tl_l, tg_d)
                    if s.live(1):
                        g = s.at(1)
                        pe.wait_ge(k_r, g + 1)
                        for j in range(G):
                            last = nc.tensor.transpose(pkt[:, j * P:(j + 1) * P], gs[:, j * P:(j + 1) * P], k.ident[:])
                        last.then_inc(kt_d, 1)
                    if s.live(2):
                        norm_sums(s, 1)
                    if s.live(0):
                        g = s.at(0)
                        pe.wait_ge(tl_l, (g + 1) * C)
                        gram(pgl, tl_hi, tl_lo, gl_d)
                        pe.wait_ge(tg_l, (g + 1) * C)
                        gram(pgg, tg_hi, tg_lo, gg_d)
                    if s.live(2):
                        norm_sums(s, 2)
                    if s.live(1):
                        g = s.at(1)
                        pe.wait_ge(kt_l, g + 1)
                        pe.wait_ge(v_l, (g + 1) * G)
                        for j in range(G):
                            js = slice(j * P, (j + 1) * P)
                            if not isinstance(s.i, int) or s.i < NG:
                                pe.wait_ge(tg_l, (g + 1) * C + j + 1)
                            nc.tensor.matmul(work[j][:], kT_hi[:, js], v_hi[:, j, :], start=True, stop=False)
                            nc.tensor.matmul(work[j][:], kT_hi[:, js], v_lo[:, j, :], start=False, stop=False)
                            nc.tensor.matmul(work[j][:], kT_lo[:, js], v_hi[:, j, :], start=False,
                                             stop=True).then_inc(o_d, 1)
                    if s.live(0):
                        g = s.at(0)
                        for j in range(G):
                            js = slice(j * P, (j + 1) * P)
                            need(pe, o_u, (g - 1) * G + j + 1)
                            for d in range(C):
                                nc.tensor.matmul(work[j][:], xT_h[:, d, js], w["m_h"][:, d, :], start=(d == 0), stop=False)
                                nc.tensor.matmul(work[j][:], xT_h[:, d, js], w["m_l"][:, d, :], start=False, stop=False)
                                last = nc.tensor.matmul(work[j][:], xT_l[:, d, js], w["m_h"][:, d, :], start=False,
                                                        stop=(d == C - 1))
                            last.then_inc(v_d, 1)
                    if s.live(2):
                        norm_sums(s, 3)
                pipeline(pe, NG, 2, 1, step, ahead=1)

            @block.scalar
            def _(act):
                def square(g, j):
                    b = g * G + j
                    tile, hi, _ = square_tiles(b)
                    if last_group(b):
                        act.wait_ge(gg_d, NG)
                    else:
                        need(act, sq_l, b)
                    settle(act, ln_r, b + 1, k.idle["act"])
                    nc.scalar.activation(tile, X[:, b, :], ACT.Square, scale=S_SQ ** 0.5).then_inc(sq_r, 1)
                    if not last_group(b):
                        need(act, ns_d, b)
                    act.wait_ge(sq_r, b + 1)
                    nc.scalar.activation(hi, tile, ACT.Copy).then_inc(sq_h, 1)

                def step(s):
                    if isinstance(s.i, int) and s.i == NG + 1:
                        early.take_root(act)
                    if s.live(0):
                        g = s.at(0)
                        need(act, v_d, g * G)
                        for d in range(0, C, 2):
                            act.wait_ge(t_d, g * C + d + 1)
                            nc.scalar.activation(xT[:, d, :, :].rearrange("p h n -> p (h n)"), work[d][:].bitcast(F16),
                                                 ACT.Copy).then_inc(xt_a, 1)
                    if s.live(2):
                        g = s.at(2)
                        for j in range(G):
                            b = g * G + j
                            settle(act, nm_r, b + 1, k.idle["act"])
                            nc.scalar.activation(X[:, b, :], X[:, b, :], ACT.Identity, scale=rs[:, 0, j:j + 1],
                                                 bias=rs[:, 1, j:j + 1]).then_inc(ln_r, 1)
                        square(g, 0)
                    if s.live(1):
                        g = s.at(1)
                        act.wait_ge(u_r, g + 1)
                        nc.scalar.activation(es[:], es[:], ACT.Exp, scale=k.s(K_G)).then_inc(e_r, 1)
                    if s.live(0):
                        g = s.at(0)
                        need(act, gl_d, g)
                        for e in range(C):
                            act.wait_ge(tl_d, g * C + e + 1)
                            nc.scalar.activation(tl_hi[:, e, :], work[e][:], ACT.Copy, scale=S_EVAC).then_inc(tl_h, 1)
                    if s.live(2):
                        square(s.at(2), 1)
                    if s.live(0):
                        g = s.at(0)
                        need(act, gg_d, g)
                        for e in range(C):
                            act.wait_ge(tg_d, g * C + e + 1)
                            nc.scalar.activation(tg_hi[:, e, :], work[e][:], ACT.Copy, scale=S_EVAC).then_inc(tg_h, 1)
                    if s.live(1):
                        g = s.at(1)
                        act.wait_ge(kt_d, g + 1)
                        need(act, o_d, g * G)
                        nc.scalar.activation(kT_hi[:], pkt[:], ACT.Copy, scale=S_K).then_inc(kt_h, 1)
                    if s.live(2):
                        square(s.at(2), 2)
                    if s.live(0):
                        g = s.at(0)
                        act.wait_ge(gl_d, g + 1)
                        nc.scalar.activation(gs[:], pgl[:], ACT.Copy).then_inc(tl_c, 1)
                    if s.live(-1):
                        g = s.at(-1)
                        need(act, t_d, g * C)
                        for j in range(G):
                            nc.scalar.activation(xs[:, 0, j, :], X[:, g * G + j, :], ACT.Copy, scale=S_LN).then_inc(xs_hi, 1)
                    if s.live(0):
                        g = s.at(0)
                        need(act, o_d, g * G)
                        act.wait_ge(v_d, g * G + 1)
                        nc.scalar.activation(v_hi[:, 0, :], work[0][:], ACT.Copy, scale=S_EVAC).then_inc(v_h, 1)
                    if s.live(2):
                        square(s.at(2), 3)
                    if s.live(0):
                        for j in range(1, G):
                            act.wait_ge(v_d, s.at(0) * G + j + 1)
                            nc.scalar.activation(v_hi[:, j, :], work[j][:], ACT.Copy, scale=S_EVAC).then_inc(v_h, 1)
                pipeline(act, NG, 2, 1, step, ahead=1)

            @block.vector
            def _(dve):
                nc.vector.tensor_scalar(mask[:], k.ident[:], -1.0, 1.0, ALU.mult, ALU.add).then_inc(msk_r, 1)
                dve.wait_ge(msk_r, 1)
                nc.vector.tensor_tensor(mask[:], mask[:], k.adj[:], ALU.mult).then_inc(msk_r, 1)
                nc.vector.tensor_copy(ident16[:], k.ident[:]).then_inc(msk_r, 1)
                ch = Chain(dve, consts)
                ch(nc.vector.tensor_scalar(k.s(EPS_L), k.s(W_WL), 1e-16 * S_LN * S_LN * S_EVAC, None, ALU.mult))
                ch(nc.vector.tensor_scalar(k.s(F_OUT2), k.s(M_M), 1.0 / (S_K * S_EVAC * S_LN), None, ALU.mult))
                ch(nc.vector.tensor_scalar(k.s(TMP_A), k.s(M_WG), 1.0 / (S_LN * S_LN * S_EVAC), None, ALU.mult))
                ch(nc.vector.tensor_scalar(k.s(K_G), k.s(TMP_A), k.s(SIG), None, ALU.mult))
                ch(nc.vector.tensor_scalar(k.s(TMP_B), k.s(GATE), 1.0, None, ALU.add))
                ch(nc.vector.reciprocal(k.s(GATE), k.s(TMP_B)))
                ch(nc.vector.tensor_scalar(k.s(UNGATE), k.s(GATE), -1.0, 1.0, ALU.mult, ALU.add))

                def lo(dst, src, hi, scale, hi_sem, n, done):
                    dve.wait_ge(hi_sem, n)
                    nc.vector.scalar_tensor_tensor(dst, src, scale, hi, ALU.mult, ALU.subtract).then_inc(done, 1)

                def counted(sem, per, g):
                    n = [0]

                    def run(ins, wait=True):
                        n[0] += 1
                        assert n[0] <= per
                        ins.then_inc(sem, 1)
                        if wait:
                            settle(dve, sem, g * per + n[0], idle)
                    return run

                def step(s):
                    if s.live(0):
                        g = s.at(0)
                        need(dve, v_d, g * G)
                        for d in range(1, C, 2):
                            dve.wait_ge(t_d, g * C + d + 1)
                            nc.vector.tensor_copy(xT[:, d, :, :].rearrange("p h n -> p (h n)"),
                                                  work[d][:].bitcast(F16)).then_inc(xt_v, 1)
                    if s.live(1):
                        g = s.at(1)
                        run = counted(ksm, SMALL, g)
                        dve.wait_ge(bc_d, 2 * g + 2)
                        run(nc.vector.tensor_tensor(gs[:], gs[:], pgl[:], ALU.add), wait=False)
                        nc.vector.tensor_tensor(es[:], es[:], pgg[:], ALU.add).then_inc(u_r, 1)
                        settle(dve, ksm, g * SMALL + 1, idle)
                        nc.vector.scalar_tensor_tensor(gs[:], gs[:], 0.0, pbc[:], ALU.max, ALU.mult).then_inc(sum_r, 1)
                    if s.live(0):
                        for e in range(2):
                            lo(tl_lo[:, e, :], work[e][:], tl_hi[:, e, :], S_EVAC, tl_h, s.at(0) * C + e + 1, tl_l)
                    if s.live(1):
                        dve.wait_ge(e_r, g + 1)
                        run(nc.vector.scalar_tensor_tensor(grouped(es[:], G), grouped(es[:], G), 1.0, over(mask[:], G),
                                                           ALU.min, ALU.mult), wait=False)
                    if s.live(0):
                        lo(tl_lo[:, 2, :], work[2][:], tl_hi[:, 2, :], S_EVAC, tl_h, s.at(0) * C + 3, tl_l)
                    if s.live(1):
                        dve.wait_ge(mask_r, g + 1)
                        run(nc.vector.tensor_reduce(sm[:, 0, :], grouped(gs[:], G), axis=AX_X, op=ALU.add), wait=False)
                        settle(dve, ksm, g * SMALL + 2, idle)
                        run(nc.vector.tensor_reduce(sm[:, 2, :], grouped(es[:], G), axis=AX_X, op=ALU.add), wait=False)
                    if s.live(0):
                        lo(tl_lo[:, 3, :], work[3][:], tl_hi[:, 3, :], S_EVAC, tl_h, s.at(0) * C + 4, tl_l)
                    if s.live(1):
                        settle(dve, ksm, g * SMALL + 3, idle)
                        run(nc.vector.tensor_tensor(sm[:, 0, :], sm[:, 0, :], rn[:], ALU.mult))
                        run(nc.vector.tensor_scalar(sm[:, 0, :], sm[:, 0, :], 1e-8, None, ALU.max))
                        run(nc.vector.reciprocal(sm[:, 1, :], sm[:, 0, :]), wait=False)
                        run(nc.vector.tensor_scalar(sm[:, 2, :], sm[:, 2, :], 1e-8, None, ALU.max))
                        run(nc.vector.reciprocal(sm[:, 3, :], sm[:, 2, :]), wait=False)
                        run(nc.vector.scalar_tensor_tensor(sm[:, 1, :], sm[:, 1, :], k.s(GATE), rn[:], ALU.mult, ALU.mult))
                        run(nc.vector.tensor_scalar(sm[:, 3, :], sm[:, 3, :], k.s(UNGATE), None, ALU.mult))
                    if s.live(1):
                        for j in range(G):
                            js = slice(j * P, (j + 1) * P)
                            run(nc.vector.tensor_scalar(gs[:, js], gs[:, js], sm[:, 1, j:j + 1], None, ALU.mult),
                                wait=False)
                        for j in range(G):
                            js = slice(j * P, (j + 1) * P)
                            settle(dve, ksm, g * SMALL + SMALL - G + 1 + j, idle)
                            ins = nc.vector.scalar_tensor_tensor(gs[:, js], es[:, js], sm[:, 3, j:j + 1], gs[:, js],
                                                                 ALU.mult, ALU.add)
                        ins.then_inc(k_r, 1)
                    if s.live(0):
                        for e in range(C):
                            lo(tg_lo[:, e, :], work[e][:], tg_hi[:, e, :], S_EVAC, tg_h, s.at(0) * C + e + 1, tg_l)
                    if s.live(1):
                        lo(kT_lo[:], pkt[:], kT_hi[:], S_K, kt_h, s.at(1) + 1, kt_l)
                    if s.live(-1):
                        g = s.at(-1)
                        for j in range(G):
                            lo(xs[:, 1, j, :], X[:, g * G + j, :], xs[:, 0, j, :], S_LN, xs_hi, g * G + j + 1, xs_lo)
                    if s.live(1):
                        for j in range(G):
                            b = s.at(1) * G + j
                            dve.wait_ge(o_d, b + 1)
                            nc.vector.scalar_tensor_tensor(X[:, b, :], work[j][:], k.s(F_OUT2), X[:, b, :], ALU.mult,
                                                           ALU.add).then_inc(o_u, 1)
                    if s.live(0):
                        g = s.at(0)
                        dve.wait_ge(tl_c, g + 1)
                        run2 = counted(diag_r, DIAG, g)
                        run2(nc.vector.tensor_tensor(grouped(dd[:]), grouped(pgl[:]), over(k.ident[:], G), ALU.mult))
                        run2(nc.vector.tensor_reduce(rn[:], grouped(dd[:]), axis=AX_X, op=ALU.add))
                        dve.wait_ge(gg_d, g + 1)
                        run2(nc.vector.tensor_tensor(grouped(dd[:]), grouped(pgg[:]), over(k.ident[:], G), ALU.mult))
                        run2(nc.vector.tensor_reduce(hs[:], grouped(dd[:]), axis=AX_X, op=ALU.add), wait=False)
                        run2(nc.vector.tensor_scalar(rn[:], rn[:], 2.0, k.s(EPS_L), ALU.mult, ALU.max), wait=False)
                        settle(dve, diag_r, g * DIAG + 4, idle)
                        for j in range(G):
                            js = slice(j * P, (j + 1) * P)
                            ins = nc.vector.tensor_scalar(es[:, js], pgg[:, js], hs[:, j:j + 1], None, ALU.subtract)
                        ins.then_inc(tg_c, 1)
                    if s.live(1):
                        for j in range(G):
                            b = s.at(1) * G + j
                            settle(dve, o_u, b + 1, idle)
                            nc.vector.bn_stats(bn[:, j, :], X[:, b, :]).then_inc(bn_r, 1)
                            settle(dve, bn_r, b + 1, idle)
                            if j == 0:
                                settle(dve, nm_r, s.at(1) * G, idle)
                            nc.vector.bn_aggr(mv[:, j, :], bn[:, j, :]).then_inc(mv_r, 1)
                    if s.live(0):
                        g = s.at(0)
                        dve.wait_ge(diag_pow, g + 1)
                        nc.vector.tensor_tensor(grouped(dd[:]), over(k.ident[:], G), spread(rn[:], P),
                                                ALU.mult).then_inc(dd_r, 1)
                        for j in range(G):
                            lo(v_lo[:, j, :], work[j][:], v_hi[:, j, :], S_EVAC, v_h, g * G + j + 1, v_l)
                    if isinstance(s.i, int) and s.i == NG:
                        dve.wait_ge(ns_d, B - G)
                        dve.wait_ge(t_d, NG * C)
                        dve.wait_ge(cleared, 1)
                        early.clamp(dve)
                        early.invert(dve)
                        early.refine(dve)
                pipeline(dve, NG, 2, 1, step, ahead=1)

            @block.gpsimd
            def _(pool):
                pool.memset(k.s(NSQ_MAX), 0.0).then_inc(cleared, 1)
                pool.memset(unit_col[:], 0.0).then_inc(unit_ready, 1)
                pool.wait_ge(unit_ready, 1)
                pool.memset(unit_col[:, B - 1:B], 1.0).then_inc(unit_ready, 1)
                pool.wait_ge(msk_r, 2)
                half = k.s(HALF)

                def square_lo(s, j):
                    b = s.at(2) * G + j
                    tile, hi, low = square_tiles(b)
                    if not last_group(b):
                        need(pool, ns_d, b)
                    pool.wait_ge(sq_h, b + 1)
                    pool.tensor_tensor(low, tile, hi, ALU.subtract).then_inc(sq_l, 1)

                def step(s):
                    if s.live(2):
                        square_lo(s, 0)
                    if s.live(1):
                        pool.wait_ge(sum_r, s.at(1) + 1)
                        pool.tensor_tensor(grouped(gs[:], G), grouped(gs[:], G), over(mask[:], G), ALU.mult).then_inc(mask_r, 1)
                    if s.live(2):
                        square_lo(s, 1)
                        square_lo(s, 2)
                    if s.live(0):
                        g = s.at(0)
                        pool.wait_ge(diag_r, (g + 1) * DIAG)
                        pool.tensor_tensor(rn[:], rn[:], half.broadcast_to([P, G]), ALU.pow).then_inc(diag_pow, 1)
                    if s.live(2):
                        square_lo(s, 3)
                    if s.live(1):
                        g = s.at(1)
                        pool.wait_ge(mv_r, (g + 1) * G)
                        need(pool, ln_r, g * G)
                        settle(pool, mv_r, (g + 1) * G, k.idle["pool"])
                        pool.tensor_scalar(rs[:, 1, :], mv[:, :, 1], LN_EPS, None, ALU.add).then_inc(rs_r, 1)
                        settle(pool, rs_r, 3 * g + 1, k.idle["pool"])
                        pool.tensor_tensor(rs[:, 0, :], rs[:, 1, :], half.broadcast_to([P, G]), ALU.pow).then_inc(rs_r, 1)
                        settle(pool, rs_r, 3 * g + 2, k.idle["pool"])
                        pool.tensor_tensor(rs[:, 1, :], mv[:, :, 0], rs[:, 0, :], ALU.mult).then_inc(rs_r, 1)
                        settle(pool, rs_r, 3 * g + 3, k.idle["pool"])
                        pool.tensor_scalar(rs[:, 1, :], rs[:, 1, :], -1.0, None, ALU.mult).then_inc(nm_r, G)
                pipeline(pool, NG, 2, 1, step)


def build(nc, x, adj, b0, b1, wl, wg, wv, wo, gate, logsig, b3, out):
    with ExitStack() as ctx:
        k = Chip(nc, ctx)
        with ExitStack() as parts:
            w = {f"{n}_{h}": k.sb(parts, f"{n}_{h}", [P, C, N], F16) for n in ("wl", "wg", "m") for h in "hl"}
            with ExitStack() as layer:
                ops = GraphOperands(k, layer)
                with ExitStack() as buffers:
                    mix = MixWeights(k, buffers, w, wl, wg, wv, wo)
                    rows_bank = k.ps(buffers, "rows_bank")
                    load_x(k, x, adj, b0, b3, gate, logsig, mix, rows_bank, scratch_tiles(ops))
                    k.release_semaphores()
                    select_neighbours(k, rows_bank, 1.0, True, mix, ops)
                    k.release_semaphores()
                propagate(k, ops, k.bias0, b1, None)
                k.release_semaphores()
            rows_bank = k.ps(ctx, "rows_bank")
            kernel_mix(k, w, rows_bank)
            k.release_semaphores()
        with ExitStack() as layer:
            ops = GraphOperands(k, layer)
            select_neighbours(k, rows_bank, S_SQ, False, None, ops)
            propagate(k, ops, k.bias3, None, out)


_INS = ['x', 'adj', 'L0_gnn_bias', 'L1_gnn_bias', 'L2_gnn_W_lang', 'L2_gnn_W_grav', 'L2_gnn_W_V', 'L2_gnn_W_O',
        'L2_gnn_gate_logit', 'L2_gnn_log_sigma', 'L3_gnn_bias']


def kernel(**inputs):
    import numpy as _np
    import concourse.bacc as _bacc
    from concourse import mybir as _mybir
    from concourse.bass_utils import run_bass_kernel_spmd as _run

    nc = _bacc.Bacc("TRN2", target_bir_lowering=False, num_devices=1)
    arrays, args = {}, []
    for name in _INS:
        a = _np.ascontiguousarray(inputs[name])
        if a.ndim == 0:
            a = a.reshape(1)
        arrays[f"in_{name}_dram"] = a
        args.append(nc.dram_tensor(f"in_{name}_dram", a.shape, _mybir.dt.from_np(a.dtype), kind="ExternalInput").ap())
    args.append(nc.dram_tensor("out_0_dram", (B, P, N), F32, kind="ExternalOutput").ap())
    build(nc, *args)
    r = _run(nc, [arrays], core_ids=[0])
    return r.results[0]["out_0_dram"]
```
